# Optimizing a Trainium2 kernel written in Bass

```python
import numpy as np
import jax
import jax.numpy as jnp

def _softmax(x, axis=-1):
    return jax.nn.softmax(x, axis=axis)

def _gelu(x):
    return jax.nn.gelu(x, approximate=True)

def _silu(x):
    return jax.nn.silu(x)

def _sigmoid(x):
    return jax.nn.sigmoid(x)

def _layernorm(x, axis=-1, eps=1e-05):
    m = jnp.mean(x, axis=axis, keepdims=True)
    v = jnp.var(x, axis=axis, keepdims=True)
    return (x - m) / jnp.sqrt(v + eps)

def _scatter_add(tgt, idx, src, axis=0):
    return tgt.at[idx].add(src)

def _segment_sum(src, seg, n):
    return jax.ops.segment_sum(src, seg, n)
kernel_name = 'mk_adaln_d1_jaxref_r8_ef915b'

def setup_inputs(seed: int=0):
    np.random.seed(seed)
    _w = jnp.asarray

    def _L0_attn_setup():
        import jax, jax.numpy as jnp
        import numpy as np
        import math
        B, L, D, H = (32, 64, 512, 32)
        HD = D // H
        key = jax.random.key(seed)
        ks = jax.random.split(key, 9)
        s = 1.0 / math.sqrt(D)
        return {'x': jax.random.normal(ks[0], (B, L, D), jnp.float32), 'Wq': jax.random.normal(ks[1], (D, D), jnp.float32) * s, 'bq': jax.random.normal(ks[2], (D,), jnp.float32) * s, 'Wk': jax.random.normal(ks[3], (D, D), jnp.float32) * s, 'bk': jax.random.normal(ks[4], (D,), jnp.float32) * s, 'Wv': jax.random.normal(ks[5], (D, D), jnp.float32) * s, 'bv': jax.random.normal(ks[6], (D,), jnp.float32) * s, 'Wo': jax.random.normal(ks[7], (D, D), jnp.float32) * s, 'bo': jax.random.normal(ks[8], (D,), jnp.float32) * s}
    _L0_attn_in = _L0_attn_setup()

    def _L0_ffn_setup():
        import jax, jax.numpy as jnp
        import numpy as np
        SCALING = 16.0 / 8.0
        GAMMA = 1.0
        EPS = 1e-12
        key = jax.random.key(seed)
        ks = jax.random.split(key, 8)
        B, T, H, O = (4, 256, 512, 512)
        E_tot, E_act, r = (16, 4, 8)
        return {'x': jax.random.normal(ks[0], (B, T, H), jnp.float32), 'W_base': jax.random.normal(ks[1], (O, H), jnp.float32) * 0.02, 'b_base': jax.random.normal(ks[2], (O,), jnp.float32) * 0.02, 'lora_A': jax.random.normal(ks[3], (E_tot, r, H), jnp.float32) * 0.02, 'lora_B': jax.random.normal(ks[4], (E_tot, O, r), jnp.float32) * 0.02, 'router_W': jax.random.normal(ks[5], (E_tot, H), jnp.float32) * 0.02, 'router_b': jax.random.normal(ks[6], (E_tot,), jnp.float32) * 0.02, 'domain_prior': jax.random.uniform(ks[7], (E_tot,), jnp.float32), 'active': jnp.arange(E_act, dtype=jnp.int32)}
    _L0_ffn_in = _L0_ffn_setup()
    _L0_c = _w((lambda *s: np.random.randn(*s).astype(np.float32) * 0.05)(4, 512))
    _L0_wmod = _w((lambda *s: np.random.randn(*s).astype(np.float32) * 0.05)(512, 6 * 512) * 512 ** (-0.5))
    _d = {'L0_attn_x': _L0_attn_in['x'], 'L0_attn_Wq': _L0_attn_in['Wq'], 'L0_attn_bq': _L0_attn_in['bq'], 'L0_attn_Wk': _L0_attn_in['Wk'], 'L0_attn_bk': _L0_attn_in['bk'], 'L0_attn_Wv': _L0_attn_in['Wv'], 'L0_attn_bv': _L0_attn_in['bv'], 'L0_attn_Wo': _L0_attn_in['Wo'], 'L0_attn_bo': _L0_attn_in['bo'], 'L0_ffn_W_base': _L0_ffn_in['W_base'], 'L0_ffn_b_base': _L0_ffn_in['b_base'], 'L0_ffn_lora_A': _L0_ffn_in['lora_A'], 'L0_ffn_lora_B': _L0_ffn_in['lora_B'], 'L0_ffn_router_W': _L0_ffn_in['router_W'], 'L0_ffn_router_b': _L0_ffn_in['router_b'], 'L0_ffn_domain_prior': _L0_ffn_in['domain_prior'], 'L0_ffn_active': _L0_ffn_in['active'], 'L0_c': _L0_c, 'L0_wmod': _L0_wmod}
    _x0 = _d['L0_attn_x']
    _d['L0_attn_x'] = jax.random.normal(jax.random.fold_in(jax.random.key(seed), 1), (4, 512, 512), dtype=_x0.dtype)
    del _x0
    return _d

def reference(L0_attn_x, L0_attn_Wq, L0_attn_bq, L0_attn_Wk, L0_attn_bk, L0_attn_Wv, L0_attn_bv, L0_attn_Wo, L0_attn_bo, L0_ffn_W_base, L0_ffn_b_base, L0_ffn_lora_A, L0_ffn_lora_B, L0_ffn_router_W, L0_ffn_router_b, L0_ffn_domain_prior, L0_ffn_active, L0_c, L0_wmod):

    def _L0_attn_ref(x, Wq, bq, Wk, bk, Wv, bv, Wo, bo):
        import jax, jax.numpy as jnp
        import numpy as np
        import math
        B, L, D, H = (32, 64, 512, 32)
        HD = D // H
        b, l, d = x.shape
        h, hd = (H, HD)
        q = (x @ Wq.T + bq).reshape(b, l, h, hd).transpose(0, 2, 1, 3)
        k = (x @ Wk.T + bk).reshape(b, l, h, hd).transpose(0, 2, 1, 3)
        v = (x @ Wv.T + bv).reshape(b, l, h, hd).transpose(0, 2, 1, 3)
        scores = jnp.einsum('bhqd,bhkd->bhqk', q, k) / math.sqrt(hd)
        causal = jnp.tril(jnp.ones((l, l), bool))
        scores = jnp.where(causal, scores, -jnp.inf)
        att = jax.nn.softmax(scores, axis=-1)
        out = jnp.einsum('bhqk,bhkd->bhqd', att, v)
        out = out.transpose(0, 2, 1, 3).reshape(b, l, d)
        return out @ Wo.T + bo

    def _L0_ffn_ref(x, W_base, b_base, lora_A, lora_B, router_W, router_b, domain_prior, active):
        import jax, jax.numpy as jnp
        import numpy as np
        SCALING = 16.0 / 8.0
        GAMMA = 1.0
        EPS = 1e-12
        y = jnp.einsum('bth,oh->bto', x, W_base) + b_base
        A = lora_A[active]
        Bm = lora_B[active]
        z = jnp.einsum('bth,erh->bter', x, A)
        contribs = jnp.einsum('bter,eor->bteo', z, Bm) * SCALING
        logits = jnp.einsum('bth,eh->bte', x, router_W) + router_b
        logits = logits[..., active]
        prior = domain_prior[active]
        alpha = jax.nn.softmax(jnp.log(prior + EPS) + logits / GAMMA, axis=-1)
        return y + jnp.einsum('bteo,bte->bto', contribs, alpha)
    x = L0_attn_x
    mod = (_silu(L0_c) @ L0_wmod).reshape(L0_c.shape[0], 6, 1, -1)
    sa, ca, ga, sb, cb, gb = (mod[:, 0], mod[:, 1], mod[:, 2], mod[:, 3], mod[:, 4], mod[:, 5])
    ga = (2 * (ga >= 0) - 1) * jnp.maximum(jnp.abs(ga), 0.25)
    gb = (2 * (gb >= 0) - 1) * jnp.maximum(jnp.abs(gb), 0.25)
    h = _layernorm(x, axis=-1) * (1 + ca) + sa
    x = x + ga * _L0_attn_ref(h, L0_attn_Wq, L0_attn_bq, L0_attn_Wk, L0_attn_bk, L0_attn_Wv, L0_attn_bv, L0_attn_Wo, L0_attn_bo)
    h = _layernorm(x, axis=-1) * (1 + cb) + sb
    x = x + gb * _L0_ffn_ref(h, L0_ffn_W_base, L0_ffn_b_base, L0_ffn_lora_A, L0_ffn_lora_B, L0_ffn_router_W, L0_ffn_router_b, L0_ffn_domain_prior, L0_ffn_active)
    return x

_drawn_inputs = setup_inputs


def setup_inputs(seed=0):
    import zlib

    import numpy as np

    out = dict(_drawn_inputs(seed))
    spreads = {}
    factors = {'L0_attn_bq': 31.076,
     'L0_attn_bk': 64.0,
     'L0_attn_bv': 5.009,
     'L0_attn_bo': 5.367,
     'L0_ffn_b_base': 8.0,
     'L0_ffn_lora_A': 7.306,
     'L0_ffn_lora_B': 7.347,
     'L0_ffn_router_W': 8.0,
     'L0_ffn_router_b': 22.802,
     'L0_ffn_domain_prior': 8.0}
    for name, (base, spread) in spreads.items():
        noise = np.random.default_rng([zlib.crc32(name.encode()), seed]).standard_normal(out[name].shape)
        drawn = base * np.exp(spread * noise) if base else spread * noise
        out[name] = jnp.asarray(drawn.astype(out[name].dtype))
    for name, factor in factors.items():
        out[name] = (out[name] * factor).astype(out[name].dtype)
    return out
```

```python
import concourse.bass as bass
from concourse import mybir
from concourse.alu_op_type import AluOpType as ALU
from contextlib import ExitStack

F32 = mybir.dt.float32
F32R = mybir.dt.float32r
BF16 = mybir.dt.bfloat16
I32 = mybir.dt.int32
ACT = mybir.ActivationFunctionType
AX_X = mybir.AxisListType.X

B, L, D, H = 4, 512, 512, 32
HD = D // H
KT = D // 128
QB = L // 128
FT = KT
NU = B * FT
SLOTS = 12
VW = HD + 1
E_TOT, E_ACT, RANK = 16, 4, 8
EZ = RANK + 1
ZR = E_ACT * RANK
NEG = -3.0e38
EPS = 1e-5
SHIFT_ROWS = 48
FILL_OFF = [0, 512, 1024]
P_LEN = 1280
BLK_OFF = [0, 512, 1024, 896]


def aux_fills(ft, last):
    if ft == 0:
        return [("q", 2), ("k", 2)] + [("v", (1, tt)) for tt in range(QB)]
    if ft == 1:
        return [("q", 3), ("k", 3)] + ([] if last else [("x", kt) for kt in range(KT)])
    if last:
        return [("m", 2 * (ft - 1)), ("m", 2 * (ft - 1) + 1)]
    if ft == 2:
        return [("q", 0), ("k", 0)]
    return [("q", 1), ("k", 1)] + [("v", (0, tt)) for tt in range(QB)]


COST = {"q": (12, 216), "k": (12, 216), "v": (12, 109), "x": (4, 109), "m": (4, 858)}
SPAN = {"q": (0, 5), "k": (0, 5), "v": (6, 11), "x": (7, 10), "m": (6, 11)}


def aux_plan(ft, last):
    fills = aux_fills(ft, last)
    slots, ends = [[] for _ in range(SLOTS)], [0] * len(fills)
    for kinds in ("qk", "vxm"):
        products = [(f, n, COST[kind][1]) for f, (kind, _) in enumerate(fills) if kind in kinds
                    for n in range(COST[kind][0])]
        whole, done = sum(c for _, _, c in products), 0
        for f, n, c in products:
            first, final = SPAN[fills[f][0]]
            if ft in (1, 2) and kinds == "qk":
                first, final = ft - 1, ft + 5
            k = first + int(done / whole * (final + 1 - first))
            done += c
            slots[k].append((f, n))
            ends[f] = k
    return fills, slots, ends


def fill_base(ft, last):
    return sum(len(aux_fills(n, last)) for n in range(ft))


FILLS_B = 20
FILLS_0 = 14


def at(b, per_batch, offset):
    return b * per_batch + offset



def adaln_block_kernel(nc, x, WqT, WkT, WvT, bqkv_cols, WoT, bo, WbT, b_base, loraAT, loraBT, bias_prior, active,
                       cT, wmod, out):
    ao_dram = nc.dram_tensor("ao_dram", [B * L, D], F32, kind="Internal").ap()
    ar_dram = nc.dram_tensor("ar_dram", [D, ZR + E_ACT], F32, kind="Internal").ap()
    br_dram = nc.dram_tensor("br_dram", [ZR, D], F32, kind="Internal").ap()
    rp_dram = nc.dram_tensor("rp_dram", [1, 2 * E_ACT], F32, kind="Internal").ap()
    gate_dram = nc.dram_tensor("gate_dram", [2, B, D], F32, kind="Internal").ap()

    ctx = ExitStack()
    with ctx:
        def sb(name, shape, dt=F32, stack=ctx):
            return stack.enter_context(nc.sbuf_tensor(name, shape, dt))

        def sem(name):
            return ctx.enter_context(nc.semaphore(name))

        ident = sb("ident", [128, 128])
        modT = sb("modT", [128, 4, KT, B])
        bcol = sb("bcol", [128, 3, KT])
        silu_c = sb("silu_c", [128, 4, KT, B])
        lnw = sb("lnw", [128, QB, 6])
        lnm = sb("lnm", [128, QB, 2])
        lns = sb("lns", [128, 3, QB])
        idx = sb("idx", [1, 3, E_ACT], I32)
        with ExitStack() as pa:
            WQ = [sb(f"WQ{i}", [128, KT, D], F32R, pa) for i in range(2)]
            WK = [sb(f"WK{i}", [128, KT, D], F32R, pa) for i in range(2)]
            WV = [sb(f"WV{i}", [128, KT, D], F32R, pa) for i in range(2)]
            HT = [sb(f"HT{i}", [128, KT, L], F32R, pa) for i in range(2)]
            QS = sb("QS", [128, FT, 4, L], F32R, pa)
            KS = sb("KS", [128, FT, 4, L], F32R, pa)
            PR = sb("PR", [128, 2, 4, P_LEN], F32, pa)
            V = sb("V", [128, QB, H, VW], F32, pa)
            XH = sb("XH", [128, QB, D], F32, pa)
            QE = sb("QE", [128, 2, L], F32R, pa)
            KE = sb("KE", [128, 2, L], F32R, pa)
            HF = sb("HF", [128, L], F32, pa)
            OE = sb("OE", [128, L], F32, pa)
            AO = sb("AO", [128, 2, QB, 128], F32, pa)
            junk = sb("junk", [128, 2, L], BF16, pa)
            tri = sb("tri", [128, L], BF16, pa)
            MB = sb("MB", [128, 2, 2 * QB, 2], F32, pa)
            NM = sb("NM", [128, 2 * QB, 2, 2], F32R, pa)
            MT = sb("MT", [8, L], F32R, pa)
            RD = sb("RD", [128, 2 * QB, 2], F32, pa)
        pbs = ctx
        WO = [sb(f"WO{i}", [128, KT, D], F32R, pbs) for i in range(2)]
        WB = [sb(f"WB{i}", [128, KT, D], F32R, pbs) for i in range(2)]
        wm_late = sb("wm_late", [128, KT, 2 * D], F32, pbs)
        raw_late = sb("raw_late", [128, 2, KT, D], F32, pbs)
        AON = sb("AON", [128, 2, QB, D], F32, pbs)
        X1 = sb("X1", [128, 2, QB, D], F32, pbs)
        AT = [sb(f"AT{i}", [128, KT, L], F32R, pbs) for i in range(2)]
        HF2 = sb("HF2", [128, 2, L], F32, pbs)
        T1 = sb("T1", [128, 2, D], F32, pbs)
        XH2 = sb("XH2", [128, QB, D], F32, pbs)
        H2 = [[sb(f"H2_{n}_{i}", [128, KT, L], F32R, pbs) for i in range(2)] for n in range(2)]
        GT = sb("GT", [128, 2, 2, D], F32, pbs)
        ART = [sb(f"ART{i}", [128, KT, 128], F32R, pbs) for i in range(2)]
        BR = sb("BR", [98, D], F32, pbs)
        BT = sb("BT", [98, D], F32R, pbs)
        small_pad = sb("small_pad", [128, 128], F32, pbs)
        MOD = sb("MOD", [128, 4, D], F32, pbs)
        ZST = sb("ZST", [98, L], F32R, pbs)
        ZTs = sb("ZTs", [128, L], F32, pbs)
        T2 = sb("T2", [128, 2, D], F32, pbs)
        GBO = sb("GBO", [128, 2, D], F32, pbs)
        G1 = sb("G1", [B, 2, D], F32, pbs)
        ARW = sb("ARW", [128, KT, ZR + E_ACT], F32, pbs)
        ZS = sb("ZS", [128, QB, 98], F32R, pbs)
        ZF = sb("ZF", [128, QB, ZR], F32, pbs)
        AL = sb("AL", [128, 4, QB, E_ACT], F32, pbs)
        AR1 = sb("AR1", [128, 3, QB], F32, pbs)
        RPB = sb("RPB", [128, E_ACT, 2], F32, pbs)
        losel = sb("losel", [128, 1], F32, pbs)

        bank = [ctx.enter_context(nc.psum_tensor(f"bank{i}", [128, 512], F32)) for i in range(8)]
        MX, ST = bank[0:2], bank[2:4]
        PO, PT = bank[4], bank[5]
        PJ = bank[6:8]

        PRf = PR[:, :, :, :].rearrange("p a h c -> p (a h c)")
        raw_w = [PRf[:, n * KT * D:(n + 1) * KT * D].rearrange("p (t c) -> p t c", t=KT) for n in range(3)]
        wm_first = PRf[:, 3 * KT * D:3 * KT * D + KT * 2 * D].rearrange("p (t c) -> p t c", t=KT)

        s_c, s_xl, s_wm, s_bias = sem("s_c"), sem("s_xl"), sem("s_wm"), sem("s_bias")
        s_raw = [sem(f"s_raw{n}") for n in range(3)]
        s_q = [sem(f"s_q{n}") for n in range(FT)]
        s_k = [sem(f"s_k{n}") for n in range(FT)]
        s_mrow = [sem(f"s_mrow{n}") for n in range(2)]
        s_ao = [sem(f"s_ao{n}") for n in range(2)]
        s_id, s_one, s_init = sem("s_id"), sem("s_one"), sem("s_init")
        s_ones = sem("s_ones")
        s_e, s_d1, s_sc = sem("s_e"), sem("s_d1"), sem("s_sc")
        s_whi, s_wlo = sem("s_whi"), sem("s_wlo")
        s_st, s_ag, s_eps, s_rstd, s_xh = (sem(n) for n in ("s_st", "s_ag", "s_eps", "s_rstd", "s_xh"))
        s_mx = [sem(f"s_mx{h}") for h in range(2)]
        s_mxf = [sem(f"s_mxf{h}") for h in range(2)]
        s_st_ = [sem(f"s_st_{h}") for h in range(2)]
        s_ex = [sem(f"s_ex{h}") for h in range(2)]
        s_nmh, s_nm, s_mtp, s_mtd = sem("s_nmh"), sem("s_nm"), sem("s_mtp"), sem("s_mtd")
        s_mask = sem("s_mask")
        s_pv, s_oe, s_otp, s_rd, s_od = (sem(n) for n in ("s_pv", "s_oe", "s_otp", "s_rd", "s_od"))
        s_pj = sem("s_pj")
        s_pjf = [sem(f"s_pjf{n}") for n in range(2)]
        s_qhi, s_khi = sem("s_qhi"), sem("s_khi")
        s_hh, s_hl = sem("s_hh"), sem("s_hl")
        s_pt0 = sem("s_pt0")
        s_rawl, s_wml, s_lh, s_ll = sem("s_rawl"), sem("s_wml"), sem("s_lh"), sem("s_ll")

        s_idx, s_ix, s_gath = sem("s_idx"), sem("s_ix"), sem("s_gath")
        s_ald, s_x1l = [sem("s_ald0"), sem("s_ald1")], [sem("s_x1l0"), sem("s_x1l1")]
        s_ga, s_gb_, s_gst = [sem("s_ga0"), sem("s_ga1")], sem("s_gb_"), sem("s_gst")
        s_lw, s_bol = sem("s_lw"), sem("s_bol")
        s_tb, s_bh, s_bl, s_z2 = sem("s_tb"), sem("s_bh"), sem("s_bl"), sem("s_z2")
        s_bf = [sem("s_bf0"), sem("s_bf1")]
        s_w, s_t1, s_x1, s_st2, s_ag2, s_ep2, s_rs2, s_xh2 = (sem(n) for n in (
            "s_w", "s_t1", "s_x1", "s_st2", "s_ag2", "s_ep2", "s_rs2", "s_xh2"))
        s_gbo, s_xb, s_f, s_t2, s_y = (sem(n) for n in ("s_gbo", "s_xb", "s_f", "s_t2", "s_y"))
        s_zt, s_ztd, s_zn, s_lg, s_ex2, s_zs, s_zsp, s_zst = (sem(n) for n in (
            "s_zt", "s_ztd", "s_zn", "s_lg", "s_ex2", "s_zs", "s_zsp", "s_zst"))
        s_gate, s_ch, s_pc, s_lset, s_btd = (sem(n) for n in ("s_gate", "s_ch", "s_pc", "s_lset", "s_btd"))
        s_out = [sem("s_out0"), sem("s_out1")]

        block = ctx.enter_context(nc.Block())


        def rows(h, n):
            return slice(64 * h, 64 * h + n)

        def wait_apart(eng, sems, count):
            if not isinstance(count, int):
                count = eng.to_reg(count)
                eng.wait_ge(s_init, 1)
            for s in sems:
                eng.wait_ge(s, count)

        def pe_max_fill(pe, b, o, k):
            f, j, s = o % 4, k // 3, k % 3
            if k == 0:
                pe.wait_ge(s_q[f], at(b, 96, 96 * (o // 4 + 1)))
                pe.wait_ge(s_k[f], at(b, 96, 96 * (o // 4 + 1)))
            for h in range(2):
                pe.wait_ge(s_mxf[h], at(b, 48, 12 * o + k))
                for qb, off in [[(3, 0)], [(2, 0), (0, 384)], [(1, 0)]][s]:
                    n = (qb + 1) * 128
                    mm = nc.tensor.matmul(MX[h][:, off:off + n], QS[rows(h, 48), f, j, qb * 128:(qb + 1) * 128],
                                          KS[rows(h, 48), f, j, 0:n], start=True, stop=True)
                mm.then_inc(s_mx[h], 1)

        def pe_score_fill(pe, b, o, k):
            f, j, s = o % 4, k // 3, k % 3
            if k % 6 == 0:
                pe.wait_ge(s_mrow[k // 6], at(b, 128, 32 * (o + 1)))
            for h in range(2):
                pe.wait_ge(s_ex[h], at(b, 48, 12 * o + k))
                for i, off in [[(0, 0)], [(1, 0), (3, 384)], [(2, 0)]][s]:
                    n = L - 128 * i
                    mm = nc.tensor.matmul(ST[h][:, off:off + n], KS[rows(h, 50), f, j, i * 128:(i + 1) * 128],
                                          QS[rows(h, 50), f, j, 128 * i:L], start=True, stop=True)
                mm.then_inc(s_st_[h], 1)

        def pe_max_transpose(pe, b, e):
            pe.wait_ge(s_nm, at(b, 8, e + 1))
            if not (isinstance(b, int) and 8 * b + e < 1):
                pe.wait_ge(s_od, at(b, 8, e - 1))
            for qb in range(QB):
                mm = nc.tensor.transpose(PT[0:8, qb * 128:(qb + 1) * 128],
                                         NM[:, 2 * qb:2 * qb + 2, :, :].rearrange("p a h j -> p (a h j)").bitcast(F32),
                                         ident[:, :])
            mm.then_inc(s_mtp, 1)

        def pe_pv(pe, b, g, blocks):
            f, gi = (g // 2) % 4, g % 2
            if 0 in blocks:
                bb = g // 8
                pe.wait_ge(s_mask, at(b, 16, 2 * g + 2))
                pe.wait_ge(s_oe, at(b, 8, g))
                for n in range(2):
                    pe.wait_ge(s_pjf[n], at(b, 10, 10 * bb + (7 if f < 2 else 10)))
            for i in blocks:
                for h4 in range(4):
                    head = 8 * f + 4 * (h4 // 2) + 2 * gi + h4 % 2
                    mm = nc.tensor.matmul(PO[32 * h4:32 * h4 + VW, 128 * i:L], V[:, i, head, :],
                                          PR[:, gi, h4, BLK_OFF[i]:BLK_OFF[i] + L - 128 * i],
                                          start=(i == 0), stop=(i == QB - 1))
            if QB - 1 in blocks:
                mm.then_inc(s_pv, 1)

        def pe_out_transpose(pe, b, g):
            pe.wait_ge(s_oe, at(b, 8, g + 1))
            pe.wait_ge(s_mtd, min(b * 8 + g + 3, 2 * NU) if isinstance(b, int) else at(b, 8, g + 3))
            pe.wait_ge(s_od, at(b, 8, g + 1))
            for qb in range(QB):
                mm = nc.tensor.transpose(PT[:, qb * 128:(qb + 1) * 128], OE[:, qb * 128:(qb + 1) * 128], ident[:, :])
            mm.then_inc(s_otp, 1)

        def pe_aux_products(pe, b, kind, arg, fill, products):
            dst = PJ[fill % 2]
            n_all = COST[kind][0]
            for n in products:
                if n == 0:
                    pe.wait_ge(s_pjf[fill % 2], at(b, 10, fill // 2))
                if kind in "qk":
                    W = WQ if kind == "q" else WK
                    kt, (wi, hi) = n // 3, [(0, 0), (0, 1), (1, 0)][n % 3]
                    mm = nc.tensor.matmul(dst[:, :], W[wi][:, kt, arg * 128:(arg + 1) * 128], HT[hi][:, kt, :],
                                          start=(n == 0), stop=(n == n_all - 1))
                elif kind == "v":
                    vh, tt = arg
                    kt, (wi, hi) = n // 3, [(0, 0), (1, 0), (0, 1)][n % 3]
                    mm = nc.tensor.matmul(dst[:, 0:256], HT[hi][:, kt, tt * 128:(tt + 1) * 128],
                                          WV[wi][:, kt, vh * 256:(vh + 1) * 256],
                                          start=(n == 0), stop=(n == n_all - 1))
                elif kind == "x":
                    mm = nc.tensor.transpose(dst[:, n * 128:(n + 1) * 128], XH[:, n, arg * 128:(arg + 1) * 128],
                                             ident[:, :])
                else:
                    src = wm_first if arg < 2 else wm_late
                    mm = nc.tensor.matmul(dst[0:B, :], silu_c[:, 3, n, :], src[:, n, (arg % 2) * D:(arg % 2 + 1) * D],
                                          start=(n == 0), stop=(n == n_all - 1))
                if n == n_all - 1:
                    mm.then_inc(s_pj, 1)

        def pe_aux(pe, b, o, k, last):
            f, up = o % 4, o // 4
            fills, slots, _ = aux_plan(f, last)
            for i, n in slots[k]:
                kind, arg = fills[i]
                if n == 0 and kind == "q" and arg == 0:
                    pe.wait_ge(s_hl, at(b, 4, 4 * up + 8))
                if n == 0 and kind == "x":
                    pe.wait_ge(s_xh, at(b, 4, 4 * up + 8))
                if n == 0 and kind == "m" and arg % 2 == 0:
                    pe.wait_ge(s_wml, 16 * (arg // 2))
                pe_aux_products(pe, b, kind, arg, FILLS_0 + FILLS_B * up + fill_base(f, last) + i, [n])

        def pe_slot(pe, b, o, k, last=False):
            final = last and o == 3
            if not final:
                pe_max_fill(pe, b, o + 1, k)
            pe_score_fill(pe, b, o, k)
            if k == 1:
                pe_max_transpose(pe, b, 2 * o + 1)
            if k == 7 and not final:
                pe_max_transpose(pe, b, 2 * o + 2)
            first = isinstance(b, int) and b == 0 and o == 0
            if k in (1, 2, 3) and not first:
                pe_pv(pe, b, 2 * o - 1, [[0], [1], [2, 3]][k - 1])
            if k in (7, 8, 9):
                pe_pv(pe, b, 2 * o, [[0], [1], [2, 3]][k - 7])
            if k == 5 and not first:
                pe_out_transpose(pe, b, 2 * o - 1)
            if k == 11:
                pe_out_transpose(pe, b, 2 * o)
            pe_aux(pe, b, o, k, last)

        def act_q(act, b, kind, o, fill):
            E, bi, s_hi, s_prev = (QE, 0, s_qhi, s_q) if kind == "q" else (KE, 1, s_khi, s_k)
            f = o % 4
            act.wait_ge(s_pj, at(b, FILLS_B, fill + 1))
            if not (isinstance(b, int) and 4 * b + o == 0):
                act.wait_ge(s_prev[(f - 1) % 4], at(b, 96, 96 * ((o - 1) // 4 + 1)))
            nc.scalar.activation(E[:, 0, :], PJ[fill % 2][:, :], ACT.Identity, bias=bcol[:, bi, f:f + 1])\
                .then_inc(s_hi, 1)

        def act_v(act, b, vh, tt, fill):
            act.wait_ge(s_pj, at(b, FILLS_B, fill + 1))
            nc.scalar.activation(V[:, tt, 16 * vh:16 * vh + 16, 0:HD],
                                 PJ[fill % 2][:, 0:256].rearrange("p (h d) -> p h d", d=HD), ACT.Copy)\
                .then_inc(s_pjf[fill % 2], 1)

        def act_x(act, b, up, kt, fill):
            act.wait_ge(s_pj, at(b, FILLS_B, fill + 1))
            nc.scalar.activation(HT[0][:, kt, :], PJ[fill % 2][:, :], ACT.Identity,
                                 scale=mod_col(1, kt, b, up), bias=mod_col(0, kt, b, up)).then_inc(s_hh, 1)

        def mod_col(which, kt, b, up):
            bb = b + up
            return modT[:, which, kt, bb:bb + 1] if isinstance(bb, int) else modT[:, which, kt, bass.ds(bb, 1)]

        def act_m(act, b, arg, fill):
            act.wait_ge(s_pj, at(b, FILLS_B, fill + 1))
            dst = AO[0:B, arg, :, :].rearrange("p a c -> p (a c)") if arg < 2 else MOD[0:B, arg - 2, :]
            nc.scalar.activation(dst, PJ[fill % 2][0:B, :], ACT.Copy).then_inc(s_pjf[fill % 2], 1)

        def act_max_rows(act, b, e):
            act.wait_ge(s_mtp, at(b, 8, e + 1))
            act.wait_ge(s_mrow[(e - 1) % 2], at(b, 128, 32 * ((e + 1) // 2)))
            nc.scalar.activation(MT[:, :], PT[0:8, :], ACT.Copy).then_inc(s_mtd, 1)

        def act_exp(act, b, o, k):
            gi, jj, s = k // 6, (k // 3) % 2, k % 3
            if k % 6 == 0:
                act.wait_ge(s_pv, at(b, 8, 2 * o + gi))
            n = [512, 512, 256][s]
            for h in range(2):
                act.wait_ge(s_st_[h], at(b, 48, 12 * o + k + 1))
                nc.scalar.activation(PR[:, gi, 2 * h + jj, FILL_OFF[s]:FILL_OFF[s] + n],
                                     ST[h][:, 0:n], ACT.Exp, scale=HD ** -0.5).then_inc(s_ex[h], 1)

        def act_out(act, b, g):
            act.wait_ge(s_pv, at(b, 8, g + 2))
            act.wait_ge(s_otp, at(b, 8, g))
            nc.scalar.activation(OE[:, :], PO[:, :], ACT.Copy).then_inc(s_oe, 1)

        def ended(o, k, last):
            o, k = (o, k - 1) if k else (o - 1, SLOTS - 1)
            if o < 0:
                return []
            f, up = o % 4, o // 4
            fills, _, ends = aux_plan(f, last)
            return [(kind, arg, FILLS_0 + FILLS_B * up + fill_base(f, last) + i, o)
                    for i, ((kind, arg), e) in enumerate(zip(fills, ends)) if e == k]

        def act_slot(act, b, o, k, last=False):
            final = last and o == 3
            first = isinstance(b, int) and b == 0 and o == 0
            act_exp(act, b, o, k)
            if k == 1:
                act_max_rows(act, b, 2 * o + 1)
            if k == 7 and not final:
                act_max_rows(act, b, 2 * o + 2)
            if k == 3 and not first:
                act_out(act, b, 2 * o - 1)
            if k == 9:
                act_out(act, b, 2 * o)
            for kind, arg, fill, oo in ended(o, k, last):
                act_aux(act, b, kind, arg, fill, oo)
            if final and k < 8:
                if k == 0:
                    act.wait_ge(s_rawl, 32)
                w, kt = k // 4, k % 4
                nc.scalar.activation((WO, WB)[w][0][:, kt, :], raw_late[:, w, kt, :], ACT.Copy).then_inc(s_lh, 1)

        def act_aux(act, b, kind, arg, fill, oo):
            if kind in "qk":
                act_q(act, b, kind, oo + 2, fill)
            elif kind == "v":
                act_v(act, b, arg[0], arg[1], fill)
            elif kind == "x":
                act_x(act, b, oo // 4 + 1, arg, fill)
            else:
                act_m(act, b, arg, fill)

        def dve_max(dve, b, o, k):
            jj, s = (k // 3) % 2, k % 3
            for h in range(2):
                wait_apart(dve, [s_mx[h]], at(b, 48, 12 * o + k + 1))
                for qb, off in [[(3, 0)], [(2, 0), (0, 384)], [(1, 0)]][s]:
                    n = (qb + 1) * 128
                    last = nc.vector.tensor_tensor_reduce(
                        out=junk[:, h, off:off + n], in0=MX[h][:, off:off + n], in1=tri[:, L - n:L], scale=1.0, scalar=NEG,
                        op0=ALU.add, op1=ALU.max, accum_out=MB[:, k // 6, 2 * qb + h, jj:jj + 1])
                last.then_inc(s_mxf[h], 1)

        def dve_neg_max(dve, b, e):
            dve.wait_ge(s_mxf[0], at(b, 48, 6 * e + 6))
            dve.wait_ge(s_mxf[1], at(b, 48, 6 * e + 6))
            dve.wait_ge(s_mtp, at(b, 8, e))
            nc.vector.tensor_scalar(NM[:, :, 0, :], MB[:, e % 2, :, :], -1.0, None, ALU.mult).then_inc(s_nmh, 1)
            dve.wait_ge(s_nmh, at(b, 8, e + 1))
            nc.vector.scalar_tensor_tensor(NM[:, :, 1, :], MB[:, e % 2, :, :], -1.0, NM[:, :, 0, :].bitcast(F32), ALU.mult,
                                           ALU.subtract).then_inc(s_nm, 1)

        def dve_out(dve, b, g):
            f, gi = (g // 2) % 4, g % 2
            dve.wait_ge(s_otp, at(b, 8, g + 1))
            if gi == 0:
                o = g // 2
                dve.wait_ge(s_ao[f % 2], at(b, 32, 16 * (2 * (o // 4) + f // 2)))
            view = PT[:, :].rearrange("p (a j w) -> p a j w", j=2, w=32)
            nc.vector.reciprocal(RD[:, :, :], view[:, :, :, HD]).then_inc(s_rd, 1)
            dve.wait_ge(s_rd, at(b, 8, g + 1))
            dst = AO[:, f % 2, :, :].rearrange("p q (h g j w) -> p (q h) g j w", h=2, g=2, j=2)[:, :, gi, :, :]
            nc.vector.tensor_tensor(dst, view[:, :, :, 0:HD], RD[:, :, :].unsqueeze(3).to_broadcast([128, 2 * QB, 2, HD]),
                                    ALU.mult).then_inc(s_od, 1)

        def dve_aux(dve, b, kind, arg, fill, oo):
            if kind in "qk":
                E, bi, s_hi = (QE, 0, s_qhi) if kind == "q" else (KE, 1, s_khi)
                o = oo + 2
                dve.wait_ge(s_hi, at(b, 4, o + 1))
                nc.vector.scalar_tensor_tensor(E[:, 1, :], PJ[fill % 2][:, :], bcol[:, bi, o % 4:o % 4 + 1],
                                               E[:, 0, :].bitcast(F32), ALU.add, ALU.subtract)\
                    .then_inc(s_pjf[fill % 2], 1)
            elif kind == "x":
                up = oo // 4 + 1
                n = 4 * up + arg
                dve.wait_ge(s_hh, at(b, 4, n + 1))
                dve.wait_ge(s_hl, at(b, 4, n))
                nc.vector.tensor_scalar(HF[:, :], PJ[fill % 2][:, :], mod_col(1, arg, b, up), mod_col(0, arg, b, up),
                                        ALU.mult, ALU.add).then_inc(s_pjf[fill % 2], 1)

        def dve_stats(dve, b, n, tt):
            if tt == 0:
                dve.wait_ge(s_xl, at(b, 16, 16 * n + 16))
                if not (isinstance(b, int) and b + n == 0):
                    dve.wait_ge(s_xh, at(b, 4, 4 * n))
            nc.vector.bn_stats(lnw[:, tt, :], XH[:, tt, :]).then_inc(s_st, 1)

        def dve_aggregate(dve, b, n):
            wait_apart(dve, [s_st], at(b, 4, 4 * n + 4))
            for tt in range(QB):
                nc.vector.bn_aggr(lnm[:, tt, :], lnw[:, tt, :]).then_inc(s_ag, 1)
            dve.wait_ge(s_ag, at(b, 4, 4 * n + 4))
            nc.vector.tensor_scalar(lns[:, 0, :], lnm[:, :, 1], EPS, None, ALU.add).then_inc(s_eps, 1)

        def dve_slot(dve, b, o, k, last=False):
            first = isinstance(b, int) and b == 0 and o == 0
            final = last and o == 3
            if not final:
                dve_max(dve, b, o + 1, k)
            if k % 6 == 5 and not final:
                dve_neg_max(dve, b, 2 * (o + 1) + k // 6)
            if k == 5 and not first:
                dve_out(dve, b, 2 * o - 1)
            if k == 11:
                dve_out(dve, b, 2 * o)
            for kind, arg, fill, oo in ended(o, k, last):
                dve_aux(dve, b, kind, arg, fill, oo)
            n = SLOTS * o + k - 9
            if 0 <= n < QB and not last:
                dve_stats(dve, b, 1, n)
            if n == QB and not last:
                dve_aggregate(dve, b, 1)

        def pool_mask(pool, b, o, k):
            gi, jj = k // 6, (k // 3) % 2
            wait_apart(pool, s_ex, at(b, 48, 12 * o + k + 1))
            for i in range(QB):
                part = PR[:, gi, jj::2, BLK_OFF[i]:BLK_OFF[i] + 128]
                last = nc.gpsimd.affine_select(out=part, in_=part, compare_op=ALU.is_ge, fill=0.0, base=0,
                                               pattern=[[0, 2], [1, 128]], channel_multiplier=-1)
            last.then_inc(s_mask, 1)

        def pool_norm(pool, b, n):
            pool.wait_ge(s_eps, at(b, 1, n + 1))
            nc.gpsimd.tensor_tensor(lns[:, 1, :], lns[:, 0, :], lns[:, 2, :], ALU.pow).then_inc(s_rstd, 1)
            wait_apart(pool, [s_rstd], at(b, 1, n + 1))

        def pool_xhat(pool, b, n, tt):
            nc.gpsimd.tensor_scalar(XH[:, tt, :], XH[:, tt, :], lnm[:, tt, 0:1], lns[:, 1, tt:tt + 1], ALU.subtract,
                                    ALU.mult).then_inc(s_xh, 1)

        def pool_aux(pool, b, kind, arg, fill, oo):
            if kind == "x":
                pool.wait_ge(s_pjf[fill % 2], at(b, 10, fill // 2 + 1))
                nc.gpsimd.tensor_tensor(HT[1][:, arg, :], HF[:, :], HT[0][:, arg, :].bitcast(F32), ALU.subtract)\
                    .then_inc(s_hl, 1)

        def pool_slot(pool, b, o, k, last=False):
            for kind, arg, fill, oo in ended(o, k, last):
                pool_aux(pool, b, kind, arg, fill, oo)
            if k % 3 == 2:
                pool_mask(pool, b, o, k)
            if o == 1 and k == 2 and not last:
                pool_norm(pool, b, 1)
            if o == 1 and 2 <= k < 2 + QB and not last:
                pool_xhat(pool, b, 1, k - 2)
            if last and o == 3 and 1 <= k < 9:
                w, kt = (k - 1) // 4, (k - 1) % 4
                pool.wait_ge(s_lh, k)
                nc.gpsimd.tensor_tensor((WO, WB)[w][1][:, kt, :], raw_late[:, w, kt, :],
                                        (WO, WB)[w][0][:, kt, :].bitcast(F32), ALU.subtract).then_inc(s_ll, 1)

        def sp_heads(sp, b, kind, o, fill):
            E, S, s_rows, parts = (QE, QS, s_q, (0, 1, 0)) if kind == "q" else (KE, KS, s_k, (0, 0, 1))
            f = o % 4
            sp.wait_ge(s_pjf[fill % 2], at(b, 10, fill // 2 + 1))
            for r, part in enumerate(parts):
                for h in range(2):
                    sp.dma_start(S[64 * h + 16 * r:64 * h + 16 * r + 16, f, :, :].rearrange("p j t -> p (j t)")
                                 .bitcast(F32), E[64 * h:64 * h + 64, part, :].bitcast(F32)).then_inc(s_rows[f], 16)

        def sp_max_rows(sp, b, e):
            f, gi = (e // 2) % 4, e % 2
            sp.wait_ge(s_mtd, at(b, 8, e + 1))
            for h in range(2):
                sp.dma_start(QS[64 * h + SHIFT_ROWS:64 * h + SHIFT_ROWS + 2, f, 2 * gi:2 * gi + 2, :]
                             .rearrange("p j t -> p (j t)").bitcast(F32), MT[4 * h:4 * h + 4, :].bitcast(F32)).then_inc(s_mrow[gi], 16)

        def sp_store_ao(sp, b, o):
            f, bb = o % 4, b + o // 4
            sp.wait_ge(s_od, at(b, 8, 2 * o + 3))
            rows_ = ao_dram[bass.ds(bb * L, L), :] if not isinstance(bb, int) else ao_dram[bb * L:(bb + 1) * L, :]
            sp.dma_start(rows_.rearrange("(q p) c -> p q c", p=128)[:, :, f * 128:(f + 1) * 128],
                         AO[:, f % 2, :, :]).then_inc(s_ao[f % 2], 16)

        def sp_load_x(sp, b, n):
            bb = b + n
            rows_ = x[bb, :, :] if isinstance(bb, int) else x[bass.ds(bb, 1), :, :].rearrange("a t c -> (a t) c")
            sp.dma_start(XH[:, :, :], rows_.rearrange("(q p) c -> p q c", p=128)).then_inc(s_xl, 16)

        def sp_slot(sp, b, o, k, last=False):
            final = last and o == 3
            first = isinstance(b, int) and b == 0 and o == 0
            if (o, k) == (0, 6) and not last:
                sp.wait_ge(s_pj, at(b, FILLS_B, 6))
                sp_load_x(sp, b, 1)
            if k == 1:
                sp_max_rows(sp, b, 2 * o + 1)
            if k == 7 and not final:
                sp_max_rows(sp, b, 2 * o + 2)
            for kind, arg, fill, oo in ended(o, k, last):
                if kind in "qk":
                    sp_heads(sp, b, kind, oo + 2, fill)
            if k == 5 and not first:
                sp_store_ao(sp, b, o - 1)
            if last and o == 1 and k == 3:
                sp.wait_ge(s_pj, FILLS_0 + FILLS_B * b + 6)
                sp.dma_start(wm_late[:, :, :], wmod[:, 2 * D:4 * D].rearrange("(t p) c -> p t c", p=128))\
                    .then_inc(s_wml, 16)
            if last and o == 1 and k == 10:
                sp.wait_ge(s_pj, FILLS_0 + FILLS_B * b + 8)
                for w, src in enumerate((WoT, WbT)):
                    sp.dma_start(raw_late[:, w, :, :], src.rearrange("(t p) c -> p t c", p=128)).then_inc(s_rawl, 16)
            if final and k == 0:
                sp.wait_ge(s_pj, FILLS_0 + FILLS_B * b + fill_base(2, True) + 2)
                sp.dma_start(wm_late[:, :, :], wmod[:, 4 * D:6 * D].rearrange("(t p) c -> p t c", p=128))\
                    .then_inc(s_wml, 16)

        def phase_a(eng, slot):
            for k in range(6):
                slot(eng, 0, 0, k)
            with eng.Fori(0, B - 1) as b:
                for n in range(6, 4 * SLOTS + 6):
                    slot(eng, b, n // SLOTS, n % SLOTS)
            for n in range(6, 4 * SLOTS):
                slot(eng, B - 1, n // SLOTS, n % SLOTS, last=True)

        PRE = [("m", 0), ("m", 1)] + [("x", kt) for kt in range(KT)] + [("q", 0), ("k", 0), ("q", 1), ("k", 1)] + \
            [("v", (0, tt)) for tt in range(QB)]

        def pre_unit(kind, arg):
            return arg - 2 if kind in "qk" else -4

        STEPS = [("W", 0, tt) for tt in range(QB)] + [("T", 1), ("X", 0)]
        for n in range(B):
            more, two = n + 1 < B, n + 2 < B
            STEPS += [("ZT", n), ("F", n, 0), ("ZN", n)] + [("W", n + 1, tt) for tt in range(2) if more] + [("ZS", n)]
            STEPS += [("W", n + 1, tt) for tt in range(2, 4) if more] + [("FL", n, 0), ("F", n, 1), ("FL", n, 1)]
            STEPS += [("T", n + 2)] * two + [("F", n, 2), ("FL", n, 2)] + [("X", n + 1)] * more
            STEPS += [("F", n, 3), ("FL", n, 3)]
        TILES = [("T", 0)] + [s for s in STEPS if s[0] in "TX"]
        TB, YW, YF, ZB, ZN = bank[0:2], bank[2:4], bank[4:6], bank[6], bank[7]

        def tile_of(kind, n, kt):
            return KT * TILES.index((kind, n)) + kt

        def pe_tile_transposes(pe, kind, n):
            src = AON[:, n % 2, :, :] if kind == "T" else XH2
            if (kind, n) == ("T", 0):
                for h in range(2):
                    pe.wait_ge(s_mxf[h], 12 * NU)
            if kind == "T":
                pe.wait_ge(s_ald[n % 2], 16 * (n // 2 + 1))
            else:
                pe.wait_ge(s_xh2, QB * (n + 1))
            for kt in range(KT):
                i = tile_of(kind, n, kt)
                pe.wait_ge(s_bf[i % 2], i // 2)
                for tt in range(QB):
                    mm = nc.tensor.transpose(TB[i % 2][:, tt * 128:(tt + 1) * 128],
                                             src[:, tt, kt * 128:(kt + 1) * 128], ident[:, :])
                mm.then_inc(s_tb, 1)

        def pe_products(pe, dst, act_parts, w_parts, tt, wait, stop):
            for kt in range(KT):
                if wait:
                    wait(kt)
                for n, (hi, wi) in enumerate([(0, 0), (0, 1), (1, 0)]):
                    mm = nc.tensor.matmul(dst[:, :], act_parts[hi][:, kt, tt * 128:(tt + 1) * 128], w_parts[wi][:, kt, :],
                                          start=(kt == 0 and n == 0), stop=(stop and kt == KT - 1 and n == 2))
            return mm

        def pe_phase_b(pe):
            for h in range(2):
                pe.wait_ge(s_pjf[h], FILLS_0 // 2 + 10 * (B - 1) + 6)
            for c in range(2):
                for kt in range(KT):
                    mm = nc.tensor.transpose(ZN[:, (c * KT + kt) * B:(c * KT + kt + 1) * B],
                                             MOD[0:B, 1 + c, kt * 128:(kt + 1) * 128], ident[0:B, 0:B])
            mm.then_inc(s_z2, 1)
            for h in range(2):
                pe.wait_ge(s_ex[h], 12 * NU)
            pe.wait_ge(s_ll, 8)
            for step in STEPS:
                kind, n = step[0], step[1]
                if kind in "TX":
                    pe_tile_transposes(pe, kind, n)
                if kind == "W":
                    tt = step[2]
                    i = QB * n + tt
                    pe.wait_ge(s_t1, i - 1 if i > 1 else 0)
                    pe_products(pe, YW[i % 2], AT, WO, tt, lambda kt: pe.wait_ge(s_bl, tile_of("T", n, kt) + 1), True)\
                        .then_inc(s_w, 1)
                if kind == "ZT":
                    if n == 0:
                        pe.wait_ge(s_lset, 2)
                    pe.wait_ge(s_zst, n)
                    for kt in range(KT):
                        pe.wait_ge(s_bl, tile_of("X", n, kt) + 1)
                        for j, (wi, hi) in enumerate([(0, 0), (1, 0), (0, 1)]):
                            mm = nc.tensor.matmul(ZB[:, :], ART[wi][:, kt, :], H2[n % 2][hi][:, kt, :],
                                                  start=(kt == 0 and j == 0), stop=(kt == KT - 1 and j == 2))
                    mm.then_inc(s_zt, 1)
                if kind == "F":
                    i = QB * n + step[2]
                    if i == 0:
                        pe.wait_ge(s_oe, 2 * NU)
                        pe.wait_ge(s_od, 2 * NU + 1)
                    pe.wait_ge(s_t2, i - 1 if i > 1 else 0)
                    pe_products(pe, YF[i % 2], H2[n % 2], WB, step[2], None, False)
                if kind == "FL":
                    i = QB * n + step[2]
                    if i == 0:
                        pe.wait_ge(s_btd, 1)
                    pe.wait_ge(s_zst, n + 1)
                    nc.tensor.matmul(YF[i % 2][:, :], ZST[:, step[2] * 128:(step[2] + 1) * 128], BT[:, :], start=False,
                                     stop=True).then_inc(s_f, 1)
                if kind == "ZN":
                    pe.wait_ge(s_ztd, n + 1)
                    pe.wait_ge(s_zs, n)
                    pe.wait_ge(s_z2, 2)
                    for tt in range(QB):
                        mm = nc.tensor.transpose(ZN[:, tt * 36:(tt + 1) * 36], ZTs[0:36, tt * 128:(tt + 1) * 128],
                                                 ident[0:36, 0:36])
                    mm.then_inc(s_zn, 1)
                if kind == "ZS":
                    pe.wait_ge(s_zs, n + 1)
                    for tt in range(QB):
                        mm = nc.tensor.transpose(ZB[0:98, tt * 128:(tt + 1) * 128], ZS[:, tt, :].bitcast(F32), ident[:, :])
                    mm.then_inc(s_zsp, 1)

        def act_tile_transposes(act, kind, n):
            for kt in range(KT):
                i = tile_of(kind, n, kt)
                act.wait_ge(s_tb, i + 1)
                if kind == "T":
                    nc.scalar.activation(AT[0][:, kt, :], TB[i % 2][:, :], ACT.Identity, bias=bcol[:, 2, kt:kt + 1])\
                        .then_inc(s_bh, 1)
                else:
                    nc.scalar.activation(H2[n % 2][0][:, kt, :], TB[i % 2][:, :], ACT.Identity,
                                         scale=modT[:, 3, kt, n:n + 1], bias=modT[:, 2, kt, n:n + 1]).then_inc(s_bh, 1)

        def act_phase_b(act):
            for step in STEPS:
                kind, n = step[0], step[1]
                if kind in "TX":
                    if kind == "X" and n == 0:
                        act.wait_ge(s_z2, 2)
                    act_tile_transposes(act, kind, n)
                if kind == "ZT":
                    act.wait_ge(s_zt, n + 1)
                    act.wait_ge(s_zn, n)
                    nc.scalar.activation(ZTs[:, :], ZB[:, :], ACT.Copy).then_inc(s_ztd, 1)
                if kind == "ZN":
                    act.wait_ge(s_lg, n + 1)
                    nc.scalar.activation(AL[:, 2, :, :], AL[:, 1, :, :], ACT.Exp).then_inc(s_ex2, 1)
                if kind == "ZS":
                    act.wait_ge(s_zsp, n + 1)
                    act.wait_ge(s_f, QB * n)
                    nc.scalar.activation(ZST[:, :], ZB[0:98, :], ACT.Copy).then_inc(s_zst, 1)

        def dve_tile_transposes(dve, kind, n):
            for kt in range(KT):
                i = tile_of(kind, n, kt)
                dve.wait_ge(s_bh, i + 1)
                dve.wait_ge(s_bl, i - 1 if i > 1 else 0)
                if kind == "T":
                    op = nc.vector.tensor_scalar(HF2[:, i % 2, :], TB[i % 2][:, :], bcol[:, 2, kt:kt + 1], None, ALU.add)
                else:
                    op = nc.vector.tensor_scalar(HF2[:, i % 2, :], TB[i % 2][:, :], modT[:, 3, kt, n:n + 1],
                                                 modT[:, 2, kt, n:n + 1], ALU.mult, ALU.add)
                op.then_inc(s_bf[i % 2], 1)

        def dve_phase_b(dve):
            chain = [0]

            def link(ins):
                chain[0] += 1
                ins.then_inc(s_ch, 1)
                dve.wait_ge(s_ch, chain[0])

            dve.wait_ge(s_ao[1], 16 * NU // 2)
            for g, row in enumerate((0, 3)):
                dve.wait_ge(s_gate, g)
                link(nc.vector.tensor_scalar(G1[:, 0, :], MOD[0:B, row, :], 0.0, 2.0, ALU.is_ge, ALU.mult))
                link(nc.vector.tensor_scalar(G1[:, 0, :], G1[:, 0, :], 1.0, None, ALU.subtract))
                link(nc.vector.scalar_tensor_tensor(G1[:, 1, :], MOD[0:B, row, :], -1.0, MOD[0:B, row, :], ALU.mult, ALU.max))
                nc.vector.scalar_tensor_tensor(MOD[0:B, row, :], G1[:, 1, :], 0.25, G1[:, 0, :], ALU.max, ALU.mult)\
                    .then_inc(s_gate, 1)
            dve.wait_ge(s_z2, 1)
            nc.vector.tensor_copy(modT[:, 2, :, :], ZN[:, 0:KT * B].rearrange("p (t b) -> p t b", b=B))
            nc.vector.tensor_scalar(modT[:, 3, :, :], ZN[:, KT * B:2 * KT * B].rearrange("p (t b) -> p t b", b=B), 1.0,
                                    None, ALU.add).then_inc(s_z2, 1)
            nc.vector.memset(ZS[:, :, 96:98].bitcast(F32), 1.0)
            for w in range(2):
                nc.vector.memset(ART[w][:, :, :].bitcast(F32), 0.0)
            dve.wait_ge(s_lw, 7 * 16)
            nc.vector.tensor_scalar(RPB[:, :, 1], RPB[:, :, 1], 1e-12, None, ALU.add)
            link(nc.vector.tensor_copy(BT[:, :], BR[:, :]))
            nc.vector.tensor_copy(ART[0][:, :, 0:36], ARW[:, :, :]).then_inc(s_lset, 1)
            dve.wait_ge(s_pc, 4)
            nc.vector.scalar_tensor_tensor(BT[:, :], BT[:, :].bitcast(F32), losel[0:98, :], BR[:, :], ALU.mult, ALU.add)\
                .then_inc(s_btd, 1)
            dve.wait_ge(s_lset, 1)
            nc.vector.tensor_tensor(ART[1][:, :, 0:36], ARW[:, :, :], ART[0][:, :, 0:36].bitcast(F32), ALU.subtract)\
                .then_inc(s_lset, 1)

            for step in STEPS:
                kind, n = step[0], step[1]
                if kind in "TX":
                    dve_tile_transposes(dve, kind, n)
                if kind == "W":
                    tt = step[2]
                    i = QB * n + tt
                    if tt == 0:
                        dve.wait_ge(s_ga[n % 2], 32 * (n // 2 + 1))
                    dve.wait_ge(s_w, i + 1)
                    nc.vector.tensor_tensor(T1[:, i % 2, :], YW[i % 2][:, :], GT[:, n % 2, 0, :], ALU.mult)\
                        .then_inc(s_t1, 1)
                    dve.wait_ge(s_t1, i + 1)
                    dve.wait_ge(s_xb, i + 1)
                    nc.vector.tensor_tensor(X1[:, n % 2, tt, :], T1[:, i % 2, :], X1[:, n % 2, tt, :], ALU.add)\
                        .then_inc(s_x1, 1)
                    dve.wait_ge(s_x1, i + 1)
                    nc.vector.bn_stats(lnw[:, tt, :], X1[:, n % 2, tt, :]).then_inc(s_st2, 1)
                    dve.wait_ge(s_st2, i + 1)
                    nc.vector.bn_aggr(lnm[:, tt, :], lnw[:, tt, :]).then_inc(s_ag2, 1)
                    dve.wait_ge(s_ag2, i + 1)
                    nc.vector.tensor_scalar(lns[:, 0, tt:tt + 1], lnm[:, tt, 1:2], EPS, None, ALU.add).then_inc(s_ep2, 1)
                    if tt % 2 or tt == QB - 1:
                        for t in (tt - 1, tt):
                            dve_normalise(dve, n, t)
                if kind == "ZN":
                    zn = ZN[:, 0:QB * 36].rearrange("p (t e z) -> p t e z", e=E_ACT, z=EZ)

                    def over_tiles(ap):
                        return ap.unsqueeze(1).to_broadcast([128, QB, E_ACT])

                    def over_experts(ap):
                        return ap.unsqueeze(2).to_broadcast([128, QB, E_ACT])

                    dve.wait_ge(s_zn, n + 1)
                    link(nc.vector.tensor_tensor(AL[:, 0, :, :], zn[:, :, :, RANK], over_tiles(RPB[:, :, 0]), ALU.add))
                    link(nc.vector.reduce_max(AR1[:, 0, :], AL[:, 0, :, :], AX_X))
                    nc.vector.tensor_tensor(AL[:, 1, :, :], AL[:, 0, :, :], over_experts(AR1[:, 0, :]), ALU.subtract)\
                        .then_inc(s_lg, 1)
                    dve.wait_ge(s_ex2, n + 1)
                    link(nc.vector.tensor_tensor(AL[:, 0, :, :], AL[:, 2, :, :], over_tiles(RPB[:, :, 1]), ALU.mult))
                    link(nc.vector.reduce_sum(AR1[:, 1, :], AL[:, 0, :, :], AX_X))
                    link(nc.vector.reciprocal(AR1[:, 2, :], AR1[:, 1, :]))
                    link(nc.vector.scalar_tensor_tensor(AL[:, 3, :, :], AL[:, 0, :, :], 2.0, over_experts(AR1[:, 2, :]),
                                                        ALU.mult, ALU.mult))
                    if n:
                        dve.wait_ge(s_zsp, n)
                    link(nc.vector.tensor_tensor(
                        ZF[:, :, :].rearrange("p t (e r) -> p t e r", r=RANK),
                        zn[:, :, :, 0:RANK],
                        AL[:, 3, :, :].unsqueeze(3).to_broadcast([128, QB, E_ACT, RANK]), ALU.mult))
                    link(nc.vector.tensor_copy(ZS[:, :, 0:ZR], ZF[:, :, :]))
                    nc.vector.tensor_copy(ZS[:, :, ZR:2 * ZR], ZF[:, :, :])
                    nc.vector.tensor_tensor(ZS[:, :, 2 * ZR:3 * ZR], ZF[:, :, :], ZS[:, :, 0:ZR].bitcast(F32),
                                            ALU.subtract).then_inc(s_zs, 1)
                if kind == "FL":
                    tt = step[2]
                    i = QB * n + tt
                    dve.wait_ge(s_f, i + 1)
                    dve.wait_ge(s_out[i % 2], 16 * (i // 2))
                    nc.vector.tensor_tensor(T2[:, i % 2, :], YF[i % 2][:, :], GT[:, n % 2, 1, :], ALU.mult)\
                        .then_inc(s_t2, 1)
                    dve.wait_ge(s_t2, i + 1)
                    nc.vector.tensor_tensor(T2[:, i % 2, :], T2[:, i % 2, :], X1[:, n % 2, tt, :], ALU.add)\
                        .then_inc(s_y, 1)

        def dve_normalise(dve, n, t):
            dve.wait_ge(s_rs2, QB * n + t + 1)
            if t == 0 and n:
                dve.wait_ge(s_tb, tile_of("X", n - 1, KT - 1) + 1)
            nc.vector.tensor_scalar(XH2[:, t, :], X1[:, n % 2, t, :], lnm[:, t, 0:1], lns[:, 1, t:t + 1], ALU.subtract,
                                    ALU.mult).then_inc(s_xh2, 1)

        def pool_tile_transposes(pool, kind, n):
            dst = AT if kind == "T" else H2[n % 2]
            for kt in range(KT):
                i = tile_of(kind, n, kt)
                pool.wait_ge(s_bf[i % 2], i // 2 + 1)
                nc.gpsimd.tensor_tensor(dst[1][:, kt, :], HF2[:, i % 2, :], dst[0][:, kt, :].bitcast(F32), ALU.subtract)\
                    .then_inc(s_bl, 1)

        def pool_phase_b(pool):
            pool.wait_ge(s_ao[1], 16 * NU // 2)
            nc.gpsimd.memset(losel[:, :], -1.0).then_inc(s_pc, 1)
            for n, (op, fill, base, mult) in enumerate([(ALU.is_ge, 0.0, -ZR, 1), (ALU.is_ge, 0.0, 2 * ZR - 1, -1),
                                                        (ALU.not_equal, -1.0, -3 * ZR - 1, 1)]):
                pool.wait_ge(s_pc, n + 1)
                nc.gpsimd.affine_select(out=losel[:, :], in_=losel[:, :], compare_op=op, fill=fill, base=base,
                                        pattern=[[0, 1]], channel_multiplier=mult).then_inc(s_pc, 1)
            pool_residual(pool, 0)
            for step in STEPS:
                kind, n = step[0], step[1]
                if kind in "TX":
                    pool_tile_transposes(pool, kind, n)
                if kind == "W":
                    i, tt = QB * n + step[2], step[2]
                    pool.wait_ge(s_ep2, i + 1)
                    nc.gpsimd.tensor_tensor(lns[:, 1, tt:tt + 1], lns[:, 0, tt:tt + 1], lns[:, 2, tt:tt + 1], ALU.pow)\
                        .then_inc(s_rs2, 1)
                if kind == "ZT" and n + 1 < B:
                    pool_residual(pool, n + 1)

        def pool_residual(pool, n):
            if n == 0:
                pool.wait_ge(s_bol, 16)
            pool.wait_ge(s_ga[n % 2], 32 * (n // 2 + 1))
            pool.wait_ge(s_x1l[n % 2], 16 * (n // 2 + 1))
            nc.gpsimd.tensor_tensor(GBO[:, 1, :], GBO[:, 0, :], GT[:, n % 2, 0, :], ALU.mult).then_inc(s_gbo, 1)
            pool.wait_ge(s_gbo, n + 1)
            for tt in range(QB):
                nc.gpsimd.tensor_tensor(X1[:, n % 2, tt, :], X1[:, n % 2, tt, :], GBO[:, 1, :], ALU.add).then_inc(s_xb, 1)

        def sp_gather_experts(sp):
            sp.wait_ge(s_ix, 3)
            for e in range(E_ACT):
                ex = sp.value_load(idx[0:1, 0, e:e + 1], min_val=0, max_val=E_TOT - 1)
                sp.dma_start(ar_dram[:, e * EZ:(e + 1) * EZ],
                             loraAT[:, bass.ds(ex, 1), :].rearrange("c a r -> c (a r)")).then_inc(s_gath, 16)
                sp.dma_start(br_dram[e * RANK:(e + 1) * RANK, :],
                             loraBT[bass.ds(ex, 1), :, :].rearrange("a r c -> (a r) c")).then_inc(s_gath, 16)
                sp.dma_start(rp_dram[:, 2 * e:2 * e + 2], bias_prior[bass.ds(ex, 1), :]).then_inc(s_gath, 16)

        def sp_load_attention(sp, n):
            for par in range(2):
                sp.wait_ge(s_ao[par], 16 * 2 * (n + 1))
            sp.dma_start(AON[:, n % 2, :, :], ao_dram[n * L:(n + 1) * L, :].rearrange("(q p) c -> p q c", p=128))\
                .then_inc(s_ald[n % 2], 16)

        def sp_load_residual(sp, n):
            sp.dma_start(X1[:, n % 2, :, :], x[n, :, :].rearrange("(q p) c -> p q c", p=128)).then_inc(s_x1l[n % 2], 16)

        def sp_load_gates(sp, n):
            for g in range(2):
                sp.dma_start(GT[:, n % 2, g, :], gate_dram[g, n:n + 1, :].to_broadcast([128, D])).then_inc(s_ga[n % 2], 16)

        def sp_early_loads(sp):
            for h in range(2):
                sp.wait_ge(s_st_[h], 12 * NU)
            sp_load_attention(sp, 0)
            sp_load_attention(sp, 1)
            sp_load_residual(sp, 0)
            sp_load_residual(sp, 1)

        def sp_phase_b(sp):
            sp.wait_ge(s_ao[1], 16 * NU // 2)
            sp.dma_start(GBO[:, 0, :], bo.to_broadcast([128, D])).then_inc(s_bol, 16)
            sp.wait_ge(s_gate, 2)
            for g, row in enumerate((0, 3)):
                sp.dma_start(gate_dram[g, :, :], MOD[0:B, row, :]).then_inc(s_gst, 16)
            sp.wait_ge(s_gst, 32)
            sp_load_gates(sp, 0)
            sp_load_gates(sp, 1)
            sp.wait_ge(s_gath, 16 * 3 * E_ACT)
            sp.dma_start(ARW[:, :, :], ar_dram.rearrange("(t p) c -> p t c", p=128)).then_inc(s_lw, 16)
            for r in range(3):
                sp.dma_start(BR[r * ZR:(r + 1) * ZR, :], br_dram).then_inc(s_lw, 16)
            for r in range(2):
                sp.dma_start(BR[3 * ZR + r:3 * ZR + r + 1, :], b_base).then_inc(s_lw, 16)
            sp.dma_start(RPB[:, :, :].rearrange("p e a -> p (e a)"), rp_dram.to_broadcast([128, 2 * E_ACT])).then_inc(s_lw, 16)
            for step in STEPS:
                kind, n = step[0], step[1]
                if kind == "T" and n + 1 < B:
                    sp.wait_ge(s_tb, tile_of("T", n - 1, KT - 1) + 1)
                    sp_load_attention(sp, n + 1)
                if kind == "FL":
                    i = QB * n + step[2]
                    sp.wait_ge(s_y, i + 1)
                    sp.dma_start(out[i * 128:(i + 1) * 128, :], T2[:, i % 2, :]).then_inc(s_out[i % 2], 16)
                    if step[2] == QB - 1 and n + 2 < B:
                        sp_load_residual(sp, n + 2)
                        sp_load_gates(sp, n + 2)
            for par in range(2):
                sp.wait_ge(s_out[par], 16 * B * QB // 2)


        @block.tensor
        def _(pe):
            pe.sem_inc(s_pv, 1)
            pe.wait_ge(s_sc, 1)
            for fill, (kind, arg) in enumerate(PRE):
                if kind == "m" and arg == 0:
                    pe.wait_ge(s_wm, 16)
                if kind == "x" and arg == 0:
                    pe.wait_ge(s_id, 2)
                    for bnk in range(2):
                        pe.wait_ge(s_pjf[bnk], 1)
                    for n in range(2 * KT):
                        mm = nc.tensor.transpose(PT[:, n * B:(n + 1) * B], AO[0:B, n // KT, n % KT, :], ident[0:B, 0:B])
                    mm.then_inc(s_pt0, 1)
                    pe.wait_ge(s_xh, 4)
                if kind == "q" and arg == 0:
                    pe.wait_ge(s_hl, 4)
                    pe.wait_ge(s_wlo, 1)
                if kind == "k" and arg == 0:
                    pe.wait_ge(s_wlo, 2)
                if kind == "v" and arg == (0, 0):
                    pe.wait_ge(s_wlo, 3)
                pe_aux_products(pe, 0, kind, arg, fill, range(COST[kind][0]))
            pe.wait_ge(s_init, 1)
            pe.wait_ge(s_od, 1)
            for k in range(SLOTS):
                pe_max_fill(pe, 0, 0, k)
            pe_max_transpose(pe, 0, 0)
            pe.wait_ge(s_ones, 32)
            phase_a(pe, pe_slot)
            last_group = 2 * NU - 1
            pe_tile_transposes(pe, "T", 0)
            pe_pv(pe, B - 1, last_group - 8 * (B - 1), range(QB))
            pe_out_transpose(pe, B - 1, last_group - 8 * (B - 1))
            pe_phase_b(pe)

        @block.scalar
        def _(act):
            act.wait_ge(s_c, 16)
            nc.scalar.activation(silu_c[:, 1, :, :], silu_c[:, 0, :, :], ACT.Exp, scale=-1.0).then_inc(s_e, 1)
            for n, W in enumerate((WQ, WK, WV)):
                act.wait_ge(s_raw[n], 16)
                nc.scalar.activation(W[0][:, :, :], raw_w[n], ACT.Copy).then_inc(s_whi, 1)
            act.wait_ge(s_bias, 16)
            for fill, (kind, arg) in enumerate(PRE):
                if kind == "x" and arg == 0:
                    act.wait_ge(s_pt0, 2)
                act_aux(act, 0, kind, arg, fill, pre_unit(kind, arg))
            act_max_rows(act, 0, 0)
            phase_a(act, act_slot)
            for kind, arg, fill, oo in ended(4, 0, True):
                act_aux(act, B - 1, kind, arg, fill, oo)
            act_tile_transposes(act, "T", 0)
            act_out(act, B - 1, 2 * NU - 1 - 8 * (B - 1))
            act_phase_b(act)

        @block.vector
        def _(dve):
            dve.wait_ge(s_e, 1)
            nc.vector.tensor_scalar(silu_c[:, 1, :, :], silu_c[:, 1, :, :], 1.0, None, ALU.add).then_inc(s_d1, 1)
            dve.wait_ge(s_d1, 1)
            nc.vector.reciprocal(silu_c[:, 2, :, :], silu_c[:, 1, :, :]).then_inc(s_d1, 1)
            dve.wait_ge(s_d1, 2)
            nc.vector.tensor_tensor(silu_c[:, 3, :, :], silu_c[:, 0, :, :], silu_c[:, 2, :, :], ALU.mult).then_inc(s_sc, 1)
            dve.wait_ge(s_idx, 16)
            nc.vector.tensor_scalar(idx[:, 1, :], idx[:, 0, :], 0, E_TOT, ALU.is_lt, ALU.mult).then_inc(s_ix, 1)
            dve.wait_ge(s_ix, 1)
            nc.vector.tensor_tensor(idx[:, 2, :], idx[:, 0, :], idx[:, 1, :], ALU.add).then_inc(s_ix, 1)
            dve.wait_ge(s_ix, 2)
            nc.vector.tensor_scalar(idx[:, 0, :], idx[:, 2, :], 0, E_TOT - 1, ALU.max, ALU.min).then_inc(s_ix, 1)
            nc.vector.memset(PO[:, :], 0.0).then_inc(s_od, 1)
            for tt in range(QB):
                dve_stats(dve, 0, 0, tt)
            dve_aggregate(dve, 0, 0)
            for n, W in enumerate((WQ, WK, WV)):
                dve.wait_ge(s_whi, n + 1)
                nc.vector.tensor_tensor(W[1][:, :, :], raw_w[n], W[0][:, :, :].bitcast(F32), ALU.subtract)\
                    .then_inc(s_wlo, 1)
            dve.wait_ge(s_pt0, 1)
            nc.vector.tensor_copy(modT[:, 0, :, :], PT[:, 0:KT * B].rearrange("p (t b) -> p t b", b=B))
            nc.vector.tensor_scalar(modT[:, 1, :, :], PT[:, KT * B:2 * KT * B].rearrange("p (t b) -> p t b", b=B), 1.0,
                                    None, ALU.add).then_inc(s_pt0, 1)
            dve.wait_ge(s_pt0, 2)
            dve.wait_ge(s_ones, 32)
            for fill, (kind, arg) in enumerate(PRE):
                dve_aux(dve, 0, kind, arg, fill, pre_unit(kind, arg))
            dve.wait_ge(s_init, 1)
            for k in range(SLOTS):
                dve_max(dve, 0, 0, k)
                if k % 6 == 5:
                    dve_neg_max(dve, 0, k // 6)
            phase_a(dve, dve_slot)
            dve_tile_transposes(dve, "T", 0)
            dve_out(dve, B - 1, 2 * NU - 1 - 8 * (B - 1))
            dve_phase_b(dve)

        @block.gpsimd
        def _(pool):
            nc.gpsimd.memset(lns[:, 2, :], -0.5)
            nc.gpsimd.memset(HF[:, :], 1.0).then_inc(s_one, 1)
            nc.gpsimd.memset(ident[:, :], 0.0).then_inc(s_id, 1)
            pool.wait_ge(s_id, 1)
            nc.gpsimd.affine_select(out=ident[:, :], in_=ident[:, :], compare_op=ALU.not_equal, fill=1.0, base=0,
                                    pattern=[[-1, 128]], channel_multiplier=1).then_inc(s_id, 1)
            pool_norm(pool, 0, 0)
            for tt in range(QB):
                pool_xhat(pool, 0, 0, tt)
            nc.gpsimd.memset(tri[:, :], 0.0).then_inc(s_id, 1)
            pool.wait_ge(s_id, 3)
            nc.gpsimd.affine_select(out=tri[:, L - 128:L], in_=tri[:, L - 128:L], compare_op=ALU.is_ge, fill=NEG,
                                    base=0, pattern=[[-1, 128]], channel_multiplier=1)
            nc.gpsimd.memset(V[:, :, :, HD:VW], 1.0).then_inc(s_init, 1)
            for fill, (kind, arg) in enumerate(PRE):
                pool_aux(pool, 0, kind, arg, fill, pre_unit(kind, arg))
            phase_a(pool, pool_slot)
            pool_tile_transposes(pool, "T", 0)
            pool_phase_b(pool)

        @block.sync
        def _(sp):
            sp.dma_start(silu_c[:, 0, :, :], cT.rearrange("(t p) b -> p t b", p=128)).then_inc(s_c, 16)
            sp_load_x(sp, 0, 0)
            sp.dma_start(idx[:, 0, :], active).then_inc(s_idx, 16)
            sp.dma_start(wm_first, wmod[:, 0:2 * D].rearrange("(t p) c -> p t c", p=128)).then_inc(s_wm, 16)
            sp.dma_start(bcol[:, :, :], bqkv_cols).then_inc(s_bias, 16)
            for n, W in enumerate((WqT, WkT, WvT)):
                sp.dma_start(raw_w[n], W.rearrange("(t p) c -> p t c", p=128)).then_inc(s_raw[n], 16)
            sp.wait_ge(s_one, 1)
            for h in range(2):
                sp.dma_start(KS[64 * h + SHIFT_ROWS:64 * h + SHIFT_ROWS + 2, :, :, :].rearrange("p f j t -> p (f j) t")
                             .bitcast(F32), HF[0:2, :].unsqueeze(1).to_broadcast([2, 4 * FT, L])).then_inc(s_ones, 16)
            sp_gather_experts(sp)
            for fill, (kind, arg) in enumerate(PRE):
                if kind in "qk":
                    sp_heads(sp, 0, kind, arg, fill)
            sp_max_rows(sp, 0, 0)
            phase_a(sp, sp_slot)
            sp_early_loads(sp)
            sp_store_ao(sp, B - 1, 3)
            sp_phase_b(sp)


def kernel(L0_attn_x, L0_attn_Wq, L0_attn_bq, L0_attn_Wk, L0_attn_bk, L0_attn_Wv, L0_attn_bv, L0_attn_Wo, L0_attn_bo,
           L0_ffn_W_base, L0_ffn_b_base, L0_ffn_lora_A, L0_ffn_lora_B, L0_ffn_router_W, L0_ffn_router_b,
           L0_ffn_domain_prior, L0_ffn_active, L0_c, L0_wmod):
    import numpy as np
    import concourse.bacc as bacc
    from concourse.bass_utils import run_bass_kernel_spmd

    def unit_order(a):
        return a.reshape(FT, 2, 4, HD, -1).transpose(0, 1, 3, 2, 4).reshape(a.shape)

    def columns(v):
        return v.reshape(KT, 128).T

    def layout(a):
        return np.ascontiguousarray(np.asarray(a))

    n = {k: np.asarray(v) for k, v in dict(
        x=L0_attn_x, Wq=L0_attn_Wq, bq=L0_attn_bq, Wk=L0_attn_Wk, bk=L0_attn_bk, Wv=L0_attn_Wv, bv=L0_attn_bv,
        Wo=L0_attn_Wo, bo=L0_attn_bo, Wb=L0_ffn_W_base, bb=L0_ffn_b_base, A=L0_ffn_lora_A, Bm=L0_ffn_lora_B,
        R=L0_ffn_router_W, rb=L0_ffn_router_b, prior=L0_ffn_domain_prior, act=L0_ffn_active, c=L0_c, wmod=L0_wmod).items()}
    arrays = dict(
        x=n["x"], WqT=unit_order(n["Wq"]).T, WkT=unit_order(n["Wk"]).T, WvT=n["Wv"].T,
        bqkv_cols=np.stack([columns(unit_order(n["bq"])), columns(unit_order(n["bk"])), columns(n["bv"])], axis=1),
        WoT=n["Wo"].T, bo=n["bo"].reshape(1, D), WbT=n["Wb"].T, b_base=n["bb"].reshape(1, D),
        loraAT=np.concatenate([n["A"], n["R"][:, None, :]], axis=1).transpose(2, 0, 1),
        loraBT=n["Bm"].transpose(0, 2, 1), bias_prior=np.stack([n["rb"], n["prior"]], axis=1), active=n["act"].reshape(1, E_ACT),
        cT=n["c"].T, wmod=n["wmod"])
    nc = bacc.Bacc("TRN2", target_bir_lowering=False, num_devices=1)
    ins, args = {}, []
    for name, a in arrays.items():
        ins[f"in_{name}"] = layout(a)
        args.append(nc.dram_tensor(f"in_{name}", ins[f"in_{name}"].shape, mybir.dt.from_np(ins[f"in_{name}"].dtype),
                                   kind="ExternalInput").ap())
    args.append(nc.dram_tensor("out_0", [B * L, D], F32, kind="ExternalOutput").ap())
    adaln_block_kernel(nc, *args)
    r = run_bass_kernel_spmd(nc, [ins], core_ids=[0])
    return r.results[0]["out_0"].reshape(B, L, D)
```

```python
import concourse.bass as bass
from concourse import mybir
from concourse.alu_op_type import AluOpType as ALU
from contextlib import ExitStack

F32 = mybir.dt.float32
F32R = mybir.dt.float32r
BF16 = mybir.dt.bfloat16
I32 = mybir.dt.int32
ACT = mybir.ActivationFunctionType
AX_X = mybir.AxisListType.X

B, L, D, H = 4, 512, 512, 32
HD = D // H
KT = D // 128
QB = L // 128
FT = KT
NU = B * FT
SLOTS = 12
VW = HD + 1
E_TOT, E_ACT, RANK = 16, 4, 8
EZ = RANK + 1
ZR = E_ACT * RANK
NEG = -3.0e38
EPS = 1e-5
SHIFT_ROWS = 48
FILL_OFF = [0, 512, 1024]
P_LEN = 1280
BLK_OFF = [0, 512, 1024, 896]


def aux_fills(ft, last):
    if ft == -1:
        return [([("q", 1), ("k", 1)], 0, 0), ([("v", (0, tt)) for tt in range(QB)], 1, 11)]
    if ft == 0:
        return [([("q", 2), ("k", 2)], 0, 6), ([("v", (1, 0)), ("v", (1, 1))], 7, 11)]
    if ft == 1:
        return [([("q", 3), ("k", 3)], 0, 5), ([("v", (1, 2)), ("v", (1, 3))], 6, 8)] + \
            ([] if last else [([("x", kt)], 9 + kt, 9 + kt) for kt in range(KT - 1)])
    if last:
        return [([("m", 2 * (ft - 1)), ("m", 2 * (ft - 1) + 1)], 3 * ft - 3, 8)]
    if ft == 2:
        return [([("x", KT - 1)], 0, 0), ([("q", 0), ("k", 0)], 1, 7), ([("v", (0, 0)), ("v", (0, 1))], 7, 11)]
    return [([("q", 1), ("k", 1)], 0, 6), ([("v", (0, 2)), ("v", (0, 3))], 7, 11)]


COST = {"q": (12, 216), "k": (12, 216), "v": (12, 109), "x": (4, 109), "m": (16, 74)}
SLOT_COST = [860, 2340, 1130, 1620, 980, 870] * 2


def aux_plan(ft, last):
    fills, slots, ends = [], [[] for _ in range(SLOTS)], []
    for kinds, first, final in aux_fills(ft, last):
        products = [(len(fills) + f, n, COST[kind][1]) for f, (kind, _) in enumerate(kinds) for n in range(COST[kind][0])]
        whole = sum(c for _, _, c in products)
        low, high = 0, 20000
        while high - low > 1:
            level = (low + high) // 2
            fits = sum(max(0, level - c) for c in SLOT_COST[first:final + 1]) >= whole
            low, high = (low, level) if fits else (level, high)
        k, room = first, max(0, high - SLOT_COST[first])
        for f, n, c in products:
            while room < c // 2 and k < final:
                k += 1
                room += max(0, high - SLOT_COST[k])
            room -= c
            slots[k].append((f, n))
            ends[f:] = [k]
        fills += kinds
    return fills, slots, ends


def fill_base(o, last):
    if o < 0:
        return PRE_FILLS
    units = [sum(len(kinds) for kinds, _, _ in aux_fills(n, last)) for n in range(FT)]
    return FILLS_0 + FILLS_B * (o // FT) + sum(units[:o % FT])


FILLS_B = 20
PRE_FILLS = 2
FILLS_0 = 8


ALL_FILLS = fill_base(FT - 1, True) + FILLS_B * (B - 1) + 2


def at(b, per_batch, offset):
    return b * per_batch + offset



def adaln_block_kernel(nc, x, WqT, WkT, WvT, bqkv_cols, WoT, bo, WbT, b_base, loraAT, loraBT, bias_prior, active,
                       cT, wmod, out):
    ao_dram = nc.dram_tensor("ao_dram", [B * L, D], F32, kind="Internal").ap()
    ar_dram = nc.dram_tensor("ar_dram", [D, ZR + E_ACT], F32, kind="Internal").ap()
    br_dram = nc.dram_tensor("br_dram", [ZR, D], F32, kind="Internal").ap()
    rp_dram = nc.dram_tensor("rp_dram", [1, 2 * E_ACT], F32, kind="Internal").ap()
    x_rows = x.rearrange("b t c -> (b t) c")
    gate_dram = nc.dram_tensor("gate_dram", [2, D // 128, 32, 128], F32, kind="Internal").ap()

    ctx = ExitStack()
    with ctx:
        def sb(name, shape, dt=F32, stack=ctx):
            return stack.enter_context(nc.sbuf_tensor(name, shape, dt))

        def sem(name):
            return ctx.enter_context(nc.semaphore(name))

        ident = sb("ident", [128, 128])
        modT = sb("modT", [128, 4, KT, B])
        bcol = sb("bcol", [128, 3, KT])
        silu_c = sb("silu_c", [128, 4, KT, B])
        lnw = sb("lnw", [128, QB, 6])
        lnm = sb("lnm", [128, QB, 2])
        veps, rstd, neg_half = sb("veps", [128, QB]), sb("rstd", [128, QB]), sb("neg_half", [128, QB])
        idx = sb("idx", [1, 3, E_ACT], I32)
        with ExitStack() as pa:
            WQ = [sb(f"WQ{i}", [128, KT, D], F32R, pa) for i in range(2)]
            WK = [sb(f"WK{i}", [128, KT, D], F32R, pa) for i in range(2)]
            WV = [sb(f"WV{i}", [128, KT, D], F32R, pa) for i in range(2)]
            HT = [sb(f"HT{i}", [128, KT, L], F32R, pa) for i in range(2)]
            QS = sb("QS", [128, FT, 4, L], F32R, pa)
            KS = sb("KS", [128, FT, 4, L], F32R, pa)
            PR = sb("PR", [128, 2, 4, P_LEN], F32, pa)
            V = sb("V", [128, QB, H, VW], F32, pa)
            XH = sb("XH", [128, QB, D], F32, pa)
            QE = sb("QE", [128, 2, L], F32R, pa)
            KE = sb("KE", [128, 2, L], F32R, pa)
            HF = sb("HF", [128, 2, L], F32, pa)
            OE = sb("OE", [128, L], F32, pa)
            AO = sb("AO", [128, 2, QB, 128], F32, pa)
            tri = sb("tri", [128, L], BF16, pa)
            MB = sb("MB", [128, 2, 2 * QB, 2], F32, pa)
            NM = sb("NM", [128, 2 * QB, 2, 2], F32R, pa)
            MT = sb("MT", [8, L], F32R, pa)
            RD = sb("RD", [128, 2 * QB, 2], F32, pa)
        pbs = ctx
        WO = [sb(f"WO{i}", [128, KT, D], F32R, pbs) for i in range(2)]
        WB = [sb(f"WB{i}", [128, KT, D], F32R, pbs) for i in range(2)]
        wm_late = sb("wm_late", [128, KT, 2 * D], F32, pbs)
        with ExitStack() as early:
            raw_late = sb("raw_late", [128, 2, KT, D], F32, early)
        AT1 = [sb(f"AT1{i}", [128, KT, L], F32R, pbs) for i in range(2)]
        AON = sb("AON", [128, 2, QB, D], F32, pbs)
        X1 = sb("X1", [128, 2, QB, D], F32, pbs)
        AT0 = [sb(f"AT0{i}", [128, KT, L], F32R, pbs) for i in range(2)]
        AT = [AT0, AT1]
        HF2 = sb("HF2", [128, 2, L], F32, pbs)
        T1 = sb("T1", [128, 2, D], F32, pbs)
        XH2 = sb("XH2", [128, QB, D], F32, pbs)
        H2 = [[sb(f"H2_{n}_{i}", [128, KT, L], F32R, pbs) for i in range(2)] for n in range(2)]
        ZST = sb("ZST", [98, L], F32R, pbs)
        ZTs = sb("ZTs", [128, L], F32, pbs)
        T2 = sb("T2", [128, 2, D], F32, pbs)
        ART = [sb(f"ART{i}", [128, KT, 128], F32R, pbs) for i in range(2)]
        BT = sb("BT", [98, D], F32R, pbs)
        ZS = sb("ZS", [128, QB, 98], F32R, pbs)
        ZF = sb("ZF", [128, QB, ZR], F32, pbs)
        AL = sb("AL", [128, 4, QB, E_ACT], F32, pbs)
        AR1 = sb("AR1", [128, 3, QB], F32, pbs)
        v_pad = sb("v_pad", [128, 40], F32, pbs)
        MOD = sb("MOD", [128, 4, 128], F32, pbs)
        BR = sb("BR", [98, D], F32, pbs)
        ARW = sb("ARW", [128, KT, ZR + E_ACT], F32, pbs)
        BO = sb("BO", [128, D], F32, pbs)
        G1 = sb("G1", [128, 2, 128], F32, pbs)
        RPB = sb("RPB", [128, E_ACT, 2], F32, pbs)
        losel = sb("losel", [128, 1], F32, pbs)
        xh_pad = sb("xh_pad", [128, 96], F32, pbs)
        GT = sb("GT", [128, 2, 2, D], F32, pbs)
        GBO = sb("GBO", [128, D], F32, pbs)

        bank = [ctx.enter_context(nc.psum_tensor(f"bank{i}", [128, 512], F32)) for i in range(8)]
        MX, ST = bank[0:2], bank[2:4]
        PO, PT = bank[4], bank[5]
        PJ = bank[6:8]

        PRf = PR[:, :, :, :].rearrange("p a h c -> p (a h c)")
        raw_w = [PRf[:, n * KT * D:(n + 1) * KT * D].rearrange("p (t c) -> p t c", t=KT) for n in range(3)]
        wm_first = PRf[:, 3 * KT * D:3 * KT * D + KT * 2 * D].rearrange("p (t c) -> p t c", t=KT)

        s_c, s_xl, s_wm, s_bias = sem("s_c"), sem("s_xl"), sem("s_wm"), sem("s_bias")
        s_raw = [sem(f"s_raw{n}") for n in range(5)]
        s_q = [sem(f"s_q{n}") for n in range(FT)]
        s_k = [sem(f"s_k{n}") for n in range(FT)]
        s_mrow = [sem(f"s_mrow{n}") for n in range(2)]
        s_ao = [sem(f"s_ao{n}") for n in range(2)]
        s_id, s_one, s_init = sem("s_id"), sem("s_one"), sem("s_init")
        s_ones = sem("s_ones")
        s_e, s_d1, s_sc = sem("s_e"), sem("s_d1"), sem("s_sc")
        s_whi, s_wlo = sem("s_whi"), sem("s_wlo")
        s_st, s_ag, s_eps, s_rstd, s_xh = (sem(n) for n in ("s_st", "s_ag", "s_eps", "s_rstd", "s_xh"))
        s_mx = [sem(f"s_mx{h}") for h in range(2)]
        s_mxf = [sem(f"s_mxf{h}") for h in range(2)]
        s_st_ = [sem(f"s_st_{h}") for h in range(2)]
        s_ex = [sem(f"s_ex{h}") for h in range(2)]
        s_nmh, s_nm, s_mtp, s_mtd = sem("s_nmh"), sem("s_nm"), sem("s_mtp"), sem("s_mtd")
        s_mask = sem("s_mask")
        s_pv, s_oe, s_otp, s_rd, s_od = (sem(n) for n in ("s_pv", "s_oe", "s_otp", "s_rd", "s_od"))
        s_pj = sem("s_pj")
        s_pjf = [sem(f"s_pjf{n}") for n in range(2)]
        s_qhi, s_khi = sem("s_qhi"), sem("s_khi")
        s_hh, s_hl = sem("s_hh"), sem("s_hl")
        s_pt0, s_x0, s_hf0 = sem("s_pt0"), sem("s_x0"), sem("s_hf0")
        s_rawl, s_wml, s_lh, s_ll = sem("s_rawl"), sem("s_wml"), sem("s_lh"), sem("s_ll")

        s_idx, s_ix, s_gath = sem("s_idx"), sem("s_ix"), sem("s_gath")
        s_ald, s_x1l = [sem("s_ald0"), sem("s_ald1")], [[sem(f"s_x1l{n}{t}") for t in range(QB)] for n in range(2)]
        s_ga, s_gb, s_gst = *([sem(f"s_g{g}{n}") for n in range(2)] for g in "ab"), sem("s_gst")
        s_lw, s_bol = sem("s_lw"), sem("s_bol")
        s_tb, s_bh, s_bl, s_z2 = sem("s_tb"), sem("s_bh"), sem("s_bl"), sem("s_z2")
        s_bf = [sem("s_bf0"), sem("s_bf1")]
        s_w, s_t1, s_x1, s_st2, s_ag2, s_ep2, s_rs2, s_xh2 = (sem(n) for n in (
            "s_w", "s_t1", "s_x1", "s_st2", "s_ag2", "s_ep2", "s_rs2", "s_xh2"))
        s_gbo, s_xb, s_f, s_t2, s_y = (sem(n) for n in ("s_gbo", "s_xb", "s_f", "s_t2", "s_y"))
        s_zt, s_ztd, s_zn, s_lg, s_ex2, s_zs, s_zsp, s_zst = (sem(n) for n in (
            "s_zt", "s_ztd", "s_zn", "s_lg", "s_ex2", "s_zs", "s_zsp", "s_zst"))
        s_gate, s_ch, s_pc, s_lset, s_btd = (sem(n) for n in ("s_gate", "s_ch", "s_pc", "s_lset", "s_btd"))
        s_out = [sem("s_out0"), sem("s_out1")]

        block = ctx.enter_context(nc.Block())


        def rows(h, n):
            return slice(64 * h, 64 * h + n)

        def wait_apart(eng, sems, count):
            if not isinstance(count, int):
                count = eng.to_reg(count)
                eng.wait_ge(s_init, 1)
            for s in sems:
                eng.wait_ge(s, count)

        def pe_max_fill(pe, b, o, k):
            f, j, s = o % 4, k // 3, k % 3
            if k == 0:
                pe.wait_ge(s_q[f], at(b, 96, 96 * (o // 4 + 1)))
                pe.wait_ge(s_k[f], at(b, 96, 96 * (o // 4 + 1)))
            for h in range(2):
                pe.wait_ge(s_mxf[h], at(b, 48, 12 * o + k))
                for qb, off in [[(3, 0)], [(2, 0), (0, 384)], [(1, 0)]][s]:
                    n = (qb + 1) * 128
                    mm = nc.tensor.matmul(MX[h][:, off:off + n], QS[rows(h, 48), f, j, qb * 128:(qb + 1) * 128],
                                          KS[rows(h, 48), f, j, 0:n], start=True, stop=True)
                mm.then_inc(s_mx[h], 1)

        def pe_score_fill(pe, b, o, k):
            f, j, s = o % 4, k // 3, k % 3
            if k % 6 == 0:
                pe.wait_ge(s_mrow[k // 6], at(b, 128, 32 * (o + 1)))
            for h in range(2):
                pe.wait_ge(s_ex[h], at(b, 48, 12 * o + k))
                for i, off in [[(0, 0)], [(1, 0), (3, 384)], [(2, 0)]][s]:
                    n = L - 128 * i
                    mm = nc.tensor.matmul(ST[h][:, off:off + n], KS[rows(h, 50), f, j, i * 128:(i + 1) * 128],
                                          QS[rows(h, 50), f, j, 128 * i:L], start=True, stop=True)
                mm.then_inc(s_st_[h], 1)

        def pe_max_transpose(pe, b, e):
            pe.wait_ge(s_nm, at(b, 8, e + 1))
            if not (isinstance(b, int) and 8 * b + e < 1):
                pe.wait_ge(s_od, at(b, 8, e - 1))
            for qb in range(QB):
                mm = nc.tensor.transpose(PT[0:8, qb * 128:(qb + 1) * 128],
                                         NM[:, 2 * qb:2 * qb + 2, :, :].rearrange("p a h j -> p (a h j)").bitcast(F32),
                                         ident[:, :])
            mm.then_inc(s_mtp, 1)

        def pe_pv(pe, b, g, blocks):
            f, gi = (g // 2) % 4, g % 2
            if 0 in blocks:
                bb = g // 8
                pe.wait_ge(s_mask, at(b, 16, 2 * g + 2))
                pe.wait_ge(s_oe, at(b, 8, g))
                for n in range(2):
                    pe.wait_ge(s_pjf[n], at(b, 10, 10 * bb + FILLS_0 // 2 + (0 if f < 2 else 4)))
            for i in blocks:
                for h4 in range(4):
                    head = 8 * f + 4 * (h4 // 2) + 2 * gi + h4 % 2
                    mm = nc.tensor.matmul(PO[32 * h4:32 * h4 + VW, 128 * i:L], V[:, i, head, :],
                                          PR[:, gi, h4, BLK_OFF[i]:BLK_OFF[i] + L - 128 * i],
                                          start=(i == 0), stop=(i == QB - 1))
            if QB - 1 in blocks:
                mm.then_inc(s_pv, 1)

        def pe_out_transpose(pe, b, g):
            pe.wait_ge(s_oe, at(b, 8, g + 1))
            pe.wait_ge(s_mtd, min(b * 8 + g + 3, 2 * NU) if isinstance(b, int) else at(b, 8, g + 3))
            pe.wait_ge(s_od, at(b, 8, g + 1))
            for qb in range(QB):
                mm = nc.tensor.transpose(PT[:, qb * 128:(qb + 1) * 128], OE[:, qb * 128:(qb + 1) * 128], ident[:, :])
            mm.then_inc(s_otp, 1)

        def pe_aux_products(pe, b, kind, arg, fill, products):
            dst = PJ[fill % 2]
            n_all = COST[kind][0]
            for n in products:
                if n == 0:
                    pe.wait_ge(s_pjf[fill % 2], at(b, 10, fill // 2))
                if kind in "qk":
                    W = WQ if kind == "q" else WK
                    kt, (wi, hi) = n // 3, [(0, 0), (0, 1), (1, 0)][n % 3]
                    mm = nc.tensor.matmul(dst[:, :], W[wi][:, kt, arg * 128:(arg + 1) * 128], HT[hi][:, kt, :],
                                          start=(n == 0), stop=(n == n_all - 1))
                elif kind == "v":
                    vh, tt = arg
                    kt, (wi, hi) = n // 3, [(0, 0), (1, 0), (0, 1)][n % 3]
                    mm = nc.tensor.matmul(dst[:, 0:256], HT[hi][:, kt, tt * 128:(tt + 1) * 128],
                                          WV[wi][:, kt, vh * 256:(vh + 1) * 256],
                                          start=(n == 0), stop=(n == n_all - 1))
                elif kind == "x":
                    mm = nc.tensor.transpose(dst[:, n * 128:(n + 1) * 128], XH[:, n, arg * 128:(arg + 1) * 128],
                                             ident[:, :])
                else:
                    kt, c = n // 4, n % 4
                    col = (arg % 2) * D + 128 * c
                    mm = nc.tensor.matmul(dst[32 * c:32 * c + B, 0:128], silu_c[:, 3, kt, :], wm_late[:, kt, col:col + 128],
                                          start=(kt == 0), stop=(kt == KT - 1))
                if n == n_all - 1:
                    mm.then_inc(s_pj, 1)

        def pe_aux(pe, b, o, k, last):
            up = o // 4
            fills, slots, _ = aux_plan(o % 4 if o >= 0 else o, last)
            for i, n in slots[k]:
                kind, arg = fills[i]
                if kind == "q" and arg == 0 and n % 3 == 0:
                    pe.wait_ge(s_hl, at(b, 4, 4 * up + 5 + n // 3))
                if n == 0 and kind == "x":
                    pe.wait_ge(s_xh, at(b, 4, 4 * up + 8))
                if n == 0 and o == -1:
                    pe.wait_ge(s_wlo, {"q": 3, "k": 4, "v": 5}[kind])
                if n == 0 and kind == "m" and arg % 2 == 0:
                    pe.wait_ge(s_wml, 16 * (arg // 2))
                pe_aux_products(pe, b, kind, arg, fill_base(o, last) + i, [n])

        def pe_slot(pe, b, o, k, last=False):
            final = last and o == 3
            if o < 0:
                pe_aux(pe, b, o, k, last)
            if not final:
                pe_max_fill(pe, b, o + 1, k)
            if o >= 0:
                pe_score_fill(pe, b, o, k)
            if k == 1 and o >= 0:
                pe_max_transpose(pe, b, 2 * o + 1)
            if k == 7 and not final:
                pe_max_transpose(pe, b, 2 * o + 2)
            first = isinstance(b, int) and 4 * b + o <= 0
            if k in (1, 2, 3) and not first:
                pe_pv(pe, b, 2 * o - 1, [[0], [1], [2, 3]][k - 1])
            if k in (7, 8, 9) and o >= 0:
                pe_pv(pe, b, 2 * o, [[0], [1], [2, 3]][k - 7])
            if k == 5 and not first:
                pe_out_transpose(pe, b, 2 * o - 1)
            if k == 11 and o >= 0:
                pe_out_transpose(pe, b, 2 * o)
            if o >= 0:
                pe_aux(pe, b, o, k, last)
            if final and k in FINAL:
                for step in FINAL[k]:
                    pe_step(pe, step)

        def act_q(act, b, kind, o, fill):
            E, bi, s_hi, s_prev = (QE, 0, s_qhi, s_q) if kind == "q" else (KE, 1, s_khi, s_k)
            f = o % 4
            act.wait_ge(s_pj, at(b, FILLS_B, fill + 1))
            if not (isinstance(b, int) and 4 * b + o == 0):
                act.wait_ge(s_prev[(f - 1) % 4], at(b, 96, 96 * ((o - 1) // 4 + 1)))
            nc.scalar.activation(E[:, 0, :], PJ[fill % 2][:, :], ACT.Identity, bias=bcol[:, bi, f:f + 1])\
                .then_inc(s_hi, 1)

        def act_v(act, b, vh, tt, fill):
            act.wait_ge(s_pj, at(b, FILLS_B, fill + 1))
            nc.scalar.activation(V[:, tt, 16 * vh:16 * vh + 16, 0:HD],
                                 PJ[fill % 2][:, 0:256].rearrange("p (h d) -> p h d", d=HD), ACT.Copy)\
                .then_inc(s_pjf[fill % 2], 1)

        def act_x(act, b, up, kt, fill):
            act.wait_ge(s_pj, at(b, FILLS_B, fill + 1))
            nc.scalar.activation(HT[0][:, kt, :], PJ[fill % 2][:, :], ACT.Identity,
                                 scale=mod_col(1, kt, b, up), bias=mod_col(0, kt, b, up)).then_inc(s_hh, 1)

        def mod_col(which, kt, b, up):
            bb = b + up
            return modT[:, which, kt, bb:bb + 1] if isinstance(bb, int) else modT[:, which, kt, bass.ds(bb, 1)]

        def act_m(act, b, arg, fill):
            act.wait_ge(s_pj, at(b, FILLS_B, fill + 1))
            nc.scalar.activation(MOD[:, arg - 2, :], PJ[fill % 2][:, 0:128], ACT.Copy).then_inc(s_pjf[fill % 2], 1)

        def act_max_rows(act, b, e):
            act.wait_ge(s_mtp, at(b, 8, e + 1))
            act.wait_ge(s_mrow[(e - 1) % 2], at(b, 128, 32 * ((e + 1) // 2)))
            nc.scalar.activation(MT[:, :], PT[0:8, :], ACT.Copy).then_inc(s_mtd, 1)

        def act_exp(act, b, o, k):
            gi, jj, s = k // 6, (k // 3) % 2, k % 3
            if k % 6 == 0:
                act.wait_ge(s_pv, at(b, 8, 2 * o + gi))
            n = [512, 512, 256][s]
            for h in range(2):
                act.wait_ge(s_st_[h], at(b, 48, 12 * o + k + 1))
                nc.scalar.activation(PR[:, gi, 2 * h + jj, FILL_OFF[s]:FILL_OFF[s] + n],
                                     ST[h][:, 0:n], ACT.Exp, scale=HD ** -0.5).then_inc(s_ex[h], 1)

        def act_out(act, b, g):
            act.wait_ge(s_pv, at(b, 8, g + 2))
            act.wait_ge(s_otp, at(b, 8, g))
            nc.scalar.activation(OE[:, :], PO[:, :], ACT.Copy).then_inc(s_oe, 1)

        def ended(o, k, last):
            o, k = (o, k - 1) if k else (o - 1, SLOTS - 1)
            if o < -1:
                return []
            fills, _, ends = aux_plan(o % 4 if o >= 0 else o, last)
            return [(kind, arg, fill_base(o, last) + i, o)
                    for i, ((kind, arg), e) in enumerate(zip(fills, ends)) if e == k]

        def act_slot(act, b, o, k, last=False):
            final = last and o == 3
            first = isinstance(b, int) and 4 * b + o <= 0
            for kind, arg, fill, oo in ended(o, k, last):
                act_aux(act, b, kind, arg, fill, oo)
            if o >= 0:
                act_exp(act, b, o, k)
            if k == 1 and o >= 0:
                act_max_rows(act, b, 2 * o + 1)
            if k == 7 and not final:
                act_max_rows(act, b, 2 * o + 2)
            if k == 3 and not first:
                act_out(act, b, 2 * o - 1)
            if k == 9 and o >= 0:
                act_out(act, b, 2 * o)
            if final and k in FINAL:
                for step in FINAL[k]:
                    act_step(act, step)
            if last and o == 2 and k >= 4:
                if k == 4:
                    act.wait_ge(s_rawl, 32)
                w, kt = (k - 4) // 4, k % 4
                nc.scalar.activation((WO, WB)[w][0][:, kt, :], raw_late[:, w, kt, :], ACT.Copy).then_inc(s_lh, 1)

        def act_aux(act, b, kind, arg, fill, oo):
            if kind in "qk":
                act_q(act, b, kind, oo + 2, fill)
            elif kind == "v":
                act_v(act, b, arg[0], arg[1], fill)
            elif kind == "x":
                act_x(act, b, oo // 4 + 1, arg, fill)
            else:
                act_m(act, b, arg, fill)

        def dve_max(dve, b, o, k):
            jj, s = (k // 3) % 2, k % 3
            for h in range(2):
                wait_apart(dve, [s_mx[h]], at(b, 48, 12 * o + k + 1))
                for qb, off in [[(3, 0)], [(2, 0), (0, 384)], [(1, 0)]][s]:
                    n = (qb + 1) * 128
                    last = nc.vector.tensor_tensor_reduce(
                        out=MX[h][:, off:off + n], in0=MX[h][:, off:off + n], in1=tri[:, L - n:L], scale=1.0, scalar=NEG,
                        op0=ALU.add, op1=ALU.max, accum_out=MB[:, k // 6, 2 * qb + h, jj:jj + 1])
                last.then_inc(s_mxf[h], 1)

        def dve_neg_max(dve, b, e):
            dve.wait_ge(s_mxf[0], at(b, 48, 6 * e + 6))
            dve.wait_ge(s_mxf[1], at(b, 48, 6 * e + 6))
            dve.wait_ge(s_mtp, at(b, 8, e))
            nc.vector.tensor_scalar(NM[:, :, 0, :], MB[:, e % 2, :, :], -1.0, None, ALU.mult).then_inc(s_nmh, 1)
            dve.wait_ge(s_nmh, at(b, 8, e + 1))
            nc.vector.scalar_tensor_tensor(NM[:, :, 1, :], MB[:, e % 2, :, :], -1.0, NM[:, :, 0, :].bitcast(F32), ALU.mult,
                                           ALU.subtract).then_inc(s_nm, 1)

        def dve_out(dve, b, g):
            f, gi = (g // 2) % 4, g % 2
            dve.wait_ge(s_otp, at(b, 8, g + 1))
            if gi == 0:
                o = g // 2
                dve.wait_ge(s_ao[f % 2], at(b, 32, 16 * (2 * (o // 4) + f // 2)))
            view = PT[:, :].rearrange("p (a j w) -> p a j w", j=2, w=32)
            nc.vector.reciprocal(RD[:, :, :], view[:, :, :, HD]).then_inc(s_rd, 1)
            dve.wait_ge(s_rd, at(b, 8, g + 1))
            dst = AO[:, f % 2, :, :].rearrange("p q (h g j w) -> p (q h) g j w", h=2, g=2, j=2)[:, :, gi, :, :]
            nc.vector.tensor_tensor(dst, view[:, :, :, 0:HD], RD[:, :, :].unsqueeze(3).to_broadcast([128, 2 * QB, 2, HD]),
                                    ALU.mult).then_inc(s_od, 1)

        def dve_aux(dve, b, kind, arg, fill, oo):
            if kind in "qk":
                E, bi, s_hi = (QE, 0, s_qhi) if kind == "q" else (KE, 1, s_khi)
                o = oo + 2
                dve.wait_ge(s_hi, at(b, 4, o + 1))
                nc.vector.scalar_tensor_tensor(E[:, 1, :], PJ[fill % 2][:, :], bcol[:, bi, o % 4:o % 4 + 1],
                                               E[:, 0, :].bitcast(F32), ALU.add, ALU.subtract)\
                    .then_inc(s_pjf[fill % 2], 1)
            elif kind == "x":
                up = oo // 4 + 1
                n = 4 * up + arg
                dve.wait_ge(s_hh, at(b, 4, n + 1))
                dve.wait_ge(s_hl, at(b, 4, n - 1))
                nc.vector.tensor_scalar(HF[:, arg % 2, :], PJ[fill % 2][:, :], mod_col(1, arg, b, up), mod_col(0, arg, b, up),
                                        ALU.mult, ALU.add).then_inc(s_pjf[fill % 2], 1)

        def dve_stats(dve, b, n, tt):
            if tt == 0:
                dve.wait_ge(s_xl, at(b, 16, 16 * n + 16))
                if not (isinstance(b, int) and b + n == 0):
                    dve.wait_ge(s_xh, at(b, 4, 4 * n))
            nc.vector.bn_stats(lnw[:, tt, :], XH[:, tt, :]).then_inc(s_st, 1)

        def dve_aggregate(dve, b, n):
            wait_apart(dve, [s_st], at(b, 4, 4 * n + 4))
            for tt in range(QB):
                nc.vector.bn_aggr(lnm[:, tt, :], lnw[:, tt, :]).then_inc(s_ag, 1)
            dve.wait_ge(s_ag, at(b, 4, 4 * n + 4))
            nc.vector.tensor_scalar(veps[:, :], lnm[:, :, 1], EPS, None, ALU.add).then_inc(s_eps, 1)

        def dve_xhat(dve, b, n, tt):
            dve.wait_ge(s_rstd, at(b, 1, n + 1))
            nc.vector.tensor_scalar(XH[:, tt, :], XH[:, tt, :], lnm[:, tt, 0:1], rstd[:, tt:tt + 1], ALU.subtract,
                                    ALU.mult).then_inc(s_xh, 1)

        def dve_slot(dve, b, o, k, last=False):
            first = isinstance(b, int) and 4 * b + o <= 0
            final = last and o == 3
            if not final:
                dve_max(dve, b, o + 1, k)
            if k % 6 == 5 and not final:
                dve_neg_max(dve, b, 2 * (o + 1) + k // 6)
            if k == 5 and not first:
                dve_out(dve, b, 2 * o - 1)
            if k == 11 and o >= 0:
                dve_out(dve, b, 2 * o)
            for kind, arg, fill, oo in ended(o, k, last):
                dve_aux(dve, b, kind, arg, fill, oo)
            if final and k in FINAL:
                for step in [s for s in FINAL[k - 1] if s[0] == "W"] if k > 2 else []:
                    dve_step(dve, step)
                for step in [s for s in FINAL[k] if s[0] == "T"]:
                    dve_step(dve, step)
            if final and k in (0, 9):
                dve_gate(dve, k // 9)
            if o == 1 and not last:
                if k < 3:
                    for tt in ([0], [1], [2, 3])[k]:
                        dve_stats(dve, b, 1, tt)
                if k == 3:
                    dve_aggregate(dve, b, 1)
                if 4 <= k < 4 + QB:
                    dve_xhat(dve, b, 1, k - 4)

        def pool_mask(pool, b, o, k):
            gi, jj = k // 6, (k // 3) % 2
            wait_apart(pool, s_ex, at(b, 48, 12 * o + k + 1))
            for i in range(QB):
                part = PR[:, gi, jj::2, BLK_OFF[i]:BLK_OFF[i] + 128]
                last = nc.gpsimd.affine_select(out=part, in_=part, compare_op=ALU.is_ge, fill=0.0, base=0,
                                               pattern=[[0, 2], [1, 128]], channel_multiplier=-1)
            last.then_inc(s_mask, 1)

        def pool_rstd(pool, b, n):
            pool.wait_ge(s_eps, at(b, 1, n + 1))
            nc.gpsimd.tensor_tensor(rstd[:, :], veps[:, :], neg_half[:, :], ALU.pow).then_inc(s_rstd, 1)

        def pool_aux(pool, b, kind, arg, fill, oo):
            if kind == "x":
                pool.wait_ge(s_pjf[fill % 2], at(b, 10, fill // 2 + 1))
                nc.gpsimd.tensor_tensor(HT[1][:, arg, :], HF[:, arg % 2, :], HT[0][:, arg, :].bitcast(F32), ALU.subtract)\
                    .then_inc(s_hl, 1)

        def pool_slot(pool, b, o, k, last=False):
            final = last and o == 3
            if last and o == 2 and k == 0:
                pool_losel(pool)
            for kind, arg, fill, oo in ended(o, k, last):
                pool_aux(pool, b, kind, arg, fill, oo)
            if k % 3 == 2 and o >= 0:
                pool_mask(pool, b, o, k)
            if final and k in FINAL and k < 10:
                for step in FINAL[k]:
                    pool_step(pool, step)
            if final and k == 8:
                pool_residual(pool, 0, 0)
            if final and k == 10:
                pool_step(pool, ("W", 0, 0))
            if o == 1 and k == 3 and not last:
                pool_rstd(pool, b, 1)
            part = SLOTS * (o - 2) + k - 5
            if last and 0 <= part < 8:
                w, kt = part // 4, part % 4
                pool.wait_ge(s_lh, part + 1)
                nc.gpsimd.tensor_tensor((WO, WB)[w][1][:, kt, :], raw_late[:, w, kt, :],
                                        (WO, WB)[w][0][:, kt, :].bitcast(F32), ALU.subtract).then_inc(s_ll, 1)

        def sp_heads(sp, b, kind, o, fill):
            E, S, s_rows, parts = (QE, QS, s_q, (0, 1, 0)) if kind == "q" else (KE, KS, s_k, (0, 0, 1))
            f = o % 4
            sp.wait_ge(s_pjf[fill % 2], at(b, 10, fill // 2 + 1))
            for r, part in enumerate(parts):
                for h in range(2):
                    sp.dma_start(S[64 * h + 16 * r:64 * h + 16 * r + 16, f, :, :].rearrange("p j t -> p (j t)")
                                 .bitcast(F32), E[64 * h:64 * h + 64, part, :].bitcast(F32)).then_inc(s_rows[f], 16)

        def sp_max_rows(sp, b, e):
            f, gi = (e // 2) % 4, e % 2
            sp.wait_ge(s_mtd, at(b, 8, e + 1))
            for h in range(2):
                sp.dma_start(QS[64 * h + SHIFT_ROWS:64 * h + SHIFT_ROWS + 2, f, 2 * gi:2 * gi + 2, :]
                             .rearrange("p j t -> p (j t)").bitcast(F32), MT[4 * h:4 * h + 4, :].bitcast(F32)).then_inc(s_mrow[gi], 16)

        def sp_store_ao(sp, b, o):
            f, bb = o % 4, b + o // 4
            sp.wait_ge(s_od, at(b, 8, 2 * o + 3))
            rows_ = ao_dram[bass.ds(bb * L, L), :] if not isinstance(bb, int) else ao_dram[bb * L:(bb + 1) * L, :]
            sp.dma_start(rows_.rearrange("(q p) c -> p q c", p=128)[:, :, f * 128:(f + 1) * 128],
                         AO[:, f % 2, :, :]).then_inc(s_ao[f % 2], 16)

        def sp_load_x(sp, b, n):
            bb = b + n
            rows_ = x[bb, :, :] if isinstance(bb, int) else x[bass.ds(bb, 1), :, :].rearrange("a t c -> (a t) c")
            sp.dma_start(XH[:, :, :], rows_.rearrange("(q p) c -> p q c", p=128)).then_inc(s_xl, 16)

        def sp_slot(sp, b, o, k, last=False):
            final = last and o == 3
            first = isinstance(b, int) and 4 * b + o <= 0
            if k == 1 and o >= 0:
                sp_max_rows(sp, b, 2 * o + 1)
            if k == 7 and not final:
                sp_max_rows(sp, b, 2 * o + 2)
            for kind, arg, fill, oo in ended(o, k, last):
                if kind in "qk":
                    sp_heads(sp, b, kind, oo + 2, fill)
            if k == 5 and not first:
                sp_store_ao(sp, b, o - 1)
            if (o, k) == (0, 8) and not last:
                sp.wait_ge(s_pj, at(b, FILLS_B, FILLS_0 - 6))
                sp_load_x(sp, b, 1)
            if last and o == 0 and 0 <= k - 8 < E_ACT:
                sp_gather_expert(sp, k - 8)
            if last and o == 1 and k == 10:
                sp.wait_ge(s_pj, fill_base(2, True) + FILLS_B * b)
                sp.dma_start(wm_late[:, :, :], wmod[:, 2 * D:4 * D].rearrange("(t p) c -> p t c", p=128))\
                    .then_inc(s_wml, 16)
                for w, src in enumerate((WoT, WbT)):
                    sp.dma_start(raw_late[:, w, :, :], src.rearrange("(t p) c -> p t c", p=128)).then_inc(s_rawl, 16)
            if last and o == 2 and k == 9:
                sp_load_lora(sp)
            if last and o == 2 and k == 3:
                for h in range(2):
                    sp.wait_ge(s_st_[h], 12 * (NU - 2))
                sp_load_attention(sp, 0)
                sp_load_attention(sp, 1)
            if last and o == 2 and k == 10:
                sp.wait_ge(s_pj, fill_base(3, True) + FILLS_B * b)
                sp.dma_start(wm_late[:, :, :], wmod[:, 4 * D:6 * D].rearrange("(t p) c -> p t c", p=128))\
                    .then_inc(s_wml, 16)
            if final and k == 0:
                sp_store_gate(sp, 0)
                sp_load_gate(sp, 0, 0)
                sp_load_gate(sp, 0, 1)
                for h in range(2):
                    sp.wait_ge(s_st_[h], 12 * (NU - 1))
                for tt in range(QB):
                    sp_load_residual(sp, 0, tt)
            if final and k == 8:
                sp.wait_ge(s_tb, tile_of("T", 0, KT - 1) + 1)
                sp_load_attention(sp, 2)
            if final and k == 10:
                sp_store_gate(sp, 1)
                sp_load_gate(sp, 1, 0)
                sp_load_gate(sp, 1, 1)

        def phase_a(eng, slot):
            for n in range(-SLOTS, 6):
                slot(eng, 0, n // SLOTS, n % SLOTS)
            with eng.Fori(0, B - 1) as b:
                for n in range(6, 4 * SLOTS + 6):
                    slot(eng, b, n // SLOTS, n % SLOTS)
            for n in range(6, 4 * SLOTS):
                slot(eng, B - 1, n // SLOTS, n % SLOTS, last=True)

        SLICES = [(WQ, 0, 128), (WK, 0, 128), (WQ, 128, D), (WK, 128, D), (WV, 0, D)]
        raw_of = {id(W): r for W, r in zip((WQ, WK, WV), raw_w)}
        XB = [*MX, *ST]

        FINAL = {2 + n * KT + kt: [("T", n, kt)] for n in range(2) for kt in range(KT)}
        FINAL |= {10: [("W", 0, 0)], 11: [("W", 0, 1)]}
        STEPS = [("W", 0, 3), ("M", 0), ("W", 1, 0), ("L", 0), ("W", 1, 1)] + [("X", 0, kt) for kt in range(KT)]
        for n in range(B):
            w = [[("W", n + 1, tt)] for tt in range(QB)] if n + 1 < B else [[], [("F", n, 0)], [("F", n, 1)], []]
            if n == 0:
                w[0] = w[1] = []
            tiles = [("T", n + 2, kt) for kt in range(KT)] if n + 2 < B else []
            tiles += [("X", n + 1, kt) for kt in range(KT)] if n + 1 < B else []
            t = [tiles[a:c] for a, c in ([(0, 2), (2, 4), (4, 6), (6, 8)] if n + 2 < B else [(0, 0), (0, 1), (1, 3), (3, 4)])]
            STEPS += w[0] + [("ZT", n)] + w[1] + [("ZN", n)] + w[2] + w[3]
            STEPS += ([("F", n, 0)] if n + 1 < B else []) + [("ZS", n)] + t[0] + ([("F", n, 1)] if n + 1 < B else [])
            STEPS += [("FL", n, 0), ("FL", n, 1)] + t[1]
            STEPS += [("F", n, 2), ("FL", n, 2)] + t[2] + [("F", n, 3), ("FL", n, 3)] + t[3]
        TILES = [s for s in [*sum(FINAL.values(), []), *STEPS] if s[0] in "TX"]
        TB, YW, YF, ZB, ZN = bank[0:2], bank[6:8], bank[4:6], bank[2], bank[3]

        def tile_of(kind, n, kt):
            return TILES.index((kind, n, kt))

        def pe_tile(pe, kind, n, kt):
            src = AON[:, n % 2, :, :] if kind == "T" else XH2
            if (kind, n, kt) == ("T", 0, 0):
                for h in range(2):
                    pe.wait_ge(s_mxf[h], 12 * NU)
            if kind == "T":
                pe.wait_ge(s_ald[n % 2], 16 * (n // 2 + 1))
            else:
                pe.wait_ge(s_xh2, QB * (n + 1))
            i = tile_of(kind, n, kt)
            pe.wait_ge(s_bf[i % 2], i // 2)
            for tt in range(QB):
                mm = nc.tensor.transpose(TB[i % 2][:, tt * 128:(tt + 1) * 128], src[:, tt, kt * 128:(kt + 1) * 128],
                                         ident[:, :])
            mm.then_inc(s_tb, 1)

        def pe_products(pe, dst, act_parts, w_parts, tt, wait, stop):
            for kt in range(KT):
                if wait:
                    wait(kt)
                for n, (hi, wi) in enumerate([(0, 0), (0, 1), (1, 0)]):
                    mm = nc.tensor.matmul(dst[:, :], act_parts[hi][:, kt, tt * 128:(tt + 1) * 128], w_parts[wi][:, kt, :],
                                          start=(kt == 0 and n == 0), stop=(stop and kt == KT - 1 and n == 2))
            return mm

        def pe_phase_b(pe):
            for step in STEPS:
                pe_step(pe, step)

        def pe_step(pe, step):
            kind, n = step[0], step[1]
            if kind == "M":
                for h in range(2):
                    pe.wait_ge(s_ex[h], 12 * NU)
                for c in range(2):
                    mm = nc.tensor.transpose(ZN[:, c * 128:(c + 1) * 128], MOD[:, 1 + c, :], ident[:, :])
                mm.then_inc(s_z2, 1)
            if kind in "TX":
                pe_tile(pe, kind, n, step[2])
            if kind == "W":
                tt = step[2]
                i = QB * n + tt
                if i < 2:
                    pe.wait_ge(s_pjf[i], ALL_FILLS // 2)
                    pe.wait_ge(s_ll, 8)
                else:
                    pe.wait_ge(s_t1, i - 1)
                pe_products(pe, YW[i % 2], AT[n % 2], WO, tt, lambda kt: pe.wait_ge(s_bl, tile_of("T", n, kt) + 1), True)\
                    .then_inc(s_w, 1)
            if kind == "ZT":
                if n == 0:
                    pe.wait_ge(s_lset, 2)
                pe.wait_ge(s_zst, n)
                for kt in range(KT):
                    pe.wait_ge(s_bl, tile_of("X", n, kt) + 1)
                    for j, (wi, hi) in enumerate([(0, 0), (1, 0), (0, 1)]):
                        mm = nc.tensor.matmul(ZB[:, :], ART[wi][:, kt, :], H2[n % 2][hi][:, kt, :],
                                              start=(kt == 0 and j == 0), stop=(kt == KT - 1 and j == 2))
                mm.then_inc(s_zt, 1)
            if kind == "F":
                i = QB * n + step[2]
                if i == 0:
                    pe.wait_ge(s_oe, 2 * NU)
                    pe.wait_ge(s_od, 2 * NU + 1)
                pe.wait_ge(s_t2, i - 1 if i > 1 else 0)
                pe_products(pe, YF[i % 2], H2[n % 2], WB, step[2], None, False)
            if kind == "FL":
                i = QB * n + step[2]
                if i == 0:
                    pe.wait_ge(s_btd, 1)
                pe.wait_ge(s_zst, n + 1)
                nc.tensor.matmul(YF[i % 2][:, :], ZST[:, step[2] * 128:(step[2] + 1) * 128], BT[:, :], start=False,
                                 stop=True).then_inc(s_f, 1)
            if kind == "ZN":
                pe.wait_ge(s_ztd, n + 1)
                pe.wait_ge(s_zs, n)
                pe.wait_ge(s_z2, 2)
                for tt in range(QB):
                    mm = nc.tensor.transpose(ZN[:, tt * 36:(tt + 1) * 36], ZTs[0:36, tt * 128:(tt + 1) * 128],
                                             ident[0:36, 0:36])
                mm.then_inc(s_zn, 1)
            if kind == "ZS":
                pe.wait_ge(s_zs, n + 1)
                for tt in range(QB):
                    mm = nc.tensor.transpose(ZB[0:98, tt * 128:(tt + 1) * 128], ZS[:, tt, :].bitcast(F32), ident[:, :])
                mm.then_inc(s_zsp, 1)

        def act_tile(act, kind, n, kt):
            i = tile_of(kind, n, kt)
            act.wait_ge(s_tb, i + 1)
            if kind == "T":
                nc.scalar.activation(AT[n % 2][0][:, kt, :], TB[i % 2][:, :], ACT.Identity, bias=bcol[:, 2, kt:kt + 1])\
                    .then_inc(s_bh, 1)
            else:
                nc.scalar.activation(H2[n % 2][0][:, kt, :], TB[i % 2][:, :], ACT.Identity,
                                     scale=modT[:, 3, kt, n:n + 1], bias=modT[:, 2, kt, n:n + 1]).then_inc(s_bh, 1)

        def act_phase_b(act):
            for step in STEPS:
                act_step(act, step)

        def act_step(act, step):
            kind, n = step[0], step[1]
            if kind in "TX":
                if step == ("X", 0, 0):
                    act.wait_ge(s_z2, 3)
                act_tile(act, kind, n, step[2])
            if kind == "ZT":
                act.wait_ge(s_zt, n + 1)
                act.wait_ge(s_zn, n)
                nc.scalar.activation(ZTs[:, :], ZB[:, :], ACT.Copy).then_inc(s_ztd, 1)
            if kind == "ZN":
                act.wait_ge(s_lg, n + 1)
                nc.scalar.activation(AL[:, 2, :, :], AL[:, 1, :, :], ACT.Exp).then_inc(s_ex2, 1)
            if kind == "ZS":
                act.wait_ge(s_zsp, n + 1)
                act.wait_ge(s_f, QB * n)
                nc.scalar.activation(ZST[:, :], ZB[0:98, :], ACT.Copy).then_inc(s_zst, 1)

        def dve_tile(dve, kind, n, kt):
            i = tile_of(kind, n, kt)
            dve.wait_ge(s_bh, i + 1)
            dve.wait_ge(s_bl, i - 1 if i > 1 else 0)
            if kind == "T":
                op = nc.vector.tensor_scalar(HF2[:, i % 2, :], TB[i % 2][:, :], bcol[:, 2, kt:kt + 1], None, ALU.add)
            else:
                op = nc.vector.tensor_scalar(HF2[:, i % 2, :], TB[i % 2][:, :], modT[:, 3, kt, n:n + 1],
                                             modT[:, 2, kt, n:n + 1], ALU.mult, ALU.add)
            op.then_inc(s_bf[i % 2], 1)

        def dve_gate(dve, g):
            row = (0, 3)[g]
            if g:
                dve.wait_ge(s_gate, 4)
            dve.wait_ge(s_pjf[row % 2], ALL_FILLS // 2 - (0 if g else 1))
            nc.vector.tensor_scalar(G1[:, 0, :], MOD[:, row, :], 0.0, 2.0, ALU.is_ge, ALU.mult).then_inc(s_gate, 1)
            nc.vector.scalar_tensor_tensor(G1[:, 1, :], MOD[:, row, :], -1.0, MOD[:, row, :], ALU.mult, ALU.max)\
                .then_inc(s_gate, 1)
            dve.wait_ge(s_gate, 4 * g + 2)
            nc.vector.tensor_scalar(G1[:, 0, :], G1[:, 0, :], 1.0, None, ALU.subtract).then_inc(s_gate, 1)
            dve.wait_ge(s_gate, 4 * g + 3)
            nc.vector.scalar_tensor_tensor(MOD[:, row, :], G1[:, 1, :], 0.25, G1[:, 0, :], ALU.max, ALU.mult)\
                .then_inc(s_gate, 1)

        chain = [0]

        def dve_phase_b(dve):
            for step in STEPS:
                dve_step(dve, step)

        def dve_step(dve, step):
            def link(ins):
                chain[0] += 1
                ins.then_inc(s_ch, 1)
                dve.wait_ge(s_ch, chain[0])

            kind, n = step[0], step[1]
            def ln_stats(i):
                dve.wait_ge(s_x1, i + 1)
                nc.vector.bn_stats(lnw[:, i % QB, :], X1[:, i // QB % 2, i % QB, :]).then_inc(s_st2, 1)

            def ln_aggregate(i):
                dve.wait_ge(s_st2, i + 1)
                nc.vector.bn_aggr(lnm[:, i % QB, :], lnw[:, i % QB, :]).then_inc(s_ag2, 1)

            def ln_eps(i):
                t = i % QB
                dve.wait_ge(s_ag2, i + 1)
                nc.vector.tensor_scalar(veps[:, t:t + 1], lnm[:, t, 1:2], EPS, None, ALU.add).then_inc(s_ep2, 1)

            def ln_normalise(i):
                n, t = i // QB, i % QB
                dve.wait_ge(s_rs2, i + 1)
                if i == 0:
                    for h in range(2):
                        dve.wait_ge(s_st_[h], 12 * NU)
                if t == 0 and n:
                    dve.wait_ge(s_tb, tile_of("X", n - 1, KT - 1) + 1)
                nc.vector.tensor_scalar(XH2[:, t, :], X1[:, n % 2, t, :], lnm[:, t, 0:1], rstd[:, t:t + 1],
                                        ALU.subtract, ALU.mult).then_inc(s_xh2, 1)

            if kind == "M":
                dve.wait_ge(s_z2, 1)
                for c in range(2):
                    nc.vector.tensor_scalar(modT[:, 2 + c, :, :], ZN[:, c * 128:(c + 1) * 128].rearrange(
                        "p (t w) -> p t w", w=32)[:, :, 0:B], float(c), None, ALU.add).then_inc(s_z2, 1)
            if kind == "L":
                dve.wait_ge(s_pv, 2 * NU + 1)
                nc.vector.memset(ZS[:, :, 96:98].bitcast(F32), 1.0)
                for w in range(2):
                    nc.vector.memset(ART[w][:, :, :].bitcast(F32), 0.0)
                dve.wait_ge(s_lw, 7 * 16)
                nc.vector.tensor_scalar(RPB[:, :, 1], RPB[:, :, 1], 1e-12, None, ALU.add)
                link(nc.vector.tensor_copy(BT[:, :], BR[:, :]))
                nc.vector.tensor_copy(ART[0][:, :, 0:36], ARW[:, :, :]).then_inc(s_lset, 1)
                dve.wait_ge(s_pc, 4)
                nc.vector.scalar_tensor_tensor(BT[:, :], BT[:, :].bitcast(F32), losel[0:98, :], BR[:, :], ALU.mult,
                                               ALU.add).then_inc(s_btd, 1)
                dve.wait_ge(s_lset, 1)
                nc.vector.tensor_tensor(ART[1][:, :, 0:36], ARW[:, :, :], ART[0][:, :, 0:36].bitcast(F32),
                                        ALU.subtract).then_inc(s_lset, 1)
            if kind in "TX":
                dve_tile(dve, kind, n, step[2])
            if kind == "W":
                tt = step[2]
                i = QB * n + tt
                if tt == 0:
                    dve.wait_ge(s_ga[n % 2], 16 * (n // 2 + 1))
                dve.wait_ge(s_w, i + 1)
                nc.vector.tensor_tensor(T1[:, i % 2, :], YW[i % 2][:, :], GT[:, n % 2, 0, :], ALU.mult)\
                    .then_inc(s_t1, 1)
                if tt:
                    ln_stats(i - 1)
                dve.wait_ge(s_t1, i + 1)
                dve.wait_ge(s_xb, i + 1)
                nc.vector.tensor_tensor(X1[:, n % 2, tt, :], T1[:, i % 2, :], X1[:, n % 2, tt, :], ALU.add)\
                    .then_inc(s_x1, 1)
                if tt:
                    ln_aggregate(i - 1)
                if tt == QB - 1:
                    ln_stats(i)
                if tt:
                    ln_eps(i - 1)
                if tt == QB - 1:
                    ln_aggregate(i)
                    ln_eps(i)
                if tt > 1:
                    ln_normalise(i - 2)
                if tt == QB - 1:
                    ln_normalise(i - 1)
                    ln_normalise(i)
            if kind == "ZN":
                zn = ZN[:, 0:QB * 36].rearrange("p (t e z) -> p t e z", e=E_ACT, z=EZ)

                def over_tiles(ap):
                    return ap.unsqueeze(1).to_broadcast([128, QB, E_ACT])

                def over_experts(ap):
                    return ap.unsqueeze(2).to_broadcast([128, QB, E_ACT])

                dve.wait_ge(s_zn, n + 1)
                link(nc.vector.tensor_tensor(AL[:, 0, :, :], zn[:, :, :, RANK], over_tiles(RPB[:, :, 0]), ALU.add))
                link(nc.vector.reduce_max(AR1[:, 0, :], AL[:, 0, :, :], AX_X))
                nc.vector.tensor_tensor(AL[:, 1, :, :], AL[:, 0, :, :], over_experts(AR1[:, 0, :]), ALU.subtract)\
                    .then_inc(s_lg, 1)
                dve.wait_ge(s_ex2, n + 1)
                link(nc.vector.tensor_tensor(AL[:, 0, :, :], AL[:, 2, :, :], over_tiles(RPB[:, :, 1]), ALU.mult))
                link(nc.vector.reduce_sum(AR1[:, 1, :], AL[:, 0, :, :], AX_X))
                link(nc.vector.reciprocal(AR1[:, 2, :], AR1[:, 1, :]))
                link(nc.vector.scalar_tensor_tensor(AL[:, 3, :, :], AL[:, 0, :, :], 2.0, over_experts(AR1[:, 2, :]),
                                                    ALU.mult, ALU.mult))
                if n:
                    dve.wait_ge(s_zsp, n)
                link(nc.vector.tensor_tensor(
                    ZF[:, :, :].rearrange("p t (e r) -> p t e r", r=RANK),
                    zn[:, :, :, 0:RANK],
                    AL[:, 3, :, :].unsqueeze(3).to_broadcast([128, QB, E_ACT, RANK]), ALU.mult))
                link(nc.vector.tensor_copy(ZS[:, :, 0:ZR], ZF[:, :, :]))
                nc.vector.tensor_copy(ZS[:, :, ZR:2 * ZR], ZF[:, :, :])
                nc.vector.tensor_tensor(ZS[:, :, 2 * ZR:3 * ZR], ZF[:, :, :], ZS[:, :, 0:ZR].bitcast(F32),
                                        ALU.subtract).then_inc(s_zs, 1)
            if kind == "FL":
                tt = step[2]
                i = QB * n + tt
                if tt == 0:
                    dve.wait_ge(s_gb[n % 2], 16 * (n // 2 + 1))
                dve.wait_ge(s_f, i + 1)
                dve.wait_ge(s_out[i % 2], 16 * (i // 2))
                nc.vector.tensor_tensor(T2[:, i % 2, :], YF[i % 2][:, :], GT[:, n % 2, 1, :], ALU.mult)\
                    .then_inc(s_t2, 1)
                dve.wait_ge(s_t2, i + 1)
                nc.vector.tensor_tensor(T2[:, i % 2, :], T2[:, i % 2, :], X1[:, n % 2, tt, :], ALU.add)\
                    .then_inc(s_y, 1)

        def pool_tile(pool, kind, n, kt):
            dst = (AT if kind == "T" else H2)[n % 2]
            i = tile_of(kind, n, kt)
            pool.wait_ge(s_bf[i % 2], i // 2 + 1)
            nc.gpsimd.tensor_tensor(dst[1][:, kt, :], HF2[:, i % 2, :], dst[0][:, kt, :].bitcast(F32), ALU.subtract)\
                .then_inc(s_bl, 1)

        def pool_phase_b(pool):
            for step in STEPS:
                pool_step(pool, step)

        def pool_step(pool, step):
            kind, n = step[0], step[1]
            if kind in "TX":
                pool_tile(pool, kind, n, step[2])
            if kind == "M":
                pool_residual(pool, 1, 0)
            if kind == "FL" and step[2] == 2 and n + 2 < B:
                pool_residual(pool, n + 2, 0)
            if kind == "W":
                if step[2] + 1 < QB:
                    pool_residual(pool, n, step[2] + 1)
                for t in [step[2] - 1] * (step[2] > 0) + [QB - 1] * (step[2] == QB - 1):
                    pool.wait_ge(s_ep2, QB * n + t + 1)
                    nc.gpsimd.tensor_tensor(rstd[:, t:t + 1], veps[:, t:t + 1], neg_half[:, t:t + 1], ALU.pow)\
                        .then_inc(s_rs2, 1)

        def pool_losel(pool):
            pool.wait_ge(s_pj, FILLS_0 + FILLS_B * (B - 1))
            nc.gpsimd.memset(losel[:, :], -1.0).then_inc(s_pc, 1)
            for n, (op, fill, base, mult) in enumerate([(ALU.is_ge, 0.0, -ZR, 1), (ALU.is_ge, 0.0, 2 * ZR - 1, -1),
                                                        (ALU.not_equal, -1.0, -3 * ZR - 1, 1)]):
                pool.wait_ge(s_pc, n + 1)
                nc.gpsimd.affine_select(out=losel[:, :], in_=losel[:, :], compare_op=op, fill=fill, base=base,
                                        pattern=[[0, 1]], channel_multiplier=mult).then_inc(s_pc, 1)

        def pool_residual(pool, n, tt):
            if tt == 0:
                if n == 0:
                    pool.wait_ge(s_bol, 16)
                pool.wait_ge(s_xb, QB * n)
                pool.wait_ge(s_ga[n % 2], 16 * (n // 2 + 1))
                nc.gpsimd.tensor_tensor(GBO[:, :], BO[:, :], GT[:, n % 2, 0, :], ALU.mult).then_inc(s_gbo, 1)
            pool.wait_ge(s_gbo, n + 1)
            pool.wait_ge(s_x1l[n % 2][tt], 16 * (n // 2 + 1))
            nc.gpsimd.tensor_tensor(X1[:, n % 2, tt, :], X1[:, n % 2, tt, :], GBO[:, :], ALU.add).then_inc(s_xb, 1)

        def sp_gather_expert(sp, e):
            sp.wait_ge(s_ix, 3)
            ex = sp.value_load(idx[0:1, 0, e:e + 1], min_val=0, max_val=E_TOT - 1)
            sp.dma_start(ar_dram[:, e * EZ:(e + 1) * EZ],
                         loraAT[:, bass.ds(ex, 1), :].rearrange("c a r -> c (a r)")).then_inc(s_gath, 16)
            sp.dma_start(br_dram[e * RANK:(e + 1) * RANK, :],
                         loraBT[bass.ds(ex, 1), :, :].rearrange("a r c -> (a r) c")).then_inc(s_gath, 16)
            sp.dma_start(rp_dram[:, 2 * e:2 * e + 2], bias_prior[bass.ds(ex, 1), :]).then_inc(s_gath, 16)

        def sp_load_attention(sp, n):
            for par in range(2):
                sp.wait_ge(s_ao[par], 16 * 2 * (n + 1))
            sp.dma_start(AON[:, n % 2, :, :], ao_dram[n * L:(n + 1) * L, :].rearrange("(q p) c -> p q c", p=128))\
                .then_inc(s_ald[n % 2], 16)

        def sp_load_residual(sp, n, tt):
            rows_ = (n * QB + tt) * 128
            sp.dma_start(X1[:, n % 2, tt, :], x_rows[rows_:rows_ + 128, :]).then_inc(s_x1l[n % 2][tt], 16)

        def sp_store_gate(sp, g):
            sp.wait_ge(s_gate, 4 * g + 4)
            sp.dma_start(gate_dram[g, :, :, :].rearrange("c b j -> (c b) j"), MOD[:, (0, 3)[g], :]).then_inc(s_gst, 16)
            sp.wait_ge(s_gst, 16 * (g + 1))

        def sp_load_gate(sp, g, n):
            sp.dma_start(GT[:, n % 2, g, :].rearrange("p (c j) -> p c j", j=128),
                         gate_dram[g, :, n, :].unsqueeze(0).to_broadcast([128, D // 128, 128]))\
                .then_inc((s_ga, s_gb)[g][n % 2], 16)

        def sp_load_lora(sp):
            sp.wait_ge(s_pj, FILLS_0 + FILLS_B * (B - 1))
            sp.wait_ge(s_gath, 16 * 3 * E_ACT)
            sp.dma_start(BO[:, :], bo.to_broadcast([128, D])).then_inc(s_bol, 16)
            sp.dma_start(ARW[:, :, :], ar_dram.rearrange("(t p) c -> p t c", p=128)).then_inc(s_lw, 16)
            for r in range(3):
                sp.dma_start(BR[r * ZR:(r + 1) * ZR, :], br_dram).then_inc(s_lw, 16)
            for r in range(2):
                sp.dma_start(BR[3 * ZR + r:3 * ZR + r + 1, :], b_base).then_inc(s_lw, 16)
            sp.dma_start(RPB[:, :, :].rearrange("p e a -> p (e a)"), rp_dram.to_broadcast([128, 2 * E_ACT])).then_inc(s_lw, 16)

        def sp_phase_b(sp):
            sp.wait_ge(s_tb, tile_of("T", 1, KT - 1) + 1)
            sp_load_attention(sp, 3)
            for step in STEPS:
                kind, n = step[0], step[1]
                if kind == "W" and step[2] == QB - 1 and n + 2 < B:
                    sp.wait_ge(s_t1, QB * (n + 1))
                    sp_load_gate(sp, 0, n + 2)
                if kind == "FL":
                    tt = step[2]
                    i = QB * n + tt
                    sp.wait_ge(s_y, i + 1)
                    sp.dma_start(out[i * 128:(i + 1) * 128, :], T2[:, i % 2, :]).then_inc(s_out[i % 2], 16)
                    if n + 2 < B:
                        sp_load_residual(sp, n + 2, tt)
                        if tt == QB - 1:
                            sp_load_gate(sp, 1, n + 2)
            for par in range(2):
                sp.wait_ge(s_out[par], 16 * B * QB // 2)

        @block.tensor
        def _(pe):
            pe.sem_inc(s_pv, 1)
            pe.wait_ge(s_id, 2)
            pe.wait_ge(s_xh, QB)

            def pe_first_x(kt):
                for tt in range(QB):
                    mm = nc.tensor.transpose(XB[kt][:, tt * 128:(tt + 1) * 128], XH[:, tt, kt * 128:(kt + 1) * 128],
                                             ident[:, :])
                mm.then_inc(s_x0, 1)

            pe_first_x(0)
            pe.wait_ge(s_sc, 1)
            pe.wait_ge(s_wm, 16)
            pe.wait_ge(s_od, 1)
            for kt in range(KT):
                for c in range(4):
                    mm = nc.tensor.matmul(PO[32 * c:32 * c + B, 0:256], silu_c[:, 3, kt, :],
                                          wm_first[:, kt, 256 * c:256 * c + 256], start=(kt == 0), stop=(kt == KT - 1))
            mm.then_inc(s_pt0, 1)
            pe_first_x(1)
            pe.wait_ge(s_pt0, 2)
            for n in range(2):
                mm = nc.tensor.transpose(PT[:, n * 128:(n + 1) * 128], OE[:, n * 128:(n + 1) * 128], ident[:, :])
            mm.then_inc(s_pt0, 1)
            pe_first_x(2)
            pe_first_x(3)
            for fill, (kind, kt) in enumerate([("q", 0), ("k", 0)]):
                pe.wait_ge(s_wlo, fill + 1)
                for n in range(COST[kind][0]):
                    if kind == "q" and n % 3 == 0:
                        pe.wait_ge(s_hl, n // 3 + 1)
                    pe_aux_products(pe, 0, kind, 0, fill, [n])
            pe.wait_ge(s_init, 1)
            pe.wait_ge(s_ones, 32)
            phase_a(pe, pe_slot)
            last_group = 2 * NU - 1
            pe_step(pe, ("W", 0, 2))
            pe_pv(pe, B - 1, last_group - 8 * (B - 1), range(QB))
            pe_out_transpose(pe, B - 1, last_group - 8 * (B - 1))
            pe_phase_b(pe)

        @block.scalar
        def _(act):
            act.wait_ge(s_c, 16)
            nc.scalar.activation(silu_c[:, 1, :, :], silu_c[:, 0, :, :], ACT.Exp, scale=-1.0).then_inc(s_e, 1)
            def act_part(n):
                W, lo, hi = SLICES[n]
                act.wait_ge(s_raw[n], 16)
                nc.scalar.activation(W[0][:, :, lo:hi], raw_of[id(W)][:, :, lo:hi], ACT.Copy).then_inc(s_whi, 1)

            act_part(0)
            act_part(1)
            act.wait_ge(s_pt0, 1)
            nc.scalar.activation(OE[:, 0:256], PO[:, 0:256], ACT.Copy).then_inc(s_pt0, 1)
            act.wait_ge(s_bias, 16)
            act.wait_ge(s_pt0, 5)
            for kt in range(KT):
                act.wait_ge(s_x0, kt + 1)
                nc.scalar.activation(HT[0][:, kt, :], XB[kt][:, :], ACT.Identity, scale=mod_col(1, kt, 0, 0),
                                     bias=mod_col(0, kt, 0, 0)).then_inc(s_hh, 1)
            for fill, kind in enumerate("qk"):
                act_part(fill + 2)
                act_q(act, 0, kind, 0, fill)
            act_part(4)
            phase_a(act, act_slot)
            for kind, arg, fill, oo in ended(4, 0, True):
                act_aux(act, B - 1, kind, arg, fill, oo)
            act_out(act, B - 1, 2 * NU - 1 - 8 * (B - 1))
            act_phase_b(act)

        @block.vector
        def _(dve):
            dve.wait_ge(s_e, 1)
            nc.vector.tensor_scalar(silu_c[:, 1, :, :], silu_c[:, 1, :, :], 1.0, None, ALU.add).then_inc(s_d1, 1)
            dve.wait_ge(s_d1, 1)
            nc.vector.reciprocal(silu_c[:, 2, :, :], silu_c[:, 1, :, :]).then_inc(s_d1, 1)
            dve.wait_ge(s_d1, 2)
            nc.vector.tensor_tensor(silu_c[:, 3, :, :], silu_c[:, 0, :, :], silu_c[:, 2, :, :], ALU.mult).then_inc(s_sc, 1)
            dve.wait_ge(s_idx, 16)
            nc.vector.tensor_scalar(idx[:, 1, :], idx[:, 0, :], 0, E_TOT, ALU.is_lt, ALU.mult).then_inc(s_ix, 1)
            dve.wait_ge(s_ix, 1)
            nc.vector.tensor_tensor(idx[:, 2, :], idx[:, 0, :], idx[:, 1, :], ALU.add).then_inc(s_ix, 1)
            dve.wait_ge(s_ix, 2)
            nc.vector.tensor_scalar(idx[:, 0, :], idx[:, 2, :], 0, E_TOT - 1, ALU.max, ALU.min).then_inc(s_ix, 1)
            nc.vector.memset(PO[:, :], 0.0).then_inc(s_od, 1)
            for tt in range(QB):
                dve_stats(dve, 0, 0, tt)
            dve_aggregate(dve, 0, 0)
            for tt in range(QB):
                dve_xhat(dve, 0, 0, tt)
            def dve_part(n):
                W, lo, hi = SLICES[n]
                dve.wait_ge(s_whi, n + 1)
                nc.vector.tensor_tensor(W[1][:, :, lo:hi], raw_of[id(W)][:, :, lo:hi], W[0][:, :, lo:hi].bitcast(F32),
                                        ALU.subtract).then_inc(s_wlo, 1)

            dve_part(0)
            dve_part(1)
            dve.wait_ge(s_pt0, 3)
            mod_cols = PT[:, 0:256].rearrange("p (n c w) -> p c n w", n=2, w=32)
            nc.vector.tensor_copy(modT[:, 0, :, :].rearrange("p (c n) b -> p c n b", n=2), mod_cols[:, 0:2, :, 0:B])\
                .then_inc(s_pt0, 1)
            nc.vector.tensor_scalar(modT[:, 1, :, :].rearrange("p (c n) b -> p c n b", n=2), mod_cols[:, 2:4, :, 0:B], 1.0,
                                    None, ALU.add).then_inc(s_pt0, 1)
            dve.wait_ge(s_pt0, 5)
            dve.wait_ge(s_ones, 32)
            for kt in range(KT):
                dve.wait_ge(s_hh, kt + 1)
                if kt > 1:
                    dve.wait_ge(s_hl, kt - 1)
                nc.vector.tensor_scalar(HF[:, kt % 2, :], XB[kt][:, :], mod_col(1, kt, 0, 0), mod_col(0, kt, 0, 0),
                                        ALU.mult, ALU.add).then_inc(s_hf0, 1)
            for fill, kind in enumerate("qk"):
                dve_part(fill + 2)
                dve_aux(dve, 0, kind, 0, fill, -2)
            dve_part(4)
            dve.wait_ge(s_init, 1)
            phase_a(dve, dve_slot)
            dve_step(dve, ("W", 0, 1))
            dve_step(dve, ("W", 0, 2))
            dve_out(dve, B - 1, 2 * NU - 1 - 8 * (B - 1))
            dve_phase_b(dve)

        @block.gpsimd
        def _(pool):
            nc.gpsimd.memset(neg_half[:, :], -0.5)
            nc.gpsimd.memset(HF[:, 0, :], 1.0).then_inc(s_one, 1)
            nc.gpsimd.memset(ident[:, :], 0.0).then_inc(s_id, 1)
            pool.wait_ge(s_id, 1)
            nc.gpsimd.affine_select(out=ident[:, :], in_=ident[:, :], compare_op=ALU.not_equal, fill=1.0, base=0,
                                    pattern=[[-1, 128]], channel_multiplier=1).then_inc(s_id, 1)
            pool_rstd(pool, 0, 0)
            nc.gpsimd.memset(tri[:, :], 0.0).then_inc(s_id, 1)
            pool.wait_ge(s_id, 3)
            nc.gpsimd.affine_select(out=tri[:, L - 128:L], in_=tri[:, L - 128:L], compare_op=ALU.is_ge, fill=NEG,
                                    base=0, pattern=[[-1, 128]], channel_multiplier=1)
            nc.gpsimd.memset(V[:, :, :, HD:VW], 1.0).then_inc(s_init, 1)
            for kt in range(KT):
                pool.wait_ge(s_hf0, kt + 1)
                nc.gpsimd.tensor_tensor(HT[1][:, kt, :], HF[:, kt % 2, :], HT[0][:, kt, :].bitcast(F32), ALU.subtract)\
                    .then_inc(s_hl, 1)
            phase_a(pool, pool_slot)
            pool_step(pool, ("W", 0, 1))
            pool_step(pool, ("W", 0, 2))
            pool_phase_b(pool)

        @block.sync
        def _(sp):
            sp.dma_start(silu_c[:, 0, :, :], cT.rearrange("(t p) b -> p t b", p=128)).then_inc(s_c, 16)
            sp.dma_start(idx[:, 0, :], active).then_inc(s_idx, 16)
            sp_load_x(sp, 0, 0)
            sources = {id(WQ): WqT, id(WK): WkT, id(WV): WvT}

            def sp_weights(n):
                W, lo, hi = SLICES[n]
                sp.dma_start(raw_of[id(W)][:, :, lo:hi],
                             sources[id(W)].rearrange("(t p) c -> p t c", p=128)[:, :, lo:hi]).then_inc(s_raw[n], 16)

            sp.dma_start(wm_first, wmod[:, 0:2 * D].rearrange("(t p) c -> p t c", p=128)).then_inc(s_wm, 16)
            sp.dma_start(bcol[:, :, :], bqkv_cols).then_inc(s_bias, 16)
            for n in range(5):
                sp_weights(n)
            sp.wait_ge(s_one, 1)
            for h in range(2):
                sp.dma_start(KS[64 * h + SHIFT_ROWS:64 * h + SHIFT_ROWS + 2, :, :, :].rearrange("p f j t -> p (f j) t")
                             .bitcast(F32), HF[0:2, 0, :].unsqueeze(1).to_broadcast([2, 4 * FT, L])).then_inc(s_ones, 16)
            for fill, kind in enumerate("qk"):
                sp_heads(sp, 0, kind, 0, fill)
            phase_a(sp, sp_slot)
            for h in range(2):
                sp.wait_ge(s_st_[h], 12 * NU)
            for tt in range(QB):
                sp_load_residual(sp, 1, tt)
            sp_store_ao(sp, B - 1, 3)
            sp_phase_b(sp)


def kernel(L0_attn_x, L0_attn_Wq, L0_attn_bq, L0_attn_Wk, L0_attn_bk, L0_attn_Wv, L0_attn_bv, L0_attn_Wo, L0_attn_bo,
           L0_ffn_W_base, L0_ffn_b_base, L0_ffn_lora_A, L0_ffn_lora_B, L0_ffn_router_W, L0_ffn_router_b,
           L0_ffn_domain_prior, L0_ffn_active, L0_c, L0_wmod):
    import numpy as np
    import concourse.bacc as bacc
    from concourse.bass_utils import run_bass_kernel_spmd

    def unit_order(a):
        return a.reshape(FT, 2, 4, HD, -1).transpose(0, 1, 3, 2, 4).reshape(a.shape)

    def columns(v):
        return v.reshape(KT, 128).T

    def layout(a):
        return np.ascontiguousarray(np.asarray(a))

    n = {k: np.asarray(v) for k, v in dict(
        x=L0_attn_x, Wq=L0_attn_Wq, bq=L0_attn_bq, Wk=L0_attn_Wk, bk=L0_attn_bk, Wv=L0_attn_Wv, bv=L0_attn_bv,
        Wo=L0_attn_Wo, bo=L0_attn_bo, Wb=L0_ffn_W_base, bb=L0_ffn_b_base, A=L0_ffn_lora_A, Bm=L0_ffn_lora_B,
        R=L0_ffn_router_W, rb=L0_ffn_router_b, prior=L0_ffn_domain_prior, act=L0_ffn_active, c=L0_c, wmod=L0_wmod).items()}
    arrays = dict(
        x=n["x"], WqT=unit_order(n["Wq"]).T, WkT=unit_order(n["Wk"]).T, WvT=n["Wv"].T,
        bqkv_cols=np.stack([columns(unit_order(n["bq"])), columns(unit_order(n["bk"])), columns(n["bv"])], axis=1),
        WoT=n["Wo"].T, bo=n["bo"].reshape(1, D), WbT=n["Wb"].T, b_base=n["bb"].reshape(1, D),
        loraAT=np.concatenate([n["A"], n["R"][:, None, :]], axis=1).transpose(2, 0, 1),
        loraBT=n["Bm"].transpose(0, 2, 1), bias_prior=np.stack([n["rb"], n["prior"]], axis=1), active=n["act"].reshape(1, E_ACT),
        cT=n["c"].T, wmod=n["wmod"])
    nc = bacc.Bacc("TRN2", target_bir_lowering=False, num_devices=1)
    ins, args = {}, []
    for name, a in arrays.items():
        ins[f"in_{name}"] = layout(a)
        args.append(nc.dram_tensor(f"in_{name}", ins[f"in_{name}"].shape, mybir.dt.from_np(ins[f"in_{name}"].dtype),
                                   kind="ExternalInput").ap())
    args.append(nc.dram_tensor("out_0", [B * L, D], F32, kind="ExternalOutput").ap())
    adaln_block_kernel(nc, *args)
    r = run_bass_kernel_spmd(nc, [ins], core_ids=[0])
    return r.results[0]["out_0"].reshape(B, L, D)
```

```python
import concourse.bass as bass
from concourse import mybir
from concourse.alu_op_type import AluOpType as ALU
from contextlib import ExitStack

F32 = mybir.dt.float32
F32R = mybir.dt.float32r
BF16 = mybir.dt.bfloat16
I32 = mybir.dt.int32
ACT = mybir.ActivationFunctionType
AX_X = mybir.AxisListType.X

B, L, D, H = 4, 512, 512, 32
HD = D // H
KT = D // 128
QB = L // 128
FT = KT
NU = B * FT
SLOTS = 12
VW = HD + 1
E_TOT, E_ACT, RANK = 16, 4, 8
EZ = RANK + 1
ZR = E_ACT * RANK
NEG = -3.0e38
EPS = 1e-5
SHIFT_ROWS = 48
FILL_OFF = [0, 512, 1024]
P_LEN = 1280
BLK_OFF = [0, 512, 1024, 896]


def aux_fills(ft, last):
    if ft == -1:
        return [([("q", 1), ("k", 1)], 0, 0), ([("v", (0, tt)) for tt in range(QB)], 1, 11)]
    if ft == 0:
        return [([("q", 2), ("k", 2)], 0, 5), ([("v", (1, 0)), ("v", (1, 1))], 6, 11)]
    if ft == 1:
        if last:
            return [([("q", 3), ("k", 3)], 0, 5), ([("v", (1, 2))], 6, 11)]
        return [([("q", 3), ("k", 3)], 0, 4), ([("v", (1, 2)), ("v", (1, 3))], 5, 8)] + \
            [([("x", kt)], 9 + kt, 9 + kt) for kt in range(KT - 1)]
    if last:
        return ([([("v", (1, 3))], 0, 2)] if ft == 2 else []) + \
            [([("m", 2 * (ft - 1)), ("m", 2 * (ft - 1) + 1)], 3 * ft - 3, 8)]
    if ft == 2:
        return [([("x", KT - 1)], 0, 0), ([("q", 0), ("k", 0)], 1, 6), ([("v", (0, 0)), ("v", (0, 1))], 7, 11)]
    return [([("q", 1), ("k", 1)], 0, 5), ([("v", (0, 2)), ("v", (0, 3))], 6, 11)]


COST = {"q": (12, 216), "k": (12, 216), "v": (12, 109), "x": (4, 109), "m": (16, 74)}
SLOT_COST = [860, 2340, 1130, 1620, 980, 870] * 2


def aux_plan(ft, last):
    fills, slots, ends = [], [[] for _ in range(SLOTS)], []
    for kinds, first, final in aux_fills(ft, last):
        products = [(len(fills) + f, n, COST[kind][1]) for f, (kind, _) in enumerate(kinds) for n in range(COST[kind][0])]
        whole = sum(c for _, _, c in products)
        low, high = 0, 20000
        while high - low > 1:
            level = (low + high) // 2
            fits = sum(max(0, level - c) for c in SLOT_COST[first:final + 1]) >= whole
            low, high = (low, level) if fits else (level, high)
        k, room = first, max(0, high - SLOT_COST[first])
        for f, n, c in products:
            while room < c // 2 and k < final:
                k += 1
                room += max(0, high - SLOT_COST[k])
            room -= c
            slots[k].append((f, n))
            ends[f:] = [k]
        fills += kinds
    return fills, slots, ends


def fill_base(o, last):
    if o < 0:
        return PRE_FILLS
    units = [sum(len(kinds) for kinds, _, _ in aux_fills(n, last)) for n in range(FT)]
    return FILLS_0 + FILLS_B * (o // FT) + sum(units[:o % FT])


FILLS_B = 20
PRE_FILLS = 2
FILLS_0 = 8


ALL_FILLS = fill_base(FT - 1, True) + FILLS_B * (B - 1) + 2


def at(b, per_batch, offset):
    return b * per_batch + offset



def adaln_block_kernel(nc, x, WqT, WkT, WvT, bqkv_cols, WoT, bo, WbT, b_base, loraAT, loraBT, bias_prior, active,
                       cT, wmod, out):
    ao_dram = nc.dram_tensor("ao_dram", [B * L, D], F32, kind="Internal").ap()
    ar_dram = nc.dram_tensor("ar_dram", [D, ZR + E_ACT], F32, kind="Internal").ap()
    br_dram = nc.dram_tensor("br_dram", [ZR, D], F32, kind="Internal").ap()
    rp_dram = nc.dram_tensor("rp_dram", [1, 2 * E_ACT], F32, kind="Internal").ap()
    x_rows = x.rearrange("b t c -> (b t) c")
    gate_dram = nc.dram_tensor("gate_dram", [2, D // 128, 32, 128], F32, kind="Internal").ap()

    ctx = ExitStack()
    with ctx:
        def sb(name, shape, dt=F32, stack=ctx):
            return stack.enter_context(nc.sbuf_tensor(name, shape, dt))

        def sem(name):
            return ctx.enter_context(nc.semaphore(name))

        ident = sb("ident", [128, 128])
        modT = sb("modT", [128, 4, KT, B])
        bcol = sb("bcol", [128, 3, KT])
        silu_c = sb("silu_c", [128, 4, KT, B])
        lnw = sb("lnw", [128, QB, 6])
        lnm = sb("lnm", [128, QB, 2])
        veps, rstd, neg_half = sb("veps", [128, QB]), sb("rstd", [128, QB]), sb("neg_half", [128, QB])
        idx = sb("idx", [1, 3, E_ACT], I32)
        with ExitStack() as pa:
            WQ = [sb(f"WQ{i}", [128, KT, D], F32R, pa) for i in range(2)]
            WK = [sb(f"WK{i}", [128, KT, D], F32R, pa) for i in range(2)]
            WV = [sb(f"WV{i}", [128, KT, D], F32R, pa) for i in range(2)]
            HT = [sb(f"HT{i}", [128, KT, L], F32R, pa) for i in range(2)]
            QS = sb("QS", [128, FT, 4, L], F32R, pa)
            KS = sb("KS", [128, FT, 4, L], F32R, pa)
            PR = sb("PR", [128, 2, 4, P_LEN], F32, pa)
            V = sb("V", [128, QB, H, VW], F32, pa)
            XH = sb("XH", [128, QB, D], F32, pa)
            QE = sb("QE", [128, 2, L], F32R, pa)
            KE = sb("KE", [128, 2, L], F32R, pa)
            HF = sb("HF", [128, 2, L], F32, pa)
            OE = sb("OE", [128, L], F32, pa)
            AO = sb("AO", [128, 2, QB, 128], F32, pa)
            tri = sb("tri", [128, L], BF16, pa)
            MB = sb("MB", [128, 2, 2 * QB, 2], F32, pa)
            NM = sb("NM", [128, 2 * QB, 2, 2], F32R, pa)
            MT = sb("MT", [8, L], F32R, pa)
            RD = sb("RD", [128, 2 * QB, 2], F32, pa)
        pbs = ctx
        with ExitStack() as early:
            raw_late = sb("raw_late", [128, 2, KT, D], F32, early)
        AT1 = [sb(f"AT1{i}", [128, KT, L], F32R, pbs) for i in range(2)]
        wm_late = sb("wm_late", [128, KT, 2 * D], F32, pbs)
        WO = [sb(f"WO{i}", [128, KT, D], F32R, pbs) for i in range(2)]
        WB = [sb(f"WB{i}", [128, KT, D], F32R, pbs) for i in range(2)]
        AON = sb("AON", [128, 2, QB, D], F32, pbs)
        X1 = sb("X1", [128, 2, QB, D], F32, pbs)
        AT0 = [sb(f"AT0{i}", [128, KT, L], F32R, pbs) for i in range(2)]
        AT = [AT0, AT1]
        HF2 = sb("HF2", [128, 2, L], F32, pbs)
        T1 = sb("T1", [128, 2, D], F32, pbs)
        XH2 = sb("XH2", [128, QB, D], F32, pbs)
        H2 = [[sb(f"H2_{n}_{i}", [128, KT, L], F32R, pbs) for i in range(2)] for n in range(2)]
        ZST = sb("ZST", [98, L], F32R, pbs)
        ZTs = sb("ZTs", [128, L], F32, pbs)
        T2 = sb("T2", [128, 2, D], F32, pbs)
        ART = sb("ART", [128, KT, 128], F32R, pbs)
        fold = sb("fold", [128, 40], F32, pbs)
        BT = sb("BT", [98, D], F32R, pbs)
        ZS = sb("ZS", [128, QB, 98], F32R, pbs)
        ZF = sb("ZF", [128, QB, ZR], F32, pbs)
        AL = sb("AL", [128, 4, QB, E_ACT], F32, pbs)
        AR1 = sb("AR1", [128, 3, QB], F32, pbs)
        v_pad = sb("v_pad", [128, 512], F32, pbs)
        MOD = sb("MOD", [128, 4, 128], F32, pbs)
        BR = sb("BR", [98, D], F32, pbs)
        ARW = sb("ARW", [128, KT, ZR + E_ACT], F32, pbs)
        BO = sb("BO", [128, D], F32, pbs)
        G1 = sb("G1", [128, 2, 128], F32, pbs)
        RPB = sb("RPB", [128, E_ACT, 2], F32, pbs)
        losel = sb("losel", [128, 1], F32, pbs)
        xh_pad = sb("xh_pad", [128, 96], F32, pbs)
        GT = sb("GT", [128, 2, 2, D], F32, pbs)
        GBO = sb("GBO", [128, D], F32, pbs)

        bank = [ctx.enter_context(nc.psum_tensor(f"bank{i}", [128, 512], F32)) for i in range(8)]
        MX, ST = bank[0:2], bank[2:4]
        PO, PT = bank[4], bank[5]
        PJ = bank[6:8]

        PRf = PR[:, :, :, :].rearrange("p a h c -> p (a h c)")
        raw_w = [PRf[:, n * KT * D:(n + 1) * KT * D].rearrange("p (t c) -> p t c", t=KT) for n in range(3)]
        wm_first = PRf[:, 3 * KT * D:3 * KT * D + KT * 2 * D].rearrange("p (t c) -> p t c", t=KT)

        s_c, s_xl, s_bias = sem("s_c"), sem("s_xl"), sem("s_bias")
        s_xt, s_wm = [sem(f"s_xt{n}") for n in range(QB)], [sem(f"s_wm{n}") for n in range(KT)]
        s_raw = [sem(f"s_raw{n}") for n in range(5)]
        s_q = [sem(f"s_q{n}") for n in range(FT)]
        s_k = [sem(f"s_k{n}") for n in range(FT)]
        s_qg, s_kg = [sem(f"s_qg{n}") for n in range(2)], [sem(f"s_kg{n}") for n in range(2)]
        s_mrow = [sem(f"s_mrow{n}") for n in range(2)]
        s_ao = [sem(f"s_ao{n}") for n in range(2)]
        s_id, s_one, s_init = sem("s_id"), sem("s_one"), sem("s_init")
        s_ones = sem("s_ones")
        s_e, s_d1, s_sc = sem("s_e"), sem("s_d1"), sem("s_sc")
        s_whi, s_wlo = sem("s_whi"), sem("s_wlo")
        s_st, s_ag, s_eps, s_rstd, s_xh = (sem(n) for n in ("s_st", "s_ag", "s_eps", "s_rstd", "s_xh"))
        s_mx = [sem(f"s_mx{h}") for h in range(2)]
        s_mxf = [sem(f"s_mxf{h}") for h in range(2)]
        s_st_ = [sem(f"s_st_{h}") for h in range(2)]
        s_ex = [sem(f"s_ex{h}") for h in range(2)]
        s_nmh, s_nm, s_mtp, s_mtd = sem("s_nmh"), sem("s_nm"), sem("s_mtp"), sem("s_mtd")
        s_mask = sem("s_mask")
        s_pv, s_oe, s_otp, s_rd, s_od = (sem(n) for n in ("s_pv", "s_oe", "s_otp", "s_rd", "s_od"))
        s_pj = sem("s_pj")
        s_pjf = [sem(f"s_pjf{n}") for n in range(2)]
        s_qhi, s_khi = sem("s_qhi"), sem("s_khi")
        s_hh, s_hl = sem("s_hh"), sem("s_hl")
        s_pt0, s_x0, s_hf0 = sem("s_pt0"), sem("s_x0"), sem("s_hf0")
        s_rawl, s_wml = [sem(f"s_rawl{n}") for n in range(4)], [sem(f"s_wml{n}") for n in range(KT)]
        s_lh, s_ll = sem("s_lh"), sem("s_ll")

        s_idx, s_ix, s_gath = sem("s_idx"), sem("s_ix"), sem("s_gath")
        s_ald, s_x1l = [sem("s_ald0"), sem("s_ald1")], [[sem(f"s_x1l{n}{t}") for t in range(QB)] for n in range(2)]
        s_ga, s_gb, s_gst = *([sem(f"s_g{g}{n}") for n in range(2)] for g in "ab"), sem("s_gst")
        s_lw, s_bol = sem("s_lw"), sem("s_bol")
        s_tb, s_bh, s_bl, s_z2 = sem("s_tb"), sem("s_bh"), sem("s_bl"), sem("s_z2")
        s_bf = [sem("s_bf0"), sem("s_bf1")]
        s_w, s_t1, s_x1, s_st2, s_ag2, s_ep2, s_rs2, s_xh2 = (sem(n) for n in (
            "s_w", "s_t1", "s_x1", "s_st2", "s_ag2", "s_ep2", "s_rs2", "s_xh2"))
        s_gbo, s_xb, s_f, s_t2, s_y = (sem(n) for n in ("s_gbo", "s_xb", "s_f", "s_t2", "s_y"))
        s_zt, s_ztd, s_zn, s_lg, s_ex2, s_zs, s_zsp, s_zst = (sem(n) for n in (
            "s_zt", "s_ztd", "s_zn", "s_lg", "s_ex2", "s_zs", "s_zsp", "s_zst"))
        s_gate, s_ch, s_pc, s_lset, s_btd = (sem(n) for n in ("s_gate", "s_ch", "s_pc", "s_lset", "s_btd"))
        s_out = [sem("s_out0"), sem("s_out1")]

        block = ctx.enter_context(nc.Block())


        def rows(h, n):
            return slice(64 * h, 64 * h + n)

        def wait_apart(eng, sems, count):
            if not isinstance(count, int):
                count = eng.to_reg(count)
                eng.wait_ge(s_init, 1)
            for s in sems:
                eng.wait_ge(s, count)

        def max_banks(b, o, k):
            first = isinstance(b, int) and 4 * b + o == 0
            return (ST if first and k % 2 else MX), (1 if first and k else 0)

        def pe_max_fill(pe, b, o, k):
            f, j, s = o % 4, k // 3, k % 3
            if k == 0:
                wait_rows(pe, b, o)
            banks, ahead = max_banks(b, o, k)
            for h in range(2):
                pe.wait_ge(s_mxf[h], at(b, 48, 12 * o + k - ahead))
                for qb, off in [[(3, 0)], [(2, 0), (0, 384)], [(1, 0)]][s]:
                    n = (qb + 1) * 128
                    mm = nc.tensor.matmul(banks[h][:, off:off + n], QS[rows(h, 48), f, j, qb * 128:(qb + 1) * 128],
                                          KS[rows(h, 48), f, j, 0:n], start=True, stop=True)
                mm.then_inc(s_mx[h], 1)

        def pe_score_fill(pe, b, o, k):
            f, j, s = o % 4, k // 3, k % 3
            if k % 6 == 0:
                pe.wait_ge(s_mrow[k // 6], at(b, 128, 32 * (o + 1)))
            for h in range(2):
                pe.wait_ge(s_ex[h], at(b, 48, 12 * o + k))
                for i, off in [[(0, 0)], [(1, 0), (3, 384)], [(2, 0)]][s]:
                    n = L - 128 * i
                    mm = nc.tensor.matmul(ST[h][:, off:off + n], KS[rows(h, 50), f, j, i * 128:(i + 1) * 128],
                                          QS[rows(h, 50), f, j, 128 * i:L], start=True, stop=True)
                mm.then_inc(s_st_[h], 1)

        def pe_max_transpose(pe, b, e):
            pe.wait_ge(s_nm, at(b, 8, e + 1))
            if not (isinstance(b, int) and 8 * b + e < 1):
                pe.wait_ge(s_od, at(b, 8, e - 1))
            for qb in range(QB):
                mm = nc.tensor.transpose(PT[0:8, qb * 128:(qb + 1) * 128],
                                         NM[:, 2 * qb:2 * qb + 2, :, :].rearrange("p a h j -> p (a h j)").bitcast(F32),
                                         ident[:, :])
            mm.then_inc(s_mtp, 1)

        def pe_pv(pe, b, g, blocks):
            f, gi = (g // 2) % 4, g % 2
            if 0 in blocks:
                bb = g // 8
                pe.wait_ge(s_mask, at(b, 16, 2 * g + 2))
                pe.wait_ge(s_oe, at(b, 8, g))
                for n in range(2):
                    pe.wait_ge(s_pjf[n], at(b, 10, 10 * bb + FILLS_0 // 2 + (0 if f < 2 else 4)))
            for i in blocks:
                for h4 in range(4):
                    head = 8 * f + 4 * (h4 // 2) + 2 * gi + h4 % 2
                    mm = nc.tensor.matmul(PO[32 * h4:32 * h4 + VW, 128 * i:L], V[:, i, head, :],
                                          PR[:, gi, h4, BLK_OFF[i]:BLK_OFF[i] + L - 128 * i],
                                          start=(i == 0), stop=(i == QB - 1))
            if QB - 1 in blocks:
                mm.then_inc(s_pv, 1)

        def pe_out_transpose(pe, b, g):
            pe.wait_ge(s_oe, at(b, 8, g + 1))
            pe.wait_ge(s_mtd, min(b * 8 + g + 3, 2 * NU) if isinstance(b, int) else at(b, 8, g + 3))
            pe.wait_ge(s_od, at(b, 8, g + 1))
            for qb in range(QB):
                mm = nc.tensor.transpose(PT[:, qb * 128:(qb + 1) * 128], OE[:, qb * 128:(qb + 1) * 128], ident[:, :])
            mm.then_inc(s_otp, 1)

        def pe_aux_products(pe, b, kind, arg, fill, products):
            dst = PJ[fill % 2]
            n_all = COST[kind][0]
            for n in products:
                if n == 0:
                    pe.wait_ge(s_pjf[fill % 2], at(b, 10, fill // 2))
                if kind in "qk":
                    W = WQ if kind == "q" else WK
                    kt, (wi, hi) = n // 3, [(0, 0), (0, 1), (1, 0)][n % 3]
                    mm = nc.tensor.matmul(dst[:, :], W[wi][:, kt, arg * 128:(arg + 1) * 128], HT[hi][:, kt, :],
                                          start=(n == 0), stop=(n == n_all - 1))
                elif kind == "v":
                    vh, tt = arg
                    kt, (wi, hi) = n // 3, [(0, 0), (1, 0), (0, 1)][n % 3]
                    mm = nc.tensor.matmul(dst[:, 0:256], HT[hi][:, kt, tt * 128:(tt + 1) * 128],
                                          WV[wi][:, kt, vh * 256:(vh + 1) * 256],
                                          start=(n == 0), stop=(n == n_all - 1))
                elif kind == "x":
                    mm = nc.tensor.transpose(dst[:, n * 128:(n + 1) * 128], XH[:, n, arg * 128:(arg + 1) * 128],
                                             ident[:, :])
                else:
                    kt, c = n // 4, n % 4
                    col = (arg % 2) * D + 128 * c
                    mm = nc.tensor.matmul(dst[32 * c:32 * c + B, 0:128], silu_c[:, 3, kt, :], wm_late[:, kt, col:col + 128],
                                          start=(kt == 0), stop=(kt == KT - 1))
                if n == n_all - 1:
                    mm.then_inc(s_pj, 1)

        def pe_aux(pe, b, o, k, last):
            up = o // 4
            fills, slots, _ = aux_plan(o % 4 if o >= 0 else o, last)
            for i, n in slots[k]:
                kind, arg = fills[i]
                if kind == "q" and arg == 0 and n % 3 == 0:
                    pe.wait_ge(s_hl, at(b, 4, 4 * up + 5 + n // 3))
                if n == 0 and kind == "x":
                    pe.wait_ge(s_xh, at(b, 4, 4 * up + 8))
                if n == 0 and o == -1:
                    pe.wait_ge(s_wlo, {"q": 3, "k": 4, "v": 5}[kind])
                if n % 4 == 0 and kind == "m" and arg % 2 == 0:
                    pe.wait_ge(s_wml[n // 4], 16 * (arg // 2))
                pe_aux_products(pe, b, kind, arg, fill_base(o, last) + i, [n])

        def pe_slot(pe, b, o, k, last=False):
            final = last and o == 3
            if o < 0:
                pe_aux(pe, b, o, k, last)
            if not final:
                pe_max_fill(pe, b, o + 1, k)
            if o >= 0:
                pe_score_fill(pe, b, o, k)
            if k == 1 and o >= 0:
                pe_max_transpose(pe, b, 2 * o + 1)
            if k == 7 and not final:
                pe_max_transpose(pe, b, 2 * o + 2)
            first = isinstance(b, int) and 4 * b + o <= 0
            if k in (1, 2, 3) and not first:
                pe_pv(pe, b, 2 * o - 1, [[0], [1], [2, 3]][k - 1])
            if k in (7, 8, 9) and o >= 0:
                pe_pv(pe, b, 2 * o, [[0], [1], [2, 3]][k - 7])
            if k == 5 and not first:
                pe_out_transpose(pe, b, 2 * o - 1)
            if k == 11 and o >= 0:
                pe_out_transpose(pe, b, 2 * o)
            if o >= 0:
                pe_aux(pe, b, o, k, last)
            if final and k in FINAL:
                for step in FINAL[k]:
                    pe_step(pe, step)

        def act_q(act, b, kind, o, fill):
            E, bi, s_hi = (QE, 0, s_qhi) if kind == "q" else (KE, 1, s_khi)
            f = o % 4
            act.wait_ge(s_pj, at(b, FILLS_B, fill + 1))
            if not (isinstance(b, int) and 4 * b + o == 0):
                wait_rows(act, b, o - 1, kind)
            nc.scalar.activation(E[:, 0, :], PJ[fill % 2][:, :], ACT.Identity, bias=bcol[:, bi, f:f + 1])\
                .then_inc(s_hi, 1)

        def act_v(act, b, vh, tt, fill):
            act.wait_ge(s_pj, at(b, FILLS_B, fill + 1))
            nc.scalar.activation(V[:, tt, 16 * vh:16 * vh + 16, 0:HD],
                                 PJ[fill % 2][:, 0:256].rearrange("p (h d) -> p h d", d=HD), ACT.Copy)\
                .then_inc(s_pjf[fill % 2], 1)

        def act_x(act, b, up, kt, fill):
            act.wait_ge(s_pj, at(b, FILLS_B, fill + 1))
            act.wait_ge(s_hl, at(b, 4, 4 * up + kt - 1))
            nc.scalar.activation(HF[:, kt % 2, :], PJ[fill % 2][:, :], ACT.Identity, scale=mod_col(1, kt, b, up),
                                 bias=mod_col(0, kt, b, up)).then_inc(s_pjf[fill % 2], 1)

        def mod_col(which, kt, b, up):
            bb = b + up
            return modT[:, which, kt, bb:bb + 1] if isinstance(bb, int) else modT[:, which, kt, bass.ds(bb, 1)]

        def act_m(act, b, arg, fill):
            act.wait_ge(s_pj, at(b, FILLS_B, fill + 1))
            nc.scalar.activation(MOD[:, arg - 2, :], PJ[fill % 2][:, 0:128], ACT.Copy).then_inc(s_pjf[fill % 2], 1)

        def act_max_rows(act, b, e):
            act.wait_ge(s_mtp, at(b, 8, e + 1))
            act.wait_ge(s_mrow[(e - 1) % 2], at(b, 128, 32 * ((e + 1) // 2)))
            nc.scalar.activation(MT[:, :], PT[0:8, :], ACT.Copy).then_inc(s_mtd, 1)

        def act_exp(act, b, o, k):
            gi, jj, s = k // 6, (k // 3) % 2, k % 3
            if k % 6 == 0:
                act.wait_ge(s_pv, at(b, 8, 2 * o + gi))
            n = [512, 512, 256][s]
            for h in range(2):
                act.wait_ge(s_st_[h], at(b, 48, 12 * o + k + 1))
                nc.scalar.activation(PR[:, gi, 2 * h + jj, FILL_OFF[s]:FILL_OFF[s] + n],
                                     ST[h][:, 0:n], ACT.Exp, scale=HD ** -0.5).then_inc(s_ex[h], 1)

        def act_out(act, b, g):
            act.wait_ge(s_pv, at(b, 8, g + 2))
            act.wait_ge(s_otp, at(b, 8, g))
            nc.scalar.activation(OE[:, :], PO[:, :], ACT.Copy).then_inc(s_oe, 1)

        def ended(o, k, last):
            if (o, k) == (0, 0):
                return []
            if o >= 0:
                o, k = (o, k - 1) if k else (o - 1, SLOTS - 1)
            fills, _, ends = aux_plan(o % 4 if o >= 0 else o, last)
            return [(kind, arg, fill_base(o, last) + i, o)
                    for i, ((kind, arg), e) in enumerate(zip(fills, ends)) if e == k]

        def act_slot(act, b, o, k, last=False):
            final = last and o == 3
            first = isinstance(b, int) and 4 * b + o <= 0
            for kind, arg, fill, oo in ended(o, k, last):
                act_aux(act, b, kind, arg, fill, oo)
            if o >= 0:
                act_exp(act, b, o, k)
            if k == 1 and o >= 0:
                act_max_rows(act, b, 2 * o + 1)
            if k == 7 and not final:
                act_max_rows(act, b, 2 * o + 2)
            if k == 3 and not first:
                act_out(act, b, 2 * o - 1)
            if k == 9 and o >= 0:
                act_out(act, b, 2 * o)
            if final and k in FINAL:
                for step in FINAL[k]:
                    act_step(act, step)
            if last and o == 2 and k >= 4:
                w, kt = (k - 4) // 4, k % 4
                if kt % 2 == 0:
                    act.wait_ge(s_rawl[(k - 4) // 2], 16)
                nc.scalar.activation((WO, WB)[w][0][:, kt, :], raw_late[:, w, kt, :], ACT.Copy).then_inc(s_lh, 1)

        def act_aux(act, b, kind, arg, fill, oo):
            if kind in "qk":
                act_q(act, b, kind, oo + 2, fill)
            elif kind == "v":
                act_v(act, b, arg[0], arg[1], fill)
            elif kind == "x":
                act_x(act, b, oo // 4 + 1, arg, fill)
            else:
                act_m(act, b, arg, fill)

        def dve_max(dve, b, o, k):
            jj, s = (k // 3) % 2, k % 3
            banks, _ = max_banks(b, o, k)
            for h in range(2):
                wait_apart(dve, [s_mx[h]], at(b, 48, 12 * o + k + 1))
                for qb, off in [[(3, 0)], [(2, 0), (0, 384)], [(1, 0)]][s]:
                    n = (qb + 1) * 128
                    last = nc.vector.tensor_tensor_reduce(
                        out=banks[h][:, off:off + n], in0=banks[h][:, off:off + n], in1=tri[:, L - n:L], scale=1.0, scalar=NEG,
                        op0=ALU.add, op1=ALU.max, accum_out=MB[:, k // 6, 2 * qb + h, jj:jj + 1])
                last.then_inc(s_mxf[h], 1)

        def dve_neg_max(dve, b, e):
            dve.wait_ge(s_mxf[0], at(b, 48, 6 * e + 6))
            dve.wait_ge(s_mxf[1], at(b, 48, 6 * e + 6))
            dve.wait_ge(s_mtp, at(b, 8, e))
            nc.vector.tensor_scalar(NM[:, :, 0, :], MB[:, e % 2, :, :], -1.0, None, ALU.mult).then_inc(s_nmh, 1)
            dve.wait_ge(s_nmh, at(b, 8, e + 1))
            nc.vector.scalar_tensor_tensor(NM[:, :, 1, :], MB[:, e % 2, :, :], -1.0, NM[:, :, 0, :].bitcast(F32), ALU.mult,
                                           ALU.subtract).then_inc(s_nm, 1)

        def dve_out(dve, b, g):
            f, gi = (g // 2) % 4, g % 2
            dve.wait_ge(s_otp, at(b, 8, g + 1))
            if gi == 0:
                o = g // 2
                dve.wait_ge(s_ao[f % 2], at(b, 32, 16 * (2 * (o // 4) + f // 2)))
            view = PT[:, :].rearrange("p (a j w) -> p a j w", j=2, w=32)
            nc.vector.reciprocal(RD[:, :, :], view[:, :, :, HD]).then_inc(s_rd, 1)
            dve.wait_ge(s_rd, at(b, 8, g + 1))
            dst = AO[:, f % 2, :, :].rearrange("p q (h g j w) -> p (q h) g j w", h=2, g=2, j=2)[:, :, gi, :, :]
            nc.vector.tensor_tensor(dst, view[:, :, :, 0:HD], RD[:, :, :].unsqueeze(3).to_broadcast([128, 2 * QB, 2, HD]),
                                    ALU.mult).then_inc(s_od, 1)

        def dve_aux(dve, b, kind, arg, fill, oo):
            if kind in "qk":
                E, bi, s_hi = (QE, 0, s_qhi) if kind == "q" else (KE, 1, s_khi)
                o = oo + 2
                dve.wait_ge(s_hi, at(b, 4, o + 1))
                nc.vector.scalar_tensor_tensor(E[:, 1, :], PJ[fill % 2][:, :], bcol[:, bi, o % 4:o % 4 + 1],
                                               E[:, 0, :].bitcast(F32), ALU.add, ALU.subtract)\
                    .then_inc(s_pjf[fill % 2], 1)
            elif kind == "x":
                dve.wait_ge(s_pjf[fill % 2], at(b, 10, fill // 2 + 1))
                nc.vector.tensor_copy(HT[0][:, arg, :], HF[:, arg % 2, :]).then_inc(s_hh, 1)

        def dve_stats(dve, b, n, tt):
            if isinstance(b, int) and b + n == 0:
                dve.wait_ge(s_xt[tt], 16)
            elif tt == 0:
                dve.wait_ge(s_xl, at(b, 16, 16 * n))
                dve.wait_ge(s_xh, at(b, 4, 4 * n))
            nc.vector.bn_stats(lnw[:, tt, :], XH[:, tt, :]).then_inc(s_st, 1)

        def dve_aggregate(dve, b, n):
            wait_apart(dve, [s_st], at(b, 4, 4 * n + 4))
            for tt in range(QB):
                nc.vector.bn_aggr(lnm[:, tt, :], lnw[:, tt, :]).then_inc(s_ag, 1)
            dve.wait_ge(s_ag, at(b, 4, 4 * n + 4))
            nc.vector.tensor_scalar(veps[:, :], lnm[:, :, 1], EPS, None, ALU.add).then_inc(s_eps, 1)

        def dve_xhat(dve, b, n, tt):
            dve.wait_ge(s_rstd, at(b, 1, n + 1))
            nc.vector.tensor_scalar(XH[:, tt, :], XH[:, tt, :], lnm[:, tt, 0:1], rstd[:, tt:tt + 1], ALU.subtract,
                                    ALU.mult).then_inc(s_xh, 1)

        def dve_slot(dve, b, o, k, last=False):
            first = isinstance(b, int) and 4 * b + o <= 0
            final = last and o == 3
            if o < 0:
                for kind, arg, fill, oo in ended(o, k, last):
                    dve_aux(dve, b, kind, arg, fill, oo)
            if not final:
                dve_max(dve, b, o + 1, k)
            if k % 6 == 5 and not final:
                dve_neg_max(dve, b, 2 * (o + 1) + k // 6)
            if k == 5 and not first:
                dve_out(dve, b, 2 * o - 1)
            if k == 11 and o >= 0:
                dve_out(dve, b, 2 * o)
            if o >= 0:
                for kind, arg, fill, oo in ended(o, k, last):
                    dve_aux(dve, b, kind, arg, fill, oo)
            if final and k in FINAL:
                for step in [s for s in FINAL[k - 1] if s[0] == "W"] if k > 2 else []:
                    dve_step(dve, step)
                for step in [s for s in FINAL[k] if s[0] == "T"]:
                    dve_step(dve, step)
            if final and k in (0, 9):
                dve_gate(dve, k // 9)
            if o == 1 and not last:
                if k < 3:
                    for tt in ([0], [1], [2, 3])[k]:
                        dve_stats(dve, b, 1, tt)
                if k == 3:
                    dve_aggregate(dve, b, 1)
                if 4 <= k < 4 + QB:
                    dve_xhat(dve, b, 1, k - 4)

        def pool_mask(pool, b, o, k):
            gi, jj = k // 6, (k // 3) % 2
            wait_apart(pool, s_ex, at(b, 48, 12 * o + k + 1))
            for i in range(QB):
                part = PR[:, gi, jj::2, BLK_OFF[i]:BLK_OFF[i] + 128]
                last = nc.gpsimd.affine_select(out=part, in_=part, compare_op=ALU.is_ge, fill=0.0, base=0,
                                               pattern=[[0, 2], [1, 128]], channel_multiplier=-1)
            last.then_inc(s_mask, 1)

        def pool_rstd(pool, b, n):
            pool.wait_ge(s_eps, at(b, 1, n + 1))
            nc.gpsimd.tensor_tensor(rstd[:, :], veps[:, :], neg_half[:, :], ALU.pow).then_inc(s_rstd, 1)

        def pool_aux(pool, b, kind, arg, fill, oo):
            if kind == "x":
                pool.wait_ge(s_hh, at(b, 4, 4 * (oo // 4 + 1) + arg + 1))
                nc.gpsimd.tensor_tensor(HT[1][:, arg, :], HF[:, arg % 2, :], HT[0][:, arg, :].bitcast(F32), ALU.subtract)\
                    .then_inc(s_hl, 1)

        def pool_slot(pool, b, o, k, last=False):
            final = last and o == 3
            if last and o == 2 and k == 0:
                pool_losel(pool)
            for kind, arg, fill, oo in ended(o, k, last):
                pool_aux(pool, b, kind, arg, fill, oo)
                if kind in "qk" and oo < 0:
                    sp_heads(pool, b, kind, oo + 2, fill, "gpsimd")
            if k % 3 == 2 and o >= 0:
                pool_mask(pool, b, o, k)
            if final and k in FINAL and k < 10:
                for step in FINAL[k]:
                    pool_step(pool, step)
            if final and k == 8:
                pool_residual(pool, 0, 0)
            if final and k == 10:
                pool_step(pool, ("W", 0, 0))
            if o == 1 and k == 3 and not last:
                pool_rstd(pool, b, 1)
            part = SLOTS * (o - 2) + k - 5
            if last and 0 <= part < 8:
                w, kt = part // 4, part % 4
                pool.wait_ge(s_lh, part + 1)
                nc.gpsimd.tensor_tensor((WO, WB)[w][1][:, kt, :], raw_late[:, w, kt, :],
                                        (WO, WB)[w][0][:, kt, :].bitcast(F32), ALU.subtract).then_inc(s_ll, 1)

        def wait_rows(eng, b, o, kinds="qk"):
            f, bb = o % 4, o // 4
            for kind in kinds:
                eng.wait_ge((s_q if kind == "q" else s_k)[f], at(b, 96, 96 * (bb + 1) - (32 if f < 2 else 0)))
                if f < 2 and bb == 0 and not (isinstance(b, int) and b):
                    eng.wait_ge((s_qg if kind == "q" else s_kg)[f], 32)

        def sp_heads(sp, b, kind, o, fill, share="all"):
            E, S, s_rows, parts = (QE, QS, s_q, (0, 1, 0)) if kind == "q" else (KE, KS, s_k, (0, 0, 1))
            f = o % 4
            if share == "gpsimd":
                s_rows = s_qg if kind == "q" else s_kg
            sp.wait_ge(s_pjf[fill % 2], at(b, 10, fill // 2 + 1))
            for r, part in enumerate(parts):
                for h in range(2):
                    if share != "all" and (share == "gpsimd") != (h == 1 and r < 2):
                        continue
                    sp.dma_start(S[64 * h + 16 * r:64 * h + 16 * r + 16, f, :, :].rearrange("p j t -> p (j t)")
                                 .bitcast(F32), E[64 * h:64 * h + 64, part, :].bitcast(F32)).then_inc(s_rows[f], 16)

        def sp_max_rows(sp, b, e):
            f, gi = (e // 2) % 4, e % 2
            sp.wait_ge(s_mtd, at(b, 8, e + 1))
            for h in range(2):
                sp.dma_start(QS[64 * h + SHIFT_ROWS:64 * h + SHIFT_ROWS + 2, f, 2 * gi:2 * gi + 2, :]
                             .rearrange("p j t -> p (j t)").bitcast(F32), MT[4 * h:4 * h + 4, :].bitcast(F32)).then_inc(s_mrow[gi], 16)

        def sp_store_ao(sp, b, o):
            f, bb = o % 4, b + o // 4
            sp.wait_ge(s_od, at(b, 8, 2 * o + 3))
            rows_ = ao_dram[bass.ds(bb * L, L), :] if not isinstance(bb, int) else ao_dram[bb * L:(bb + 1) * L, :]
            sp.dma_start(rows_.rearrange("(q p) c -> p q c", p=128)[:, :, f * 128:(f + 1) * 128],
                         AO[:, f % 2, :, :]).then_inc(s_ao[f % 2], 16)

        def sp_load_x(sp, b, n):
            bb = b + n
            rows_ = x[bb, :, :] if isinstance(bb, int) else x[bass.ds(bb, 1), :, :].rearrange("a t c -> (a t) c")
            sp.dma_start(XH[:, :, :], rows_.rearrange("(q p) c -> p q c", p=128)).then_inc(s_xl, 16)

        def sp_slot(sp, b, o, k, last=False):
            final = last and o == 3
            first = isinstance(b, int) and 4 * b + o <= 0
            if k == 1 and o >= 0:
                sp_max_rows(sp, b, 2 * o + 1)
            if k == 7 and not final:
                sp_max_rows(sp, b, 2 * o + 2)
            for kind, arg, fill, oo in ended(o, k, last):
                if kind in "qk":
                    sp_heads(sp, b, kind, oo + 2, fill, "sync" if oo < 0 else "all")
            if k == 5 and not first:
                sp_store_ao(sp, b, o - 1)
            if (o, k) == (0, 7) and not last:
                sp.wait_ge(s_pj, at(b, FILLS_B, FILLS_0 - 6))
                sp_load_x(sp, b, 1)
            if last and o == 0 and 0 <= k - 8 < E_ACT:
                sp_gather_expert(sp, k - 8)
            if last and o == 1 and k >= 8:
                kt = k - 8
                sp.wait_ge(s_pj, fill_base(1, True) + 2 + FILLS_B * b)
                sp.dma_start(wm_late[:, kt, :], wmod[kt * 128:(kt + 1) * 128, 2 * D:4 * D]).then_inc(s_wml[kt], 16)
            if last and o == 2 and k in (0, 1, 3, 4):
                part = (0, 1, None, 2, 3)[k]
                w, kt = part // 2, 2 * (part % 2)
                sp.dma_start(raw_late[:, w, kt:kt + 2, :], (WoT, WbT)[w].rearrange("(t p) c -> p t c", p=128)[:, kt:kt + 2, :])\
                    .then_inc(s_rawl[part], 16)
            if last and o == 2 and k == 3:
                for h in range(2):
                    sp.wait_ge(s_st_[h], 12 * (NU - 2))
                sp_load_attention(sp, 0)
                sp_load_attention(sp, 1)
            if last and (o, k) in ((2, 9), (2, 10), (2, 11), (3, 0)):
                kt = (k - 9) % SLOTS
                sp.wait_ge(s_pj, fill_base(3, True) + FILLS_B * b)
                sp.dma_start(wm_late[:, kt, :], wmod[kt * 128:(kt + 1) * 128, 4 * D:6 * D]).then_inc(s_wml[kt], 16)
            if final and k == 1:
                sp_store_gate(sp, 0)
                sp_load_gate(sp, 0, 0)
                sp_load_gate(sp, 0, 1)
                for h in range(2):
                    sp.wait_ge(s_st_[h], 12 * (NU - 1))
                for tt in range(QB):
                    sp_load_residual(sp, 0, tt)
            if final and k == 3:
                sp_load_lora(sp)
            if final and k == 8:
                sp.wait_ge(s_tb, tile_of("T", 0, KT - 1) + 1)
                sp_load_attention(sp, 2)
            if final and k == 10:
                sp_store_gate(sp, 1)
                sp_load_gate(sp, 1, 0)
                sp_load_gate(sp, 1, 1)

        def phase_a(eng, slot):
            for n in range(-SLOTS, 6):
                slot(eng, 0, n // SLOTS, n % SLOTS)
            with eng.Fori(0, B - 1) as b:
                for n in range(6, 4 * SLOTS + 6):
                    slot(eng, b, n // SLOTS, n % SLOTS)
            for n in range(6, 4 * SLOTS):
                slot(eng, B - 1, n // SLOTS, n % SLOTS, last=True)

        SLICES = [(WQ, 0, 128), (WK, 0, 128), (WQ, 128, D), (WK, 128, D), (WV, 0, D)]
        raw_of = {id(W): r for W, r in zip((WQ, WK, WV), raw_w)}
        XB = [*MX, *ST]

        FINAL = {2 + n * KT + kt: [("T", n, kt)] for n in range(2) for kt in range(KT)}
        FINAL |= {10: [("W", 0, 0)], 11: [("W", 0, 1)]}
        STEPS = [("W", 0, 3), ("M", 0), ("W", 1, 0), ("W", 1, 1)] + [("X", 0, kt) for kt in range(KT)]
        STEPS += [("L", 0), ("W", 1, 2)]
        for n in range(B):
            w = [[("W", n + 1, tt)] for tt in range(QB)] if n else [[], [("W", 1, 3)], [], []]
            if n == B - 1:
                STEPS += [("ZT", n), ("F", n, 0), ("ZN", n), ("F", n, 1), ("ZS", n), ("F", n, 2), ("FL", n, 0),
                          ("FL", n, 1), ("FL", n, 2), ("F", n, 3), ("FL", n, 3)]
                continue
            tiles = [("T", n + 2, kt) for kt in range(KT)] if n + 2 < B else []
            tiles += [("X", n + 1, kt) for kt in range(KT)]
            cuts = (0, 2, 3, 5, 7, 8) if n == 0 else (0, 2, 2, 4, 6, 8) if n + 2 < B else (0, 0, 0, 2, 4, 4)
            t = [tiles[a:c] for a, c in zip(cuts, cuts[1:])]
            if n == 0:
                STEPS += w[1] + [("ZT", n)] + t[0] + [("ZN", n), ("F", n, 0), ("F", n, 1), ("ZS", n)] + t[1]
            else:
                STEPS += w[0] + w[1] + [("ZT", n)] + w[2] + [("ZN", n)] + w[3]
                STEPS += [("F", n, 0)] + t[0] + [("ZS", n), ("F", n, 1)]
            STEPS += [("FL", n, 0), ("FL", n, 1)] + t[2]
            STEPS += [("F", n, 2), ("FL", n, 2)] + t[3] + [("F", n, 3), ("FL", n, 3)] + t[4]
        TILES = [s for s in [*sum(FINAL.values(), []), *STEPS] if s[0] in "TX"]
        TB, YW, ZB, ZN = bank[0:2], bank[6:8], bank[2], bank[3]
        YF = [bank[4 + i % 2] for i in range(B * QB - 2)] + YW

        def tiles_first(steps):
            steps = [s for s in steps if s != ("W", 1, 1)]
            steps.insert(steps.index(("X", 0, 1)) + 1, ("W", 1, 1))
            return steps

        def tile_of(kind, n, kt):
            return TILES.index((kind, n, kt))

        def pe_tile(pe, kind, n, kt):
            src = AON[:, n % 2, :, :] if kind == "T" else XH2
            if (kind, n, kt) == ("T", 0, 0):
                for h in range(2):
                    pe.wait_ge(s_mxf[h], 12 * NU)
            if kind == "T":
                pe.wait_ge(s_ald[n % 2], 16 * (n // 2 + 1))
            else:
                pe.wait_ge(s_xh2, QB * (n + 1))
            i = tile_of(kind, n, kt)
            pe.wait_ge(s_bf[i % 2], i // 2)
            for tt in range(QB):
                mm = nc.tensor.transpose(TB[i % 2][:, tt * 128:(tt + 1) * 128], src[:, tt, kt * 128:(kt + 1) * 128],
                                         ident[:, :])
            mm.then_inc(s_tb, 1)

        def pe_products(pe, dst, act_parts, w_parts, tt, wait, stop):
            for kt in range(KT):
                if wait:
                    wait(kt)
                for n, (hi, wi) in enumerate([(0, 0), (0, 1), (1, 0)]):
                    mm = nc.tensor.matmul(dst[:, :], act_parts[hi][:, kt, tt * 128:(tt + 1) * 128], w_parts[wi][:, kt, :],
                                          start=(kt == 0 and n == 0), stop=(stop and kt == KT - 1 and n == 2))
            return mm

        def pe_phase_b(pe):
            for step in STEPS[1:]:
                pe_step(pe, step)

        def pe_step(pe, step):
            kind, n = step[0], step[1]
            if kind == "M":
                for h in range(2):
                    pe.wait_ge(s_ex[h], 12 * NU)
                for c in range(2):
                    mm = nc.tensor.transpose(ZN[:, c * 128:(c + 1) * 128], MOD[:, 1 + c, :], ident[:, :])
                mm.then_inc(s_z2, 1)
            if kind in "TX":
                pe_tile(pe, kind, n, step[2])
            if kind == "W":
                tt = step[2]
                i = QB * n + tt
                if i < 2:
                    pe.wait_ge(s_pjf[i], ALL_FILLS // 2)
                    pe.wait_ge(s_ll, 8)
                else:
                    pe.wait_ge(s_t1, i - 1)
                pe_products(pe, YW[i % 2], AT[n % 2], WO, tt, lambda kt: pe.wait_ge(s_bl, tile_of("T", n, kt) + 1), True)\
                    .then_inc(s_w, 1)
            if kind == "ZT":
                if n == 0:
                    pe.wait_ge(s_lset, 2)
                pe.wait_ge(s_zst, n)
                for kt in range(KT):
                    pe.wait_ge(s_bl, tile_of("X", n, kt) + 1)
                    for hi in range(2):
                        mm = nc.tensor.matmul(ZB[:, :], ART[:, kt, :], H2[n % 2][hi][:, kt, :],
                                              start=(kt == 0 and hi == 0), stop=(kt == KT - 1 and hi == 1))
                mm.then_inc(s_zt, 1)
            if kind == "F":
                i = QB * n + step[2]
                if i == 0:
                    pe.wait_ge(s_oe, 2 * NU)
                    pe.wait_ge(s_od, 2 * NU + 1)
                if i < B * QB - 2:
                    pe.wait_ge(s_t2, i - 1 if i > 1 else 0)
                else:
                    pe.wait_ge(s_t1, B * QB)
                pe_products(pe, YF[i], H2[n % 2], WB, step[2], None, False)
            if kind == "FL":
                i = QB * n + step[2]
                if i == 0:
                    pe.wait_ge(s_btd, 1)
                pe.wait_ge(s_zst, n + 1)
                nc.tensor.matmul(YF[i][:, :], ZST[:, step[2] * 128:(step[2] + 1) * 128], BT[:, :], start=False,
                                 stop=True).then_inc(s_f, 1)
            if kind == "ZN":
                pe.wait_ge(s_ztd, n + 1)
                pe.wait_ge(s_zs, n)
                pe.wait_ge(s_z2, 2)
                for tt in range(QB):
                    mm = nc.tensor.matmul(ZN[:, tt * 36:(tt + 1) * 36], ZTs[:, tt * 128:(tt + 1) * 128], fold[:, 0:36],
                                          start=True, stop=True)
                mm.then_inc(s_zn, 1)
            if kind == "ZS":
                pe.wait_ge(s_zs, n + 1)
                for tt in range(QB):
                    mm = nc.tensor.transpose(ZB[0:98, tt * 128:(tt + 1) * 128], ZS[:, tt, :].bitcast(F32), ident[:, :])
                mm.then_inc(s_zsp, 1)

        def act_tile(act, kind, n, kt):
            i = tile_of(kind, n, kt)
            act.wait_ge(s_tb, i + 1)
            act.wait_ge(s_bl, i - 1 if i > 1 else 0)
            if kind == "T":
                op = nc.scalar.activation(HF2[:, i % 2, :], TB[i % 2][:, :], ACT.Identity, bias=bcol[:, 2, kt:kt + 1])
            else:
                op = nc.scalar.activation(HF2[:, i % 2, :], TB[i % 2][:, :], ACT.Identity,
                                          scale=modT[:, 3, kt, n:n + 1], bias=modT[:, 2, kt, n:n + 1])
            op.then_inc(s_bf[i % 2], 1)

        def act_phase_b(act):
            for step in STEPS[1:]:
                act_step(act, step)

        def act_step(act, step):
            kind, n = step[0], step[1]
            if kind in "TX":
                if step == ("X", 0, 0):
                    act.wait_ge(s_z2, 3)
                act_tile(act, kind, n, step[2])
            if kind == "ZT":
                act.wait_ge(s_zt, n + 1)
                act.wait_ge(s_zn, n)
                nc.scalar.activation(ZTs[:, :], ZB[:, :], ACT.Copy).then_inc(s_ztd, 1)
            if kind == "ZN":
                act.wait_ge(s_lg, n + 1)
                nc.scalar.activation(AL[:, 2, :, :], AL[:, 1, :, :], ACT.Exp).then_inc(s_ex2, 1)
            if kind == "ZS":
                act.wait_ge(s_zsp, n + 1)
                act.wait_ge(s_f, QB * n)
                nc.scalar.activation(ZST[:, :], ZB[0:98, :], ACT.Copy).then_inc(s_zst, 1)

        def dve_tile(dve, kind, n, kt):
            i = tile_of(kind, n, kt)
            dve.wait_ge(s_bf[i % 2], i // 2 + 1)
            nc.vector.tensor_copy((AT if kind == "T" else H2)[n % 2][0][:, kt, :], HF2[:, i % 2, :]).then_inc(s_bh, 1)

        def dve_gate(dve, g):
            row = (0, 3)[g]
            if g:
                dve.wait_ge(s_gate, 4)
            dve.wait_ge(s_pjf[row % 2], ALL_FILLS // 2 - (0 if g else 1))
            nc.vector.tensor_scalar(G1[:, 0, :], MOD[:, row, :], 0.0, 2.0, ALU.is_ge, ALU.mult).then_inc(s_gate, 1)
            nc.vector.scalar_tensor_tensor(G1[:, 1, :], MOD[:, row, :], -1.0, MOD[:, row, :], ALU.mult, ALU.max)\
                .then_inc(s_gate, 1)
            dve.wait_ge(s_gate, 4 * g + 2)
            nc.vector.tensor_scalar(G1[:, 0, :], G1[:, 0, :], 1.0, None, ALU.subtract).then_inc(s_gate, 1)
            dve.wait_ge(s_gate, 4 * g + 3)
            nc.vector.scalar_tensor_tensor(MOD[:, row, :], G1[:, 1, :], 0.25, G1[:, 0, :], ALU.max, ALU.mult)\
                .then_inc(s_gate, 1)

        chain = [0]

        def dve_phase_b(dve):
            for step in tiles_first(STEPS)[1:]:
                dve_step(dve, step)

        def dve_step(dve, step):
            def link(ins):
                chain[0] += 1
                ins.then_inc(s_ch, 1)
                dve.wait_ge(s_ch, chain[0])

            kind, n = step[0], step[1]
            def ln_stats(i):
                dve.wait_ge(s_x1, i + 1)
                nc.vector.bn_stats(lnw[:, i % QB, :], X1[:, i // QB % 2, i % QB, :]).then_inc(s_st2, 1)

            def ln_aggregate(i):
                dve.wait_ge(s_st2, i + 1)
                nc.vector.bn_aggr(lnm[:, i % QB, :], lnw[:, i % QB, :]).then_inc(s_ag2, 1)

            def ln_eps(i):
                t = i % QB
                dve.wait_ge(s_ag2, i + 1)
                nc.vector.tensor_scalar(veps[:, t:t + 1], lnm[:, t, 1:2], EPS, None, ALU.add).then_inc(s_ep2, 1)

            def ln_normalise(i):
                n, t = i // QB, i % QB
                dve.wait_ge(s_rs2, i + 1)
                if i == 0:
                    for h in range(2):
                        dve.wait_ge(s_st_[h], 12 * NU)
                if t == 0 and n:
                    dve.wait_ge(s_tb, tile_of("X", n - 1, KT - 1) + 1)
                nc.vector.tensor_scalar(XH2[:, t, :], X1[:, n % 2, t, :], lnm[:, t, 0:1], rstd[:, t:t + 1],
                                        ALU.subtract, ALU.mult).then_inc(s_xh2, 1)

            if kind == "M":
                dve.wait_ge(s_z2, 1)
                for c in range(2):
                    nc.vector.tensor_scalar(modT[:, 2 + c, :, :], ZN[:, c * 128:(c + 1) * 128].rearrange(
                        "p (t w) -> p t w", w=32)[:, :, 0:B], float(c), None, ALU.add).then_inc(s_z2, 1)
            if kind == "L":
                dve.wait_ge(s_pv, 2 * NU + 1)
                nc.vector.memset(ZS[:, :, 96:98].bitcast(F32), 1.0)
                nc.vector.memset(ART[:, :, :].bitcast(F32), 0.0)
                link(nc.vector.memset(fold[:, :], 0.0))
                for r in range(2):
                    nc.vector.tensor_copy(fold[64 * r:64 * r + 36, 0:36], ident[64 * r:64 * r + 36, 64 * r:64 * r + 36])
                dve.wait_ge(s_lw, 7 * 16)
                nc.vector.tensor_scalar(RPB[:, :, 1], RPB[:, :, 1], 1e-12, None, ALU.add)
                link(nc.vector.tensor_copy(BT[:, :], BR[:, :]))
                nc.vector.tensor_copy(ART[:, :, 0:36], ARW[:, :, :]).then_inc(s_lset, 1)
                dve.wait_ge(s_pc, 4)
                nc.vector.scalar_tensor_tensor(BT[:, :], BT[:, :].bitcast(F32), losel[0:98, :], BR[:, :], ALU.mult,
                                               ALU.add).then_inc(s_btd, 1)
                dve.wait_ge(s_lset, 1)
                nc.vector.tensor_tensor(ART[:, :, 64:100], ARW[:, :, :], ART[:, :, 0:36].bitcast(F32),
                                        ALU.subtract).then_inc(s_lset, 1)
            if kind in "TX":
                dve_tile(dve, kind, n, step[2])
            if kind == "W":
                tt = step[2]
                i = QB * n + tt
                if tt == 0:
                    dve.wait_ge(s_ga[n % 2], 16 * (n // 2 + 1))
                dve.wait_ge(s_w, i + 1)
                nc.vector.tensor_tensor(T1[:, i % 2, :], YW[i % 2][:, :], GT[:, n % 2, 0, :], ALU.mult)\
                    .then_inc(s_t1, 1)
                if tt:
                    ln_stats(i - 1)
                dve.wait_ge(s_t1, i + 1)
                dve.wait_ge(s_xb, i + 1)
                nc.vector.tensor_tensor(X1[:, n % 2, tt, :], T1[:, i % 2, :], X1[:, n % 2, tt, :], ALU.add)\
                    .then_inc(s_x1, 1)
                if tt:
                    ln_aggregate(i - 1)
                if tt == QB - 1:
                    ln_stats(i)
                if tt:
                    ln_eps(i - 1)
                if tt == QB - 1:
                    ln_aggregate(i)
                    ln_eps(i)
                if tt > 1:
                    ln_normalise(i - 2)
                if tt == QB - 1:
                    ln_normalise(i - 1)
                    ln_normalise(i)
            if kind == "ZN":
                zn = ZN[:, 0:QB * 36].rearrange("p (t e z) -> p t e z", e=E_ACT, z=EZ)

                def over_tiles(ap):
                    return ap.unsqueeze(1).to_broadcast([128, QB, E_ACT])

                def over_experts(ap):
                    return ap.unsqueeze(2).to_broadcast([128, QB, E_ACT])

                dve.wait_ge(s_zn, n + 1)
                link(nc.vector.tensor_tensor(AL[:, 0, :, :], zn[:, :, :, RANK], over_tiles(RPB[:, :, 0]), ALU.add))
                link(nc.vector.reduce_max(AR1[:, 0, :], AL[:, 0, :, :], AX_X))
                nc.vector.tensor_tensor(AL[:, 1, :, :], AL[:, 0, :, :], over_experts(AR1[:, 0, :]), ALU.subtract)\
                    .then_inc(s_lg, 1)
                dve.wait_ge(s_ex2, n + 1)
                link(nc.vector.tensor_tensor(AL[:, 0, :, :], AL[:, 2, :, :], over_tiles(RPB[:, :, 1]), ALU.mult))
                link(nc.vector.reduce_sum(AR1[:, 1, :], AL[:, 0, :, :], AX_X))
                link(nc.vector.reciprocal(AR1[:, 2, :], AR1[:, 1, :]))
                link(nc.vector.scalar_tensor_tensor(AL[:, 3, :, :], AL[:, 0, :, :], 2.0, over_experts(AR1[:, 2, :]),
                                                    ALU.mult, ALU.mult))
                if n:
                    dve.wait_ge(s_zsp, n)
                link(nc.vector.tensor_tensor(
                    ZF[:, :, :].rearrange("p t (e r) -> p t e r", r=RANK),
                    zn[:, :, :, 0:RANK],
                    AL[:, 3, :, :].unsqueeze(3).to_broadcast([128, QB, E_ACT, RANK]), ALU.mult))
                link(nc.vector.tensor_copy(ZS[:, :, 0:ZR], ZF[:, :, :]))
                nc.vector.tensor_copy(ZS[:, :, ZR:2 * ZR], ZF[:, :, :])
                nc.vector.tensor_tensor(ZS[:, :, 2 * ZR:3 * ZR], ZF[:, :, :], ZS[:, :, 0:ZR].bitcast(F32),
                                        ALU.subtract).then_inc(s_zs, 1)
            if kind == "FL":
                tt = step[2]
                i = QB * n + tt
                if tt == 0:
                    dve.wait_ge(s_gb[n % 2], 16 * (n // 2 + 1))
                dve.wait_ge(s_f, i + 1)
                dve.wait_ge(s_out[i % 2], 16 * (i // 2))
                nc.vector.tensor_tensor(T2[:, i % 2, :], YF[i][:, :], GT[:, n % 2, 1, :], ALU.mult)\
                    .then_inc(s_t2, 1)
                dve.wait_ge(s_t2, i + 1)
                nc.vector.tensor_tensor(T2[:, i % 2, :], T2[:, i % 2, :], X1[:, n % 2, tt, :], ALU.add)\
                    .then_inc(s_y, 1)

        def pool_tile(pool, kind, n, kt):
            dst = (AT if kind == "T" else H2)[n % 2]
            i = tile_of(kind, n, kt)
            pool.wait_ge(s_bh, i + 1)
            nc.gpsimd.tensor_tensor(dst[1][:, kt, :], HF2[:, i % 2, :], dst[0][:, kt, :].bitcast(F32), ALU.subtract)\
                .then_inc(s_bl, 1)

        def pool_phase_b(pool):
            for step in tiles_first(STEPS)[1:]:
                pool_step(pool, step)

        def pool_step(pool, step):
            kind, n = step[0], step[1]
            if kind in "TX":
                pool_tile(pool, kind, n, step[2])
            if step == ("W", 0, QB - 1):
                pool_residual(pool, 1, 0)
            if kind == "FL" and step[2] == 2 and n + 2 < B:
                pool_residual(pool, n + 2, 0)
            if kind == "W":
                if step[2] + 1 < QB:
                    pool_residual(pool, n, step[2] + 1)
                for t in [step[2] - 1] * (step[2] > 0) + [QB - 1] * (step[2] == QB - 1):
                    pool.wait_ge(s_ep2, QB * n + t + 1)
                    nc.gpsimd.tensor_tensor(rstd[:, t:t + 1], veps[:, t:t + 1], neg_half[:, t:t + 1], ALU.pow)\
                        .then_inc(s_rs2, 1)

        def pool_losel(pool):
            pool.wait_ge(s_pj, FILLS_0 + FILLS_B * (B - 1))
            nc.gpsimd.memset(losel[:, :], -1.0).then_inc(s_pc, 1)
            for n, (op, fill, base, mult) in enumerate([(ALU.is_ge, 0.0, -ZR, 1), (ALU.is_ge, 0.0, 2 * ZR - 1, -1),
                                                        (ALU.not_equal, -1.0, -3 * ZR - 1, 1)]):
                pool.wait_ge(s_pc, n + 1)
                nc.gpsimd.affine_select(out=losel[:, :], in_=losel[:, :], compare_op=op, fill=fill, base=base,
                                        pattern=[[0, 1]], channel_multiplier=mult).then_inc(s_pc, 1)

        def pool_residual(pool, n, tt):
            if tt == 0:
                if n == 0:
                    pool.wait_ge(s_bol, 16)
                pool.wait_ge(s_xb, QB * n)
                pool.wait_ge(s_ga[n % 2], 16 * (n // 2 + 1))
                nc.gpsimd.tensor_tensor(GBO[:, :], BO[:, :], GT[:, n % 2, 0, :], ALU.mult).then_inc(s_gbo, 1)
            pool.wait_ge(s_gbo, n + 1)
            pool.wait_ge(s_x1l[n % 2][tt], 16 * (n // 2 + 1))
            nc.gpsimd.tensor_tensor(X1[:, n % 2, tt, :], X1[:, n % 2, tt, :], GBO[:, :], ALU.add).then_inc(s_xb, 1)

        def sp_gather_expert(sp, e):
            sp.wait_ge(s_ix, 3)
            ex = sp.value_load(idx[0:1, 0, e:e + 1], min_val=0, max_val=E_TOT - 1)
            sp.dma_start(ar_dram[:, e * EZ:(e + 1) * EZ],
                         loraAT[:, bass.ds(ex, 1), :].rearrange("c a r -> c (a r)")).then_inc(s_gath, 16)
            sp.dma_start(br_dram[e * RANK:(e + 1) * RANK, :],
                         loraBT[bass.ds(ex, 1), :, :].rearrange("a r c -> (a r) c")).then_inc(s_gath, 16)
            sp.dma_start(rp_dram[:, 2 * e:2 * e + 2], bias_prior[bass.ds(ex, 1), :]).then_inc(s_gath, 16)

        def sp_load_attention(sp, n):
            for par in range(2):
                sp.wait_ge(s_ao[par], 16 * 2 * (n + 1))
            sp.dma_start(AON[:, n % 2, :, :], ao_dram[n * L:(n + 1) * L, :].rearrange("(q p) c -> p q c", p=128))\
                .then_inc(s_ald[n % 2], 16)

        def sp_load_residual(sp, n, tt):
            rows_ = (n * QB + tt) * 128
            sp.dma_start(X1[:, n % 2, tt, :], x_rows[rows_:rows_ + 128, :]).then_inc(s_x1l[n % 2][tt], 16)

        def sp_store_gate(sp, g):
            sp.wait_ge(s_gate, 4 * g + 4)
            sp.dma_start(gate_dram[g, :, :, :].rearrange("c b j -> (c b) j"), MOD[:, (0, 3)[g], :]).then_inc(s_gst, 16)
            sp.wait_ge(s_gst, 16 * (g + 1))

        def sp_load_gate(sp, g, n):
            sp.dma_start(GT[:, n % 2, g, :].rearrange("p (c j) -> p c j", j=128),
                         gate_dram[g, :, n, :].unsqueeze(0).to_broadcast([128, D // 128, 128]))\
                .then_inc((s_ga, s_gb)[g][n % 2], 16)

        def sp_load_lora(sp):
            sp.wait_ge(s_pj, FILLS_0 + FILLS_B * (B - 1))
            sp.wait_ge(s_gath, 16 * 3 * E_ACT)
            sp.dma_start(BO[:, :], bo.to_broadcast([128, D])).then_inc(s_bol, 16)
            sp.dma_start(ARW[:, :, :], ar_dram.rearrange("(t p) c -> p t c", p=128)).then_inc(s_lw, 16)
            for r in range(3):
                sp.dma_start(BR[r * ZR:(r + 1) * ZR, :], br_dram).then_inc(s_lw, 16)
            for r in range(2):
                sp.dma_start(BR[3 * ZR + r:3 * ZR + r + 1, :], b_base).then_inc(s_lw, 16)
            sp.dma_start(RPB[:, :, :].rearrange("p e a -> p (e a)"), rp_dram.to_broadcast([128, 2 * E_ACT])).then_inc(s_lw, 16)

        def sp_phase_b(sp):
            sp.wait_ge(s_tb, tile_of("T", 1, KT - 1) + 1)
            sp_load_attention(sp, 3)
            for step in STEPS:
                kind, n = step[0], step[1]
                if kind == "W" and step[2] == QB - 1 and n + 2 < B:
                    sp.wait_ge(s_t1, QB * (n + 1))
                    sp_load_gate(sp, 0, n + 2)
                if kind == "FL":
                    tt = step[2]
                    i = QB * n + tt
                    sp.wait_ge(s_y, i + 1)
                    sp.dma_start(out[i * 128:(i + 1) * 128, :], T2[:, i % 2, :]).then_inc(s_out[i % 2], 16)
                    if n + 2 < B:
                        sp_load_residual(sp, n + 2, tt)
                        if tt == QB - 1:
                            sp_load_gate(sp, 1, n + 2)
            for par in range(2):
                sp.wait_ge(s_out[par], 16 * B * QB // 2)

        @block.tensor
        def _(pe):
            pe.sem_inc(s_pv, 1)
            pe.wait_ge(s_id, 2)

            def pe_first_x(kt):
                for tt in range(QB):
                    mm = nc.tensor.transpose(XB[kt][:, tt * 128:(tt + 1) * 128], XH[:, tt, kt * 128:(kt + 1) * 128],
                                             ident[:, :])
                mm.then_inc(s_x0, 1)

            pe.wait_ge(s_sc, 1)
            pe.wait_ge(s_od, 1)
            for kt in range(KT):
                if kt == KT - 1:
                    pe.wait_ge(s_xh, QB)
                    pe_first_x(0)
                pe.wait_ge(s_wm[kt], 16)
                for c in range(4):
                    mm = nc.tensor.matmul(PO[32 * c:32 * c + B, 0:256], silu_c[:, 3, kt, :],
                                          wm_first[:, kt, 256 * c:256 * c + 256], start=(kt == 0), stop=(kt == KT - 1))
            mm.then_inc(s_pt0, 1)
            pe_first_x(1)
            pe.wait_ge(s_pt0, 2)
            for n in range(2):
                mm = nc.tensor.transpose(PT[:, n * 128:(n + 1) * 128], OE[:, n * 128:(n + 1) * 128], ident[:, :])
            mm.then_inc(s_pt0, 1)
            pe_first_x(2)
            pe_first_x(3)
            for fill, (kind, kt) in enumerate([("q", 0), ("k", 0)]):
                pe.wait_ge(s_wlo, fill + 1)
                for n in range(COST[kind][0]):
                    if kind == "q" and n % 3 == 0:
                        pe.wait_ge(s_hl, n // 3 + 1)
                    pe_aux_products(pe, 0, kind, 0, fill, [n])
            pe.wait_ge(s_init, 1)
            pe.wait_ge(s_ones, 32)
            phase_a(pe, pe_slot)
            last_group = 2 * NU - 1
            pe_step(pe, ("W", 0, 2))
            pe_pv(pe, B - 1, last_group - 8 * (B - 1), range(QB))
            pe_step(pe, ("W", 0, 3))
            pe_out_transpose(pe, B - 1, last_group - 8 * (B - 1))
            pe_phase_b(pe)

        @block.scalar
        def _(act):
            act.wait_ge(s_c, 16)
            nc.scalar.activation(silu_c[:, 1, :, :], silu_c[:, 0, :, :], ACT.Exp, scale=-1.0).then_inc(s_e, 1)
            def act_part(n):
                W, lo, hi = SLICES[n]
                act.wait_ge(s_raw[n], 16)
                nc.scalar.activation(W[0][:, :, lo:hi], raw_of[id(W)][:, :, lo:hi], ACT.Copy).then_inc(s_whi, 1)

            act_part(0)
            act_part(1)
            act.wait_ge(s_pt0, 1)
            nc.scalar.activation(OE[:, 0:256], PO[:, 0:256], ACT.Copy).then_inc(s_pt0, 1)
            act.wait_ge(s_bias, 16)
            act.wait_ge(s_pt0, 5)
            act.wait_ge(s_ones, 32)
            for kt in range(KT):
                act.wait_ge(s_x0, kt + 1)
                act.wait_ge(s_hl, max(kt - 1, 0))
                nc.scalar.activation(HF[:, kt % 2, :], XB[kt][:, :], ACT.Identity, scale=mod_col(1, kt, 0, 0),
                                     bias=mod_col(0, kt, 0, 0)).then_inc(s_hf0, 1)
            for fill, kind in enumerate("qk"):
                act_part(fill + 2)
                act_q(act, 0, kind, 0, fill)
            act_part(4)
            phase_a(act, act_slot)
            for kind, arg, fill, oo in ended(4, 0, True):
                act_aux(act, B - 1, kind, arg, fill, oo)
            act_out(act, B - 1, 2 * NU - 1 - 8 * (B - 1))
            act_phase_b(act)

        @block.vector
        def _(dve):
            dve.wait_ge(s_e, 1)
            nc.vector.tensor_scalar(silu_c[:, 1, :, :], silu_c[:, 1, :, :], 1.0, None, ALU.add).then_inc(s_d1, 1)
            dve.wait_ge(s_d1, 1)
            nc.vector.reciprocal(silu_c[:, 2, :, :], silu_c[:, 1, :, :]).then_inc(s_d1, 1)
            dve.wait_ge(s_d1, 2)
            nc.vector.tensor_tensor(silu_c[:, 3, :, :], silu_c[:, 0, :, :], silu_c[:, 2, :, :], ALU.mult).then_inc(s_sc, 1)
            nc.vector.memset(PO[:, :], 0.0).then_inc(s_od, 1)
            for tt in range(QB):
                dve_stats(dve, 0, 0, tt)
            dve_aggregate(dve, 0, 0)
            for tt in range(QB):
                dve_xhat(dve, 0, 0, tt)
            dve.wait_ge(s_idx, 16)
            nc.vector.tensor_scalar(idx[:, 1, :], idx[:, 0, :], 0, E_TOT, ALU.is_lt, ALU.mult).then_inc(s_ix, 1)
            dve.wait_ge(s_ix, 1)
            nc.vector.tensor_tensor(idx[:, 2, :], idx[:, 0, :], idx[:, 1, :], ALU.add).then_inc(s_ix, 1)
            dve.wait_ge(s_ix, 2)
            nc.vector.tensor_scalar(idx[:, 0, :], idx[:, 2, :], 0, E_TOT - 1, ALU.max, ALU.min).then_inc(s_ix, 1)

            def dve_part(n):
                W, lo, hi = SLICES[n]
                dve.wait_ge(s_whi, n + 1)
                nc.vector.tensor_tensor(W[1][:, :, lo:hi], raw_of[id(W)][:, :, lo:hi], W[0][:, :, lo:hi].bitcast(F32),
                                        ALU.subtract).then_inc(s_wlo, 1)

            dve_part(0)
            dve_part(1)
            dve.wait_ge(s_pt0, 3)
            mod_cols = PT[:, 0:256].rearrange("p (n c w) -> p c n w", n=2, w=32)
            nc.vector.tensor_copy(modT[:, 0, :, :].rearrange("p (c n) b -> p c n b", n=2), mod_cols[:, 0:2, :, 0:B])\
                .then_inc(s_pt0, 1)
            nc.vector.tensor_scalar(modT[:, 1, :, :].rearrange("p (c n) b -> p c n b", n=2), mod_cols[:, 2:4, :, 0:B], 1.0,
                                    None, ALU.add).then_inc(s_pt0, 1)
            dve.wait_ge(s_pt0, 5)
            for kt in range(KT):
                dve.wait_ge(s_hf0, kt + 1)
                nc.vector.tensor_copy(HT[0][:, kt, :], HF[:, kt % 2, :]).then_inc(s_hh, 1)
                if kt == 0:
                    dve.wait_ge(s_hh, 1)
                    nc.vector.tensor_tensor(HT[1][:, 0, :], HF[:, 0, :], HT[0][:, 0, :].bitcast(F32), ALU.subtract)\
                        .then_inc(s_hl, 1)
            dve_part(2)
            for fill, kind in enumerate("qk"):
                dve_aux(dve, 0, kind, 0, fill, -2)
            dve_part(3)
            dve_part(4)
            dve.wait_ge(s_init, 1)
            phase_a(dve, dve_slot)
            dve_step(dve, ("W", 0, 1))
            dve_step(dve, ("W", 0, 2))
            dve_step(dve, ("W", 0, 3))
            dve_out(dve, B - 1, 2 * NU - 1 - 8 * (B - 1))
            dve_phase_b(dve)

        @block.gpsimd
        def _(pool):
            nc.gpsimd.memset(neg_half[:, :], -0.5)
            nc.gpsimd.memset(HF[:, 0, :], 1.0).then_inc(s_one, 1)
            nc.gpsimd.memset(ident[:, :], 0.0).then_inc(s_id, 1)
            pool.wait_ge(s_id, 1)
            nc.gpsimd.affine_select(out=ident[:, :], in_=ident[:, :], compare_op=ALU.not_equal, fill=1.0, base=0,
                                    pattern=[[-1, 128]], channel_multiplier=1).then_inc(s_id, 1)
            pool_rstd(pool, 0, 0)
            nc.gpsimd.memset(tri[:, :], 0.0).then_inc(s_id, 1)
            pool.wait_ge(s_id, 3)
            nc.gpsimd.affine_select(out=tri[:, L - 128:L], in_=tri[:, L - 128:L], compare_op=ALU.is_ge, fill=NEG,
                                    base=0, pattern=[[-1, 128]], channel_multiplier=1)
            nc.gpsimd.memset(V[:, :, :, HD:VW], 1.0).then_inc(s_init, 1)
            pool.wait_ge(s_hl, 1)
            for kt in range(1, KT):
                pool.wait_ge(s_hh, kt + 1)
                nc.gpsimd.tensor_tensor(HT[1][:, kt, :], HF[:, kt % 2, :], HT[0][:, kt, :].bitcast(F32), ALU.subtract)\
                    .then_inc(s_hl, 1)
            for fill, kind in enumerate("qk"):
                sp_heads(pool, 0, kind, 0, fill, "gpsimd")
            phase_a(pool, pool_slot)
            pool_step(pool, ("W", 0, 1))
            pool_step(pool, ("W", 0, 2))
            pool_step(pool, ("W", 0, 3))
            pool_phase_b(pool)

        @block.sync
        def _(sp):
            sp.dma_start(silu_c[:, 0, :, :], cT.rearrange("(t p) b -> p t b", p=128)).then_inc(s_c, 16)
            for tt in range(QB):
                sp.dma_start(XH[:, tt, :], x_rows[tt * 128:(tt + 1) * 128, :]).then_inc(s_xt[tt], 16)
            sp.dma_start(idx[:, 0, :], active).then_inc(s_idx, 16)
            sp.wait_ge(s_one, 1)
            for h in range(2):
                sp.dma_start(KS[64 * h + SHIFT_ROWS:64 * h + SHIFT_ROWS + 2, :, :, :].rearrange("p f j t -> p (f j) t")
                             .bitcast(F32), HF[0:2, 0, :].unsqueeze(1).to_broadcast([2, 4 * FT, L])).then_inc(s_ones, 16)
            sources = {id(WQ): WqT, id(WK): WkT, id(WV): WvT}

            def sp_weights(n):
                W, lo, hi = SLICES[n]
                sp.dma_start(raw_of[id(W)][:, :, lo:hi],
                             sources[id(W)].rearrange("(t p) c -> p t c", p=128)[:, :, lo:hi]).then_inc(s_raw[n], 16)

            for kt in range(KT):
                sp.dma_start(wm_first[:, kt, :], wmod[kt * 128:(kt + 1) * 128, 0:2 * D]).then_inc(s_wm[kt], 16)
            sp.dma_start(bcol[:, :, :], bqkv_cols).then_inc(s_bias, 16)
            for n in range(5):
                sp_weights(n)
            for fill, kind in enumerate("qk"):
                sp_heads(sp, 0, kind, 0, fill, "sync")
            phase_a(sp, sp_slot)
            for h in range(2):
                sp.wait_ge(s_st_[h], 12 * NU)
            for tt in range(QB):
                sp_load_residual(sp, 1, tt)
            sp_store_ao(sp, B - 1, 3)
            sp_phase_b(sp)


def kernel(L0_attn_x, L0_attn_Wq, L0_attn_bq, L0_attn_Wk, L0_attn_bk, L0_attn_Wv, L0_attn_bv, L0_attn_Wo, L0_attn_bo,
           L0_ffn_W_base, L0_ffn_b_base, L0_ffn_lora_A, L0_ffn_lora_B, L0_ffn_router_W, L0_ffn_router_b,
           L0_ffn_domain_prior, L0_ffn_active, L0_c, L0_wmod):
    import numpy as np
    import concourse.bacc as bacc
    from concourse.bass_utils import run_bass_kernel_spmd

    def unit_order(a):
        return a.reshape(FT, 2, 4, HD, -1).transpose(0, 1, 3, 2, 4).reshape(a.shape)

    def columns(v):
        return v.reshape(KT, 128).T

    def layout(a):
        return np.ascontiguousarray(np.asarray(a))

    n = {k: np.asarray(v) for k, v in dict(
        x=L0_attn_x, Wq=L0_attn_Wq, bq=L0_attn_bq, Wk=L0_attn_Wk, bk=L0_attn_bk, Wv=L0_attn_Wv, bv=L0_attn_bv,
        Wo=L0_attn_Wo, bo=L0_attn_bo, Wb=L0_ffn_W_base, bb=L0_ffn_b_base, A=L0_ffn_lora_A, Bm=L0_ffn_lora_B,
        R=L0_ffn_router_W, rb=L0_ffn_router_b, prior=L0_ffn_domain_prior, act=L0_ffn_active, c=L0_c, wmod=L0_wmod).items()}
    arrays = dict(
        x=n["x"], WqT=unit_order(n["Wq"]).T, WkT=unit_order(n["Wk"]).T, WvT=n["Wv"].T,
        bqkv_cols=np.stack([columns(unit_order(n["bq"])), columns(unit_order(n["bk"])), columns(n["bv"])], axis=1),
        WoT=n["Wo"].T, bo=n["bo"].reshape(1, D), WbT=n["Wb"].T, b_base=n["bb"].reshape(1, D),
        loraAT=np.concatenate([n["A"], n["R"][:, None, :]], axis=1).transpose(2, 0, 1),
        loraBT=n["Bm"].transpose(0, 2, 1), bias_prior=np.stack([n["rb"], n["prior"]], axis=1), active=n["act"].reshape(1, E_ACT),
        cT=n["c"].T, wmod=n["wmod"])
    nc = bacc.Bacc("TRN2", target_bir_lowering=False, num_devices=1)
    ins, args = {}, []
    for name, a in arrays.items():
        ins[f"in_{name}"] = layout(a)
        args.append(nc.dram_tensor(f"in_{name}", ins[f"in_{name}"].shape, mybir.dt.from_np(ins[f"in_{name}"].dtype),
                                   kind="ExternalInput").ap())
    args.append(nc.dram_tensor("out_0", [B * L, D], F32, kind="ExternalOutput").ap())
    adaln_block_kernel(nc, *args)
    r = run_bass_kernel_spmd(nc, [ins], core_ids=[0])
    return r.results[0]["out_0"].reshape(B, L, D)
```
